# Optimizing a Trainium2 kernel written in Bass

```python
import numpy as np
import jax
import jax.numpy as jnp

def _softmax(x, axis=-1):
    return jax.nn.softmax(x, axis=axis)

def _gelu(x):
    return jax.nn.gelu(x, approximate=True)

def _silu(x):
    return jax.nn.silu(x)

def _sigmoid(x):
    return jax.nn.sigmoid(x)

def _layernorm(x, axis=-1, eps=1e-05):
    m = jnp.mean(x, axis=axis, keepdims=True)
    v = jnp.var(x, axis=axis, keepdims=True)
    return (x - m) / jnp.sqrt(v + eps)

def _scatter_add(tgt, idx, src, axis=0):
    return tgt.at[idx].add(src)

def _segment_sum(src, seg, n):
    return jax.ops.segment_sum(src, seg, n)
kernel_name = 'mk_decoder_postln_d2_seqx_r8_e48afc'

def setup_inputs(seed: int=0):
    np.random.seed(seed)
    _w = jnp.asarray

    def _rec_inputs():
        import jax
        import jax.numpy as jnp
        _rk = jax.random.key(seed)
        x = 7.22e-05 + 1 * jax.random.normal(jax.random.fold_in(_rk, 1), (128, 64, 128), jnp.float32)
        _lenS = 64 - jax.random.randint(jax.random.fold_in(_rk, 7), (128,), 0, max(1, 64 // 4) + 1, jnp.int32)
        _lenS2 = 64 - jax.random.randint(jax.random.fold_in(_rk, 8), (128,), 0, max(1, 64 // 4) + 1, jnp.int32)
        _ctx_1024P = jax.random.normal(jax.random.fold_in(_rk, 11), (128, 16, 128), jnp.float32)
        _ctx_1024c = jax.random.dirichlet(jax.random.fold_in(_rk, 511), 0.3 * jnp.ones((16,), jnp.float32), (128, 64))
        _ctx_1024t = jnp.einsum('bsk,bkd->bsd', _ctx_1024c, _ctx_1024P)
        _ctx_1024t = _ctx_1024t * jax.lax.rsqrt(jnp.mean(jnp.square(_ctx_1024t)) + 1e-12) * 0.953939
        ctx_1024 = 4.13588e-05 + 0.999923 * (_ctx_1024t + 0.3 * jax.random.normal(jax.random.fold_in(_rk, 611), (128, 64, 128), jnp.float32))
        _validS = jnp.arange(64)[None, :] < _lenS[:, None]
        _validS2 = jnp.arange(64)[None, :] < _lenS2[:, None]
        _causal = jnp.tril(jnp.ones((64, 64), dtype=bool))
        mask_BxS2_bf1 = jnp.ones((128, 64), dtype=bool)
        return (x, ctx_1024, mask_BxS2_bf1)
    x, ctx_1024, mask_BxS2_bf1 = _rec_inputs()

    def _L0_attn_setup():
        import jax, jax.numpy as jnp
        import numpy as np
        D_MODEL = 128
        N_HEADS = 16
        D_HEAD = 64
        B, S = (8, 128)
        EPS = 1.1920929e-07
        key = jax.random.key(seed)
        k1, k2, k3 = jax.random.split(key, 3)
        x = jax.random.normal(k1, (B, S, D_MODEL), dtype=jnp.float32)
        W_qkv = jax.random.normal(k2, (3 * N_HEADS * D_HEAD, D_MODEL), dtype=jnp.float32) * 0.02
        b_qkv = jnp.zeros((3 * N_HEADS * D_HEAD,), dtype=jnp.float32)
        W_o = jax.random.normal(k3, (D_MODEL, N_HEADS * D_HEAD), dtype=jnp.float32) * 0.02
        b_o = jnp.zeros((D_MODEL,), dtype=jnp.float32)
        return {'x': x, 'W_qkv': W_qkv, 'b_qkv': b_qkv, 'W_o': W_o, 'b_o': b_o}
    _L0_attn_all = _L0_attn_setup()
    _L0_attn_in = {k: v for k, v in _L0_attn_all.items() if k in ('W_qkv', 'b_qkv', 'W_o', 'b_o')}
    del _L0_attn_all

    def _L0_xattn_setup():
        import jax, jax.numpy as jnp
        import numpy as np
        D_MODEL = 128
        NUM_HEADS = 16
        HEAD_DIM = D_MODEL // NUM_HEADS
        B, S = (4, 256)
        key = jax.random.key(seed)
        ks = jax.random.split(key, 11)
        sc = 1.0 / np.sqrt(D_MODEL)
        inp = {'query': jax.random.normal(ks[0], (B, S, D_MODEL), jnp.float32), 'key': jax.random.normal(ks[1], (B, S, D_MODEL), jnp.float32), 'value': jax.random.normal(ks[2], (B, S, D_MODEL), jnp.float32), 'Wq': jax.random.normal(ks[3], (D_MODEL, D_MODEL), jnp.float32) * sc, 'bq': jnp.zeros((D_MODEL,), jnp.float32), 'Wk': jax.random.normal(ks[4], (D_MODEL, D_MODEL), jnp.float32) * sc, 'bk': jnp.zeros((D_MODEL,), jnp.float32), 'Wv': jax.random.normal(ks[5], (D_MODEL, D_MODEL), jnp.float32) * sc, 'bv': jnp.zeros((D_MODEL,), jnp.float32), 'Wo': jax.random.normal(ks[6], (D_MODEL, D_MODEL), jnp.float32) * sc, 'bo': jnp.zeros((D_MODEL,), jnp.float32)}
        return inp
    _L0_xattn_all = _L0_xattn_setup()
    _L0_xattn_in = {k: v for k, v in _L0_xattn_all.items() if k in ('Wq', 'bq', 'Wk', 'bk', 'Wv', 'bv', 'Wo', 'bo')}
    del _L0_xattn_all

    def _L0_ffn_setup():
        import jax, jax.numpy as jnp
        import numpy as np
        LN_EPS = 0.001
        EPS = 1e-05
        QB = 128.0

        def ste_round(x):
            return x + jax.lax.stop_gradient(jnp.round(x) - x)
        key = jax.random.key(seed)
        k1, k2 = jax.random.split(key)
        x = jax.random.normal(k1, (4, 1024, 128), dtype=jnp.float32)
        weight = jax.random.normal(k2, (128, 128), dtype=jnp.float32) * 0.02
        ln_gamma = jnp.ones((128,), dtype=jnp.float32)
        ln_beta = jnp.zeros((128,), dtype=jnp.float32)
        return {'x': x, 'weight': weight, 'ln_gamma': ln_gamma, 'ln_beta': ln_beta}
    _L0_ffn_all = _L0_ffn_setup()
    _L0_ffn_in = {k: v for k, v in _L0_ffn_all.items() if k in ('weight', 'ln_gamma', 'ln_beta')}
    del _L0_ffn_all

    def _L1_attn_setup():
        import math
        import jax, jax.numpy as jnp
        import numpy as np
        N_HEAD = 16
        key = jax.random.key(seed)
        k1, k2, k3, k4 = jax.random.split(key, 4)
        B, T, C, R = (4, 256, 128, 64)
        std = 0.02
        return {'hidden_states': jax.random.normal(k1, (B, T, C), dtype=jnp.float32), 'W_basis': jax.random.normal(k2, (R, C), dtype=jnp.float32) * std, 'W_v': jax.random.normal(k3, (C, C), dtype=jnp.float32) * std, 'b_v': jnp.zeros((C,), dtype=jnp.float32), 'W_o': jax.random.normal(k4, (C, C), dtype=jnp.float32) * std, 'b_o': jnp.zeros((C,), dtype=jnp.float32)}
    _L1_attn_all = _L1_attn_setup()
    _L1_attn_in = {k: v for k, v in _L1_attn_all.items() if k in ('W_basis', 'W_v', 'b_v', 'W_o', 'b_o')}
    del _L1_attn_all

    def _L1_xattn_setup():
        import jax, jax.numpy as jnp
        import numpy as np
        DIM = 128
        DIM_LATENT = 128
        DIM_HEAD = 64
        HEADS = 16
        INNER = HEADS * DIM_HEAD

        def layernorm(x, g, b, eps=1e-05):
            m = jnp.mean(x, axis=-1, keepdims=True)
            v = jnp.mean((x - m) ** 2, axis=-1, keepdims=True)
            return (x - m) / jnp.sqrt(v + eps) * g + b

        def rmsnorm(x, gamma, eps=1e-08):
            n = jnp.linalg.norm(x, axis=-1, keepdims=True) * x.shape[-1] ** (-0.5)
            return x / jnp.maximum(n, eps) * gamma
        key = jax.random.key(seed)
        ks = jax.random.split(key, 8)
        b, n, m = (4, 512, 64)
        x = jax.random.normal(ks[0], (b, n, DIM), dtype=jnp.float32)
        latents = jax.random.normal(ks[1], (b, m, DIM_LATENT), dtype=jnp.float32)
        mask = jnp.ones((b, n), dtype=bool)
        s = 0.02
        return {'x': x, 'latents': latents, 'mask': mask, 'ln_x_g': jnp.ones((DIM,), jnp.float32), 'ln_x_b': jnp.zeros((DIM,), jnp.float32), 'ln_l_g': jnp.ones((DIM_LATENT,), jnp.float32), 'ln_l_b': jnp.zeros((DIM_LATENT,), jnp.float32), 'qn_g': jnp.ones((DIM_HEAD,), jnp.float32), 'kn_g': jnp.ones((DIM_HEAD,), jnp.float32), 'Wq': jax.random.normal(ks[2], (DIM_LATENT, INNER), jnp.float32) * s, 'Wkv': jax.random.normal(ks[3], (DIM, 2 * INNER), jnp.float32) * s, 'Wout': jax.random.normal(ks[4], (INNER, DIM_LATENT), jnp.float32) * s, 'bout': jnp.zeros((DIM_LATENT,), jnp.float32)}
    _L1_xattn_all = _L1_xattn_setup()
    _L1_xattn_in = {k: v for k, v in _L1_xattn_all.items() if k in ('ln_x_g', 'ln_x_b', 'ln_l_g', 'ln_l_b', 'qn_g', 'kn_g', 'Wq', 'Wkv', 'Wout', 'bout')}
    del _L1_xattn_all

    def _L1_ffn_setup():
        import jax, jax.numpy as jnp
        import numpy as np
        B, S, D_IN, D_OUT, E, K = (2, 256, 128, 128, 8, 2)
        key = jax.random.key(seed)
        k1, k2, k3, k4 = jax.random.split(key, 4)
        scale = 1.0 / np.sqrt(D_IN)
        return {'inputs': jax.random.normal(k1, (B, S, D_IN), dtype=jnp.float32), 'Wg': jax.random.normal(k2, (E, D_IN), dtype=jnp.float32) * scale, 'We': jax.random.normal(k3, (E, D_OUT, D_IN), dtype=jnp.float32) * scale, 'be': jax.random.normal(k4, (E, D_OUT), dtype=jnp.float32) * scale}
    _L1_ffn_all = _L1_ffn_setup()
    _L1_ffn_in = {k: v for k, v in _L1_ffn_all.items() if k in ('Wg', 'We', 'be')}
    del _L1_ffn_all
    return {'x': x, 'ctx_1024': ctx_1024, 'mask_BxS2_bf1': mask_BxS2_bf1, 'L0_attn_W_qkv': _L0_attn_in['W_qkv'], 'L0_attn_b_qkv': _L0_attn_in['b_qkv'], 'L0_attn_W_o': _L0_attn_in['W_o'], 'L0_attn_b_o': _L0_attn_in['b_o'], 'L0_xattn_Wq': _L0_xattn_in['Wq'], 'L0_xattn_bq': _L0_xattn_in['bq'], 'L0_xattn_Wk': _L0_xattn_in['Wk'], 'L0_xattn_bk': _L0_xattn_in['bk'], 'L0_xattn_Wv': _L0_xattn_in['Wv'], 'L0_xattn_bv': _L0_xattn_in['bv'], 'L0_xattn_Wo': _L0_xattn_in['Wo'], 'L0_xattn_bo': _L0_xattn_in['bo'], 'L0_ffn_weight': _L0_ffn_in['weight'], 'L0_ffn_ln_gamma': _L0_ffn_in['ln_gamma'], 'L0_ffn_ln_beta': _L0_ffn_in['ln_beta'], 'L1_attn_W_basis': _L1_attn_in['W_basis'], 'L1_attn_W_v': _L1_attn_in['W_v'], 'L1_attn_b_v': _L1_attn_in['b_v'], 'L1_attn_W_o': _L1_attn_in['W_o'], 'L1_attn_b_o': _L1_attn_in['b_o'], 'L1_xattn_ln_x_g': _L1_xattn_in['ln_x_g'], 'L1_xattn_ln_x_b': _L1_xattn_in['ln_x_b'], 'L1_xattn_ln_l_g': _L1_xattn_in['ln_l_g'], 'L1_xattn_ln_l_b': _L1_xattn_in['ln_l_b'], 'L1_xattn_qn_g': _L1_xattn_in['qn_g'], 'L1_xattn_kn_g': _L1_xattn_in['kn_g'], 'L1_xattn_Wq': _L1_xattn_in['Wq'], 'L1_xattn_Wkv': _L1_xattn_in['Wkv'], 'L1_xattn_Wout': _L1_xattn_in['Wout'], 'L1_xattn_bout': _L1_xattn_in['bout'], 'L1_ffn_Wg': _L1_ffn_in['Wg'], 'L1_ffn_We': _L1_ffn_in['We'], 'L1_ffn_be': _L1_ffn_in['be']}

def reference(x, ctx_1024, mask_BxS2_bf1, L0_attn_W_qkv, L0_attn_b_qkv, L0_attn_W_o, L0_attn_b_o, L0_xattn_Wq, L0_xattn_bq, L0_xattn_Wk, L0_xattn_bk, L0_xattn_Wv, L0_xattn_bv, L0_xattn_Wo, L0_xattn_bo, L0_ffn_weight, L0_ffn_ln_gamma, L0_ffn_ln_beta, L1_attn_W_basis, L1_attn_W_v, L1_attn_b_v, L1_attn_W_o, L1_attn_b_o, L1_xattn_ln_x_g, L1_xattn_ln_x_b, L1_xattn_ln_l_g, L1_xattn_ln_l_b, L1_xattn_qn_g, L1_xattn_kn_g, L1_xattn_Wq, L1_xattn_Wkv, L1_xattn_Wout, L1_xattn_bout, L1_ffn_Wg, L1_ffn_We, L1_ffn_be):
    import jax
    import jax.numpy as jnp

    def _L0_attn_ref(x, W_qkv, b_qkv, W_o, b_o):
        import jax, jax.numpy as jnp
        import numpy as np
        D_MODEL = 128
        N_HEADS = 16
        D_HEAD = 64
        B, S = (8, 128)
        EPS = 1.1920929e-07
        normed = x * jax.lax.rsqrt(jnp.mean(x * x, axis=-1, keepdims=True) + EPS)
        qkv = normed @ W_qkv.T + b_qkv
        qkv = qkv.reshape(*qkv.shape[:-1], N_HEADS, D_HEAD, 3)
        q, k, v = (qkv[..., 0], qkv[..., 1], qkv[..., 2])
        scores = jnp.einsum('bqhd,bkhd->bhqk', q, k)
        seq = x.shape[-2]
        causal_mask = jnp.triu(jnp.ones((seq, seq), dtype=bool), k=1)
        scores = jnp.where(causal_mask, -jnp.inf, scores)
        attn = jax.nn.softmax(scores, axis=-2)
        z = jnp.einsum('bhqk,bkhd->bqhd', attn, v)
        z = z.reshape(*z.shape[:-2], N_HEADS * D_HEAD)
        return z @ W_o.T + b_o

    def _L0_xattn_ref(query, key, value, Wq, bq, Wk, bk, Wv, bv, Wo, bo):
        import jax, jax.numpy as jnp
        import numpy as np
        D_MODEL = 128
        NUM_HEADS = 16
        HEAD_DIM = D_MODEL // NUM_HEADS
        B, S = (4, 256)

        def split_heads(x):
            b, s, _ = x.shape
            return x.reshape(b, s, NUM_HEADS, HEAD_DIM).transpose(0, 2, 1, 3)
        q = split_heads(query @ Wq + bq)
        k = split_heads(key @ Wk + bk)
        v = split_heads(value @ Wv + bv)
        scores = jnp.einsum('bhqd,bhkd->bhqk', q, k) / jnp.sqrt(jnp.float32(HEAD_DIM))
        weights = jax.nn.softmax(scores, axis=-1)
        attn = jnp.einsum('bhqk,bhkd->bhqd', weights, v)
        attn = attn.transpose(0, 2, 1, 3).reshape(query.shape[0], query.shape[1], D_MODEL)
        return attn @ Wo + bo

    def _L0_ffn_ref(x, weight, ln_gamma, ln_beta):
        import jax, jax.numpy as jnp
        import numpy as np
        LN_EPS = 0.001
        EPS = 1e-05
        QB = 128.0

        def ste_round(x):
            return x + jax.lax.stop_gradient(jnp.round(x) - x)
        mu = jnp.mean(x, axis=-1, keepdims=True)
        var = jnp.var(x, axis=-1, keepdims=True)
        xn = (x - mu) * jax.lax.rsqrt(var + LN_EPS) * ln_gamma + ln_beta
        beta = jnp.mean(jnp.abs(weight))
        w_q = jnp.clip(ste_round(weight / (beta + EPS)), -1.0, 1.0)
        gamma = jnp.max(jnp.abs(xn))
        xq = jnp.clip(xn * QB / gamma, -QB + EPS, QB - EPS)
        y = jnp.einsum('bsd,du->bsu', xq, w_q)
        return y * (gamma * beta / QB)

    def _L1_attn_ref(hidden_states, W_basis, W_v, b_v, W_o, b_o):
        import math
        import jax, jax.numpy as jnp
        import numpy as np
        N_HEAD = 16
        B, T, C = hidden_states.shape
        nh = N_HEAD
        hd = C // nh
        R = W_basis.shape[0]
        latent = hidden_states @ W_basis.T
        v = hidden_states @ W_v.T + b_v
        v = v.reshape(B, T, nh, hd).transpose(0, 2, 1, 3)
        scores = jnp.einsum('bqr,bkr->bqk', latent, latent) * (1.0 / math.sqrt(R))
        causal = jnp.tril(jnp.ones((T, T), dtype=bool))
        scores = jnp.where(causal[None, :, :], scores, -jnp.inf)
        att = jax.nn.softmax(scores, axis=-1)
        y = jnp.einsum('bqk,bhkd->bhqd', att, v)
        y = y.transpose(0, 2, 1, 3).reshape(B, T, C)
        out = y @ W_o.T + b_o
        return out

    def _L1_xattn_ref(x, latents, mask, ln_x_g, ln_x_b, ln_l_g, ln_l_b, qn_g, kn_g, Wq, Wkv, Wout, bout):
        import jax, jax.numpy as jnp
        import numpy as np
        DIM = 128
        DIM_LATENT = 128
        DIM_HEAD = 64
        HEADS = 16
        INNER = HEADS * DIM_HEAD

        def layernorm(x, g, b, eps=1e-05):
            m = jnp.mean(x, axis=-1, keepdims=True)
            v = jnp.mean((x - m) ** 2, axis=-1, keepdims=True)
            return (x - m) / jnp.sqrt(v + eps) * g + b

        def rmsnorm(x, gamma, eps=1e-08):
            n = jnp.linalg.norm(x, axis=-1, keepdims=True) * x.shape[-1] ** (-0.5)
            return x / jnp.maximum(n, eps) * gamma
        b, n, _ = x.shape
        m = latents.shape[1]
        h, d = (HEADS, DIM_HEAD)
        scale = d ** (-0.5)
        xn = layernorm(x, ln_x_g, ln_x_b)
        ln = layernorm(latents, ln_l_g, ln_l_b)
        q = (ln @ Wq).reshape(b, m, h, d).transpose(0, 2, 1, 3)
        kv = jnp.concatenate([xn @ Wkv, ln @ Wkv], axis=1)
        kv = kv.reshape(b, n + m, 2, h, d)
        k = kv[:, :, 0].transpose(0, 2, 1, 3)
        v = kv[:, :, 1].transpose(0, 2, 1, 3)
        qn = rmsnorm(q, qn_g) * scale
        kn = rmsnorm(k, kn_g)
        sim = jnp.einsum('bhid,bhjd->bhij', qn, kn)
        max_neg = -jnp.finfo(sim.dtype).max
        padded_mask = jnp.concatenate([mask, jnp.ones((b, m), bool)], axis=1)
        sim = jnp.where(padded_mask[:, None, None, :], sim, max_neg)
        attn = jax.nn.softmax(sim.astype(jnp.float32), axis=-1).astype(sim.dtype)
        out = jnp.einsum('bhij,bhjd->bhid', attn, v)
        out = out.transpose(0, 2, 1, 3).reshape(b, m, h * d)
        return out @ Wout + bout

    def _L1_ffn_ref(inputs, Wg, We, be):
        import jax, jax.numpy as jnp
        import numpy as np
        B, S, D_IN, D_OUT, E, K = (2, 256, 128, 128, 8, 2)
        logits = jnp.einsum('bsd,ed->bse', inputs, Wg)
        topw, sel = jax.lax.top_k(logits, K)
        topw = jax.nn.softmax(topw.astype(jnp.float32), axis=-1).astype(inputs.dtype)
        cw = jnp.sum(jax.nn.one_hot(sel, E, dtype=topw.dtype) * topw[..., None], axis=-2)
        y = jnp.einsum('bsd,eod->bseo', inputs, We) + be
        return jnp.einsum('bseo,bse->bso', y, cw)
    x = _layernorm(x + _L0_attn_ref(x, L0_attn_W_qkv, L0_attn_b_qkv, L0_attn_W_o, L0_attn_b_o), axis=-1)
    x = _layernorm(x + _L0_xattn_ref(x, ctx_1024, ctx_1024, L0_xattn_Wq, L0_xattn_bq, L0_xattn_Wk, L0_xattn_bk, L0_xattn_Wv, L0_xattn_bv, L0_xattn_Wo, L0_xattn_bo), axis=-1)
    x = _layernorm(x + _L0_ffn_ref(x, L0_ffn_weight, L0_ffn_ln_gamma, L0_ffn_ln_beta), axis=-1)
    x = _layernorm(x + _L1_attn_ref(x, L1_attn_W_basis, L1_attn_W_v, L1_attn_b_v, L1_attn_W_o, L1_attn_b_o), axis=-1)
    x = _layernorm(x + _L1_xattn_ref(ctx_1024, x, mask_BxS2_bf1, L1_xattn_ln_x_g, L1_xattn_ln_x_b, L1_xattn_ln_l_g, L1_xattn_ln_l_b, L1_xattn_qn_g, L1_xattn_kn_g, L1_xattn_Wq, L1_xattn_Wkv, L1_xattn_Wout, L1_xattn_bout), axis=-1)
    x = _layernorm(x + _L1_ffn_ref(x, L1_ffn_Wg, L1_ffn_We, L1_ffn_be), axis=-1)
    return x

_drawn_inputs = setup_inputs


def setup_inputs(seed=0):
    import zlib

    import numpy as np

    out = dict(_drawn_inputs(seed))
    spreads = {'L0_attn_b_qkv': (0.0, 0.1),
     'L0_attn_b_o': (0.0, 0.1),
     'L0_xattn_bq': (0.0, 0.1),
     'L0_xattn_bk': (0.0, 2.0),
     'L0_xattn_bv': (0.0, 0.1),
     'L0_xattn_bo': (0.0, 0.1),
     'L0_ffn_ln_gamma': (1.0, 0.2),
     'L0_ffn_ln_beta': (0.0, 0.1),
     'L1_attn_b_v': (0.0, 0.1),
     'L1_attn_b_o': (0.0, 0.1),
     'L1_xattn_ln_x_g': (1.0, 0.2),
     'L1_xattn_ln_x_b': (0.0, 0.1),
     'L1_xattn_ln_l_g': (1.0, 0.2),
     'L1_xattn_ln_l_b': (0.0, 0.1),
     'L1_xattn_qn_g': (1.0, 0.2),
     'L1_xattn_kn_g': (1.0, 0.2),
     'L1_xattn_bout': (0.0, 0.1)}
    factors = {'L1_attn_W_basis': 50.6}
    for name, (base, spread) in spreads.items():
        noise = np.random.default_rng([zlib.crc32(name.encode()), seed]).standard_normal(out[name].shape)
        drawn = base * np.exp(spread * noise) if base else spread * noise
        out[name] = jnp.asarray(drawn.astype(out[name].dtype))
    for name, factor in factors.items():
        out[name] = (out[name] * factor).astype(out[name].dtype)
    return out
```

```python
from contextlib import ExitStack

import numpy as np

import concourse.bass as bass
from concourse import mybir

F32, F16, U32, U8 = mybir.dt.float32, mybir.dt.float16, mybir.dt.uint32, mybir.dt.uint8
ALU = mybir.AluOpType
ACT = mybir.ActivationFunctionType
AX = mybir.AxisListType

P = 128
B, S, D = 128, 64, 128
NH, DH = 16, 64
NP = NH // 2
INNER = NH * DH
TILES = 4
G = B * S // (TILES * P)
GT = TILES * P
SEQ = GT // S
NX = 16
DX = D // NX
R = 64
E8 = 8
QB = 128.0

WEIGHTS = [
    ("q0", INNER), ("k0", INNER), ("v0", INNER), ("o0", INNER),
    ("xq", D), ("xk", D), ("xv", D), ("xo", D), ("ffn", D),
    ("basis", R), ("v1", D), ("o1", D),
    ("yq", INNER), ("yk", INNER), ("yv", INNER), ("yo", INNER),
    ("gate", E8), ("exp", E8 * D),
    ("bq0", NP), ("bk0", NP), ("bxq", 1), ("bxk", 1), ("bv1", 1),
    ("gx", 1), ("bx", 1), ("gl", 1), ("bl", 1), ("qg", 1), ("kg", 1),
    ("rv0", INNER), ("ro0", D), ("rxv", D), ("rxo", D), ("rfg", D), ("rfb", D), ("ro1", D), ("ryo", D),
]
CONSTS = [
    ("ident", P), ("ones", P), ("sel", 64), ("mask4", 4), ("maskq", 4), ("mask2", P), ("half", 2),
    ("eps0", 1), ("eps5", 1), ("eps3", 1), ("iota", E8), ("zero", 1),
]


def columns(table):
    at, out = 0, {}
    for name, width in table:
        out[name] = slice(at, at + width)
        at += width
    return out, at


WCOL, WN = columns(WEIGHTS)
CCOL, CN = columns(CONSTS)


class Signal:

    def __init__(self, sem, per, lead=0):
        self.sem, self.per, self.lead = sem, per, lead

    def at(self, g, n):
        return g * self.per + (n + self.lead)


class Chain:

    def __init__(self, eng, sem):
        self.eng, self.sem, self.n = eng, sem, 0

    def __call__(self, ins):
        self.n += 1
        ins.then_inc(self.sem, 1)
        self.eng.wait_ge(self.sem, self.n)

    def done(self):
        self.eng.sem_clear(self.sem)


def decoder(nc, x, ctx_t, ctx, mask_t, weights, be, consts, consts16, out):
    x_v = x.rearrange("(g t p) c -> g p t c", t=TILES, p=P)
    ctx_v = ctx.rearrange("(g t p) c -> g p t c", t=TILES, p=P)
    ctxt_v = ctx_t.rearrange("c (g n) -> g c n", n=GT)
    out_v = out.rearrange("(g t p) c -> g p t c", t=TILES, p=P)

    with ExitStack() as stack:
        def sb(name, shape, dt=F32):
            return stack.enter_context(nc.sbuf_tensor(name, shape, dt))

        def ps(name, shape):
            return stack.enter_context(nc.psum_tensor(name, shape, F32))

        def sig(name, per=1, lead=0):
            return Signal(stack.enter_context(nc.semaphore(name)), per, lead)

        pa = ps("pa", [P, 1024])
        pb = ps("pb", [P, 1024])
        pc = ps("pc", [P, 1024])
        pd = ps("pd", [P, 512])
        pe_ = ps("pe", [P, 512])

        wts = sb("wts", [P, WN])
        cst = sb("cst", [P, CN])
        cst16 = sb("cst16", [P, P + 1024], F16)
        be_sb = sb("be_sb", [E8, D])
        ident16, causal_t, causal_1 = cst16[:, 0:P], cst16[:, P:P + 512], cst16[:, P + 512:P + 1024]

        def w(name, a=0, b=None):
            c = WCOL[name]
            return wts[:, c.start + a:c.start + b if b is not None else c.stop]

        def k(name, a=0, b=None):
            c = CCOL[name]
            return cst[:, c.start + a:c.start + b if b is not None else c.stop]

        ident = k("ident")
        state = sb("state", [P, G * GT])
        fstat = sb("fstat", [P, G * 2 * TILES])
        qblk = sb("qblk", [P, NP, 2, GT])
        kt = sb("kt", [P, NP, GT])
        v = sb("v", [P, 2, INNER])
        st = sb("st", [P, 2, 1024])
        zt = sb("zt", [P, NP, GT])
        pblk = sb("pblk", [P, NH, 2, S])
        x_in = sb("x_in", [P, TILES, D])
        c_in = sb("c_in", [P, TILES, D])
        nrm = sb("nrm", [P, TILES, D])
        tT = sb("tT", [P, GT])
        res = sb("res", [P, TILES, D])
        x1 = sb("x1", [P, TILES, D])
        xb = sb("xb", [P, TILES, D])
        zx = sb("zx", [P, TILES, D])
        y = sb("y", [P, TILES, D])
        x2 = sb("x2", [P, TILES, D])
        junk = sb("junk", [P, TILES, D])
        latt = sb("latt", [R, GT])
        cwt = sb("cwt", [E8, GT])
        vblk = sb("vblk", [P, SEQ, NP, 18])
        small = sb("small", [P, 592])
        used = [0]

        def tiny(*shape):
            n = int(np.prod(shape))
            a = small[:, used[0]:used[0] + n]
            used[0] += n
            names = "abc"[:len(shape)]
            if len(shape) > 1:
                a = a.rearrange(f"p ({' '.join(names)}) -> p {' '.join(names)}", **dict(zip(names[1:], shape[1:])))
            return a

        ssq, lnv, rms = tiny(TILES), tiny(TILES), tiny(TILES)
        mx, sm, rs = tiny(2, NH), tiny(2, NH), tiny(2, NH)
        stats, mv = tiny(TILES, 6), tiny(TILES, 2)
        rstd, rstdf = tiny(TILES), tiny(TILES)
        fstl = tiny(8)
        rq = tiny(NH)
        mbl = tiny(SEQ)
        peaks, peak = tiny(2), tiny(2)
        bxqm = tiny(4)
        mqs = tiny(4)
        rz = tiny(NP, 2)
        rk = tiny(4, NH)
        rkl = tiny(4, NH)
        gqk = tiny(1)
        ffs = tiny(8)
        lg = tiny(TILES, E8)
        top = tiny(TILES, E8)
        topi = tiny(TILES, E8)
        selc = tiny(TILES, E8)
        selc2 = tiny(TILES, E8)
        cw = tiny(TILES, E8)
        p1, p2 = tiny(TILES), tiny(TILES)
        ix = tiny(TILES, 2)
        maskb = sb("maskb", [P, B])
        mask8 = sb("mask8", [S, B], U8)
        topu = sb("topu", [P, TILES, E8], U32)
        wq = sb("wq", [P, D])
        fold = sb("fold", [P, 2 * D])

        ktf = kt[:, :, :].rearrange("p a n -> p (a n)")
        qg = ktf[:, 0:4 * GT].rearrange("p (j n) -> p j n", n=GT)
        kj = ktf[:, 4 * GT:8 * GT].rearrange("p (j n) -> p j n", n=GT)
        ztf = zt[:, :, :].rearrange("p a n -> p (a n)")
        zta = [ztf[:, 1024 * i:1024 * i + 1024].rearrange("p (a n) -> p a n", n=P) for i in range(2)]
        pt = [ztf[:, 2048 + 1024 * i:3072 + 1024 * i].rearrange("p (a n) -> p a n", n=P) for i in range(2)]
        pflat = pblk[:, :, :, :].rearrange("p h a n -> p (h a n)")
        sqt, qs = pflat[:, 0:1024], pflat[:, 1024:2048]
        kvt = vblk[:, :, :, :].rearrange("p b i n -> p (b i n)")[:, 0:SEQ * P].rearrange("p (b n) -> p b n", n=P)
        vdata = vblk[:, :, :, 0:16]
        vbias = fold[:, 0:D]
        sqk = [pflat[:, 512 * i:512 * i + 512] for i in range(2)]

        def flat(a):
            return a[:, :, :].rearrange("p t c -> p (t c)")

        def hview(a, n=S):
            return a.rearrange("p (h n) -> p h n", n=n)

        def over(a, n):
            return a.unsqueeze(2).broadcast_to([a.shape[0], a.shape[1], n])

        def tiled(a, n):
            return a.unsqueeze(1).broadcast_to([a.shape[0], n, a.shape[1]])

        loaded = sig("loaded")
        setup = sig("setup")
        x_loaded, c_loaded = sig("x_loaded", 16), sig("c_loaded", 16)
        xb_ready, rms_ready, n_ready, n_turned, nt_ready = (
            sig("xb_ready", 1, 1), sig("rms_ready", 1), sig("n_ready", 1, 1), sig("n_turned", 1), sig("nt_ready", 1))
        q_made, k_made, q_kept, k_kept = sig("q_made", NP), sig("k_made", NP), sig("q_kept", NP), sig("k_kept", NP)
        v_made, v_kept = sig("v_made", TILES), sig("v_kept", TILES)
        s_made, s_shifted, s_exp, s_norm = (
            sig("s_made", TILES), sig("s_shifted", TILES), sig("s_exp", TILES), sig("s_norm", TILES))
        p_ready = sig("p_ready", 2 * TILES)
        z_made, z_kept, o_made = sig("z_made", TILES), sig("z_kept", TILES), sig("o_made", 1)
        stat1, rstd1, x1_ready, x1_turned, x1t_ready = (
            sig("stat1"), sig("rstd1"), sig("x1_ready"), sig("x1_turned"), sig("x1t_ready"))
        kx_made, vx_made, vx_masked, vx_ready, qx_made, kx_kept, qx_kept = (
            sig("kx_made"), sig("vx_made", 1, 1), sig("vx_masked"), sig("vx_ready"), sig("qx_made"), sig("kx_kept"), sig("qx_kept"))
        sx_made, sx_shifted, sx_exp, px_turned = (
            sig("sx_made", TILES), sig("sx_shifted", TILES), sig("sx_exp", TILES), sig("px_turned", TILES))
        px_a, px_v = sig("px_a", TILES), sig("px_v", TILES)
        zx_made, zx_ready, zx_turned, zxt_ready, ox_made = (
            sig("zx_made", TILES), sig("zx_ready", TILES), sig("zx_turned"), sig("zxt_ready"), sig("ox_made"))
        x1b_ready, r2_ready, rstd2, x2_ready, stat3, rstd3, peak_done = (
            sig("x1b_ready"), sig("r2_ready", 1, 1), sig("rstd2"), sig("x2_ready"), sig("stat3"), sig("rstd3"), sig("peak_done", 1, 1))

        peak_local, weight_sum, peak_all, between = sig("peak_local"), sig("weight_sum"), sig("peak_all"), sig("between")
        cb_loaded, xn_ready, xn_turned, xq_ready, f_made = (
            sig("cb_loaded", 16), sig("xn_ready"), sig("xn_turned"), sig("xq_ready"), sig("f_made"))
        cn_stat, cn_rstd, cn_ready, cn_turned, cn_kept = (
            sig("cn_stat"), sig("cn_rstd"), sig("cn_ready", 1, 1), sig("cn_turned"), sig("cn_kept"))
        x3_stat, x3_rstd, x3_ready, x3_turned, x3t_ready, x3b_ready = (
            sig("x3_stat"), sig("x3_rstd"), sig("x3_ready"), sig("x3_turned"), sig("x3t_ready"), sig("x3b_ready"))
        lat_made, lat_kept, v1_made, v1_kept = sig("lat_made"), sig("lat_kept"), sig("v1_made"), sig("v1_kept")
        s1_made, s1_shifted, s1_exp, p1_ready, p1_turned, p1t_ready, z1_made, z1_kept, o1_made = (
            sig("s1_made"), sig("s1_shifted"), sig("s1_exp"), sig("p1_ready"), sig("p1_turned"), sig("p1t_ready"),
            sig("z1_made", 1, 1), sig("z1_kept"), sig("o1_made"))
        x4_stat, x4_rstd, x4_ready, x4b_ready, ln_stat, ln_rstd, ln_ready, ln_turned, ln_kept = (
            sig("x4_stat"), sig("x4_rstd"), sig("x4_ready"), sig("x4b_ready"), sig("ln_stat"), sig("ln_rstd"),
            sig("ln_ready"), sig("ln_turned", 1, 1), sig("ln_kept"))
        yq_made, yq_squared, yq_sum, yq_root, yq_scaled, yq_turned, yq_a, yq_v = (
            sig("yq_made", TILES), sig("yq_squared", TILES), sig("yq_sum", TILES), sig("yq_root", TILES),
            sig("yq_scaled", TILES), sig("yq_turned", TILES), sig("yq_a", TILES), sig("yq_v", TILES))
        yk_made, yk_kept, yk_squared, yk_summed = (
            sig("yk_made", 2 * NP), sig("yk_kept", 2 * NP), sig("yk_squared", 2 * NP), sig("yk_summed", 2 * NP))
        yk_sum_kept, yk_sum_turned, yk_mean, yk_root = (
            sig("yk_sum_kept", 2), sig("yk_sum_turned", 2), sig("yk_mean", 2), sig("yk_root", 2))
        yv_made, yv_kept, ys_made, ys_scaled, yp_ready, yl_made, yl_inv, yz_made, yz_kept, yo_made = (
            sig("yv_made", SEQ), sig("yv_kept", SEQ), sig("ys_made", SEQ), sig("ys_scaled", SEQ), sig("yp_ready", SEQ, 1),
            sig("yl_made", SEQ), sig("yl_inv", SEQ), sig("yz_made", SEQ), sig("yz_kept", SEQ), sig("yo_made"))
        x5_stat, x5_rstd, x5_ready, x5_turned, x5t_ready = (
            sig("x5_stat"), sig("x5_rstd"), sig("x5_ready"), sig("x5_turned"), sig("x5t_ready"))
        gate_made, gap_ready, gap_exp, cw_ready, cw_turned, cwt_ready, be_made = (
            sig("gate_made"), sig("gap_ready"), sig("gap_exp"), sig("cw_ready"), sig("cw_turned"), sig("cwt_ready"),
            sig("be_made"))
        e_made, e_scaled = sig("e_made", TILES), sig("e_scaled", TILES)
        x6_stat, x6_rstd, x6_ready, stored = sig("x6_stat"), sig("x6_rstd"), sig("x6_ready"), sig("stored", 16, 16)
        x2_copied = sig("x2_copied")
        lat_placed, peak_kept = sig("lat_placed"), sig("peak_kept")
        act_own, dve_own, pool_own, pool_hold = [stack.enter_context(nc.semaphore(n))
                                                 for n in ("act_own", "dve_own", "pool_own", "pool_hold")]
        gap_a, gap_v, gap_s = sig("gap_a"), sig("gap_v"), sig("gap_s")

        block = stack.enter_context(nc.Block())

        @block.sync
        def _(sp):
            for ahead in (xb_ready, n_ready, vx_made, r2_ready, peak_done, cn_ready, stored, z1_made, yp_ready,
                          ln_turned):
                sp.sem_inc(ahead.sem, ahead.lead)
            for dst, src in ((wts, weights), (cst, consts), (cst16, consts16), (be_sb, be)):
                sp.dma_start(dst[:, :], src).then_inc(loaded.sem, 16)
            sp.dma_start(mask8[:, :], mask_t).then_inc(loaded.sem, 16)
            with sp.Fori(0, G) as g:
                sp.wait_ge(xb_ready.sem, xb_ready.at(g, 0))
                sp.wait_ge(n_ready.sem, n_ready.at(g, 0))
                sp.dma_start(x_in[:, :, :], x_v[g]).then_inc(x_loaded.sem, 16)
                sp.wait_ge(vx_made.sem, vx_made.at(g, 0))
                sp.dma_start(flat(c_in), ctxt_v[g]).then_inc(c_loaded.sem, 16)
            with sp.Fori(0, G) as g:
                sp.wait_ge(peak_done.sem, G + peak_done.lead)
                sp.wait_ge(cn_ready.sem, cn_ready.at(g, 0))
                sp.dma_start(c_in[:, :, :], ctx_v[g]).then_inc(cb_loaded.sem, 16)
                sp.wait_ge(x6_ready.sem, x6_ready.at(g, 1))
                sp.dma_start(out_v[g], zx[:, :, :]).then_inc(stored.sem, 16)
            sp.wait_ge(stored.sem, 16 * G + stored.lead)

        @block.tensor
        def _(pe):
            pe.wait_ge(loaded.sem, 80)
            pe.wait_ge(setup.sem, 2)
            with pe.Fori(0, G) as g:
                pe.wait_ge(n_ready.sem, n_ready.at(g, 1))
                for t in range(TILES):
                    last = pe.transpose(pe_[:, t * P:(t + 1) * P], nrm[:, t, :], ident)
                last.then_inc(n_turned.sem, 1)
                pe.wait_ge(nt_ready.sem, nt_ready.at(g, 1))
                pe.wait_ge(r2_ready.sem, r2_ready.at(g, 0))
                for p in range(NP):
                    if p >= 2:
                        pe.wait_ge(q_kept.sem, q_kept.at(g, p - 1))
                    pe.matmul(pa[:, 512 * (p % 2):512 * (p % 2) + 512], w("q0", P * p, P * p + P), tT[:, :],
                              start=True, stop=True).then_inc(q_made.sem, 1)
                    if p >= 2:
                        pe.wait_ge(k_kept.sem, k_kept.at(g, p - 1))
                    pe.matmul(pb[:, 512 * (p % 2):512 * (p % 2) + 512], w("k0", P * p, P * p + P), tT[:, :],
                              start=True, stop=True).then_inc(k_made.sem, 1)

                def values(t):
                    if t == 0:
                        pe.wait_ge(q_kept.sem, q_kept.at(g, NP))
                    else:
                        pe.wait_ge(v_kept.sem, v_kept.at(g, t))
                    for c in range(2):
                        last = pe.matmul(pa[:, 512 * c:512 * c + 512], tT[:, t * P:(t + 1) * P],
                                         w("v0", 512 * c, 512 * c + 512), start=True, stop=True)
                    last.then_inc(v_made.sem, 1)

                def scores(t):
                    if t == 0:
                        pe.wait_ge(k_kept.sem, k_kept.at(g, NP))
                    else:
                        pe.wait_ge(s_shifted.sem, s_shifted.at(g, t))
                    for c in range(2):
                        pe.matmul(pc[:, 512 * c:512 * c + 512], ident16, causal_t, start=True, stop=False,
                                  skip_group_check=True)
                    for p in range(NP):
                        for b in range(2):
                            at = t * P + b * S
                            last = pe.matmul(pc[S * b:S * b + S, P * p:P * p + P], kt[:, p, at:at + S],
                                             qblk[:, p, :, at:at + S], start=False, stop=(p % 4 == 3),
                                             skip_group_check=True)
                    last.then_inc(s_made.sem, 1)

                def attend(t):
                    pe.wait_ge(p_ready.sem, p_ready.at(g, 2 * t + 2))
                    pe.wait_ge(v_kept.sem, v_kept.at(g, t + 1))
                    if t >= 1:
                        pe.wait_ge(z_kept.sem, z_kept.at(g, t))
                    for h in range(NH):
                        last = pe.matmul(pb[S * (h % 2):S * (h % 2) + S, P * (h // 2):P * (h // 2) + P],
                                         v[:, t % 2, DH * h:DH * h + DH],
                                         pblk[:, h, :, :], start=True, stop=True)
                    last.then_inc(z_made.sem, 1)

                def project(t):
                    pe.wait_ge(z_kept.sem, z_kept.at(g, t + 1))
                    for p in range(NP):
                        last = pe.matmul(pd[:, t * P:t * P + P], zta[t % 2][:, p, :], w("o0", P * p, P * p + P),
                                         start=(p == 0), stop=(p == NP - 1))
                    if t == TILES - 1:
                        last.then_inc(o_made.sem, 1)

                for t in range(TILES + 2):
                    if t < TILES:
                        values(t)
                        scores(t)
                    if 1 <= t <= TILES:
                        attend(t - 1)
                    if t >= 2:
                        project(t - 2)

                pe.wait_ge(c_loaded.sem, c_loaded.at(g, 16))
                ctxt = flat(c_in)
                pe.wait_ge(v_kept.sem, v_kept.at(g, TILES))
                pe.matmul(pa[:, 512:1024], w("xk"), ctxt, start=True, stop=True).then_inc(kx_made.sem, 1)
                for b in range(SEQ):
                    for e in range(2):
                        last = pe.matmul(pb[S * e:S * e + S, P * b:P * b + P], ctxt[:, S * b:S * b + S], w("xv"),
                                         start=True, stop=True)
                last.then_inc(vx_made.sem, 1)
                pe.wait_ge(x1_ready.sem, x1_ready.at(g, 1))
                for t in range(TILES):
                    last = pe.transpose(pe_[:, t * P:(t + 1) * P], x1[:, t, :], ident)
                last.then_inc(x1_turned.sem, 1)
                pe.wait_ge(x1t_ready.sem, x1t_ready.at(g, 1))
                pe.matmul(pa[:, 0:512], w("xq"), tT[:, :], start=True, stop=True).then_inc(qx_made.sem, 1)

                def scores_x(t):
                    if t == 0:
                        pe.wait_ge(qx_kept.sem, qx_kept.at(g, 1))
                        pe.wait_ge(kx_kept.sem, kx_kept.at(g, 1))
                    else:
                        pe.wait_ge(sx_shifted.sem, sx_shifted.at(g, t))
                    for q in range(4):
                        for b in range(2):
                            at = t * P + b * S
                            last = pe.matmul(pc[S * b:S * b + S, 256 * q:256 * q + 256], qg[:, q, at:at + S],
                                             kj[:, :, at:at + S], start=True, stop=True)
                    last.then_inc(sx_made.sem, 1)

                def turn_x(t):
                    pe.wait_ge(sx_exp.sem, sx_exp.at(g, t + 1))
                    if t >= 1:
                        pe.wait_ge(px_a.sem, px_a.at(g, t))
                        pe.wait_ge(px_v.sem, px_v.at(g, t))
                    for i in range(NP):
                        last = pe.transpose(pa[:, P * i:P * i + P], st[:, t % 2, P * i:P * i + P], ident)
                    last.then_inc(px_turned.sem, 1)

                def attend_x(t):
                    if t == 0:
                        pe.wait_ge(vx_ready.sem, vx_ready.at(g, 1))
                    else:
                        pe.wait_ge(zx_ready.sem, zx_ready.at(g, t))
                    pe.wait_ge(px_a.sem, px_a.at(g, t + 1))
                    pe.wait_ge(px_v.sem, px_v.at(g, t + 1))
                    for i in range(NP):
                        last = pe.matmul(pd[:, 36 * i:36 * i + 36], pt[t % 2][:, i, :],
                                         vblk[:, 2 * t:2 * t + 2, i, :], start=True, stop=True)
                    last.then_inc(zx_made.sem, 1)

                scores_x(0)
                for t in range(TILES):
                    if t + 1 < TILES:
                        scores_x(t + 1)
                    turn_x(t)
                    if t >= 1:
                        attend_x(t - 1)
                attend_x(TILES - 1)
                pe.wait_ge(zx_ready.sem, zx_ready.at(g, TILES))
                for t in range(TILES):
                    last = pe.transpose(pe_[:, t * P:(t + 1) * P], zx[:, t, :], ident)
                last.then_inc(zx_turned.sem, 1)
                pe.wait_ge(zxt_ready.sem, zxt_ready.at(g, 1))
                for t in range(TILES):
                    last = pe.matmul(pa[:, t * P:(t + 1) * P], tT[:, t * P:(t + 1) * P], w("xo"),
                                     start=True, stop=True)
                last.then_inc(ox_made.sem, 1)
            with pe.Fori(0, G) as g:
                def turn(dst, src, signal):
                    for t in range(TILES):
                        last = pe.transpose(dst[:, t * P:(t + 1) * P], src[:, t, :], ident)
                    last.then_inc(signal.sem, 1)

                pe.wait_ge(cn_ready.sem, cn_ready.at(g, 1))
                turn(pd, y, cn_turned)
                pe.wait_ge(xn_ready.sem, xn_ready.at(g, 1))
                turn(pe_, nrm, xn_turned)
                pe.wait_ge(xq_ready.sem, xq_ready.at(g, 1))
                pe.wait_ge(between.sem, 1)
                for t in range(TILES):
                    last = pe.matmul(pa[:, t * P:(t + 1) * P], tT[:, t * P:(t + 1) * P], wq[:, :],
                                     start=True, stop=True)
                last.then_inc(f_made.sem, 1)
                pe.wait_ge(x3_ready.sem, x3_ready.at(g, 1))
                turn(pe_, x1, x3_turned)
                pe.wait_ge(x3t_ready.sem, x3t_ready.at(g, 1))
                pe.matmul(pb[0:R, 0:512], w("basis"), tT[:, :], start=True, stop=True).then_inc(lat_made.sem, 1)
                for t in range(TILES):
                    last = pe.matmul(pa[:, 512 + t * P:512 + (t + 1) * P], tT[:, t * P:(t + 1) * P], w("v1"),
                                     start=True, stop=True)
                last.then_inc(v1_made.sem, 1)
                pe.matmul(pc[:, 0:512], ident16, causal_1, start=True, stop=False, skip_group_check=True)
                pe.wait_ge(lat_kept.sem, lat_kept.at(g, 1))
                for t in range(TILES):
                    a = slice(t * P, (t + 1) * P)
                    last = pe.matmul(pc[:, a], latt[:, a], latt[:, a], start=False, stop=(t == TILES - 1),
                                     skip_group_check=True)
                last.then_inc(s1_made.sem, 1)
                pe.wait_ge(p1_ready.sem, p1_ready.at(g, 1))
                for t in range(TILES):
                    last = pe.transpose(pe_[:, t * P:(t + 1) * P], st[:, 0, t * P:(t + 1) * P], ident)
                last.then_inc(p1_turned.sem, 1)
                pe.wait_ge(p1t_ready.sem, p1t_ready.at(g, 1))
                pe.wait_ge(v1_kept.sem, v1_kept.at(g, 1))
                for t in range(TILES):
                    last = pe.matmul(pb[:, 512 + t * P:512 + (t + 1) * P], x2[:, t, :], st[:, 1, t * P:(t + 1) * P],
                                     start=True, stop=True)
                last.then_inc(z1_made.sem, 1)
                pe.wait_ge(z1_kept.sem, z1_kept.at(g, 1))
                for t in range(TILES):
                    last = pe.matmul(pa[:, t * P:(t + 1) * P], st[:, 1, 512 + t * P:512 + (t + 1) * P], w("o1"),
                                     start=True, stop=True)
                last.then_inc(o1_made.sem, 1)

                pe.wait_ge(ln_ready.sem, ln_ready.at(g, 1))
                turn(pe_, nrm, ln_turned)
                pe.wait_ge(ln_kept.sem, ln_kept.at(g, 1))

                def queries(t):
                    dst = (pa, pc)[t % 2]
                    if t >= 2:
                        pe.wait_ge(yq_scaled.sem, yq_scaled.at(g, t - 1))
                    for c in range(2):
                        last = pe.matmul(dst[:, 512 * c:512 * c + 512], tT[:, t * P:(t + 1) * P],
                                         w("yq", 512 * c, 512 * c + 512), start=True, stop=True)
                    last.then_inc(yq_made.sem, 1)

                def turn_q(t):
                    pe.wait_ge(yq_scaled.sem, yq_scaled.at(g, t + 1))
                    if t >= 1:
                        pe.wait_ge(yq_a.sem, yq_a.at(g, t))
                        pe.wait_ge(yq_v.sem, yq_v.at(g, t))
                    for p in range(NP):
                        last = pe.transpose(pb[:, P * p:P * p + P], qs[:, P * p:P * p + P], ident)
                    last.then_inc(yq_turned.sem, 1)

                for t in range(TILES + 1):
                    if t < TILES:
                        queries(t)
                    if t >= 1:
                        turn_q(t - 1)

                for c in range(2):
                    if c == 0:
                        pe.wait_ge(yq_a.sem, yq_a.at(g, TILES))
                        pe.wait_ge(yq_v.sem, yq_v.at(g, TILES))
                        pe.wait_ge(lat_placed.sem, lat_placed.at(g, 1))
                        pe.wait_ge(cn_kept.sem, cn_kept.at(g, 1))
                    else:
                        pe.wait_ge(yz_kept.sem, yz_kept.at(g, 4))
                    for p in range(NP + 2):
                        if p < NP:
                            if p >= 2:
                                pe.wait_ge(yk_kept.sem, yk_kept.at(g, NP * c + p - 1))
                            pe.matmul(pb[:, 512 * (p % 2):512 * (p % 2) + 512], w("yk", P * p, P * p + P),
                                      kvt[:, 4 * c:4 * c + 4, :], start=True, stop=True).then_inc(yk_made.sem, 1)
                        if p >= 2:
                            u = p - 2
                            pe.wait_ge(yk_squared.sem, yk_squared.at(g, NP * c + u + 1))
                            row = 32 * (u // 2)
                            pe.matmul(pd[row:row + 32, :], k("sel", 32 * (u % 2), 32 * (u % 2) + 32), sqk[u % 2],
                                      start=(u % 2 == 0), stop=(u % 2 == 1),
                                      skip_group_check=True).then_inc(yk_summed.sem, 1)
                    pe.wait_ge(yk_sum_kept.sem, yk_sum_kept.at(g, c + 1))
                    for i in range(4):
                        last = pe.transpose(pd[:, P * i:P * i + P], st[:, 0, P * i:P * i + P], ident)
                    last.then_inc(yk_sum_turned.sem, 1)
                    pe.wait_ge(yk_kept.sem, yk_kept.at(g, NP * c + NP))

                    def values_y(b):
                        if b >= 1:
                            pe.wait_ge(yv_kept.sem, yv_kept.at(g, b))
                        for h in range(2):
                            last = pe.matmul(pa[:, 512 * h:512 * h + 512], kvt[:, b, :],
                                             w("yv", 512 * h, 512 * h + 512), start=True, stop=True)
                        last.then_inc(yv_made.sem, 1)

                    def scores_y(b):
                        if b >= 1:
                            pe.wait_ge(ys_scaled.sem, ys_scaled.at(g, b))
                        at = P * (b % 4)
                        for p in range(NP):
                            last = pe.matmul(pc[:, P * p:P * p + P], kt[:, p, at:at + P],
                                             qblk[:, p, :, S * b:S * b + S], start=True, stop=True)
                        last.then_inc(ys_made.sem, 1)

                    def attend_y(b):
                        pe.wait_ge(yp_ready.sem, yp_ready.at(g, b + 1))
                        pr = hview(st[:, b % 2, :])
                        if b % 4 == 0:
                            pe.wait_ge(yk_mean.sem, yk_mean.at(g, b // 4 + 1))
                        if b >= 1:
                            pe.wait_ge(yl_inv.sem, yl_inv.at(g, b))
                        for e in range(2):
                            last = pe.matmul(pd[S * e:S * e + S, :], k("ones", 0, S), pr[:, e:NH:2, :],
                                             start=True, stop=True)
                        last.then_inc(yl_made.sem, 1)
                        pe.wait_ge(yv_kept.sem, yv_kept.at(g, b + 1))
                        if b >= 1:
                            pe.wait_ge(yz_kept.sem, yz_kept.at(g, b))
                        for p in range(NP):
                            last = pe.matmul(pb[:, P * p:P * p + P], v[:, b % 2, P * p:P * p + P],
                                             st[:, b % 2, P * p:P * p + P], start=True, stop=True)
                        last.then_inc(yz_made.sem, 1)

                    def project_y(t):
                        pe.wait_ge(yz_kept.sem, yz_kept.at(g, 2 * t + 2))
                        for p in range(NP):
                            last = pe.matmul(pe_[:, t * P:t * P + P], zt[:, p, t * P:t * P + P],
                                             w("yo", P * p, P * p + P), start=(p == 0), stop=(p == NP - 1))
                        if t == TILES - 1:
                            last.then_inc(yo_made.sem, 1)

                    for i in range(6):
                        b = 4 * c + i
                        if i < 4:
                            values_y(b)
                            scores_y(b)
                        if 1 <= i <= 4:
                            attend_y(b - 1)
                        if i in (3, 5):
                            project_y((b - 2) // 2)

                pe.wait_ge(x5_ready.sem, x5_ready.at(g, 1))
                turn(pd, x1, x5_turned)
                pe.wait_ge(x5t_ready.sem, x5t_ready.at(g, 1))
                for t in range(TILES):
                    last = pe.matmul(pc[:, E8 * t:E8 * t + E8], tT[:, t * P:(t + 1) * P], w("gate"),
                                     start=True, stop=True)
                last.then_inc(gate_made.sem, 1)

                def experts(t):
                    dst = (pa, pb)[t % 2]
                    if t >= 2:
                        pe.wait_ge(e_scaled.sem, e_scaled.at(g, t - 1))
                    for c in range(2):
                        last = pe.matmul(dst[:, 512 * c:512 * c + 512], tT[:, t * P:(t + 1) * P],
                                         w("exp", 512 * c, 512 * c + 512), start=True, stop=True)
                    last.then_inc(e_made.sem, 1)

                experts(0)
                experts(1)
                pe.wait_ge(cw_ready.sem, cw_ready.at(g, 1))
                for t in range(TILES):
                    last = pe.transpose(pc[0:E8, 512 + t * P:512 + (t + 1) * P], cw[:, t, :], ident)
                last.then_inc(cw_turned.sem, 1)
                pe.wait_ge(cwt_ready.sem, cwt_ready.at(g, 1))
                for t in range(TILES):
                    last = pe.matmul(pd[:, t * P:(t + 1) * P], cwt[:, t * P:(t + 1) * P], be_sb[:, :],
                                     start=True, stop=True)
                last.then_inc(be_made.sem, 1)
                experts(2)
                experts(3)
                pe.wait_ge(x6_stat.sem, x6_stat.at(g, 1))

        @block.scalar
        def _(act):
            act.wait_ge(loaded.sem, 80)
            act.wait_ge(setup.sem, 2)
            with act.Fori(0, G) as g:
                own = Chain(act, act_own)
                act.wait_ge(x_loaded.sem, x_loaded.at(g, 16))
                for t in range(TILES):
                    last = act.activation(junk[:, t, :], x_in[:, t, :], ACT.Square, accum_out=ssq[:, t:t + 1])
                own(last)
                own(act.activation(lnv, ssq, ACT.Ln, scale=1.0 / D, bias=k("eps0")))
                act.activation(rms, lnv, ACT.Exp, scale=-0.5).then_inc(rms_ready.sem, 1)
                for p in range(NP):
                    act.wait_ge(q_made.sem, q_made.at(g, p + 1))
                    for e in range(2):
                        r = slice(DH * e, DH * e + DH)
                        last = act.activation(qblk[r, p, e, :], pa[r, 512 * (p % 2):512 * (p % 2) + 512],
                                              ACT.Identity, bias=w("bq0", p, p + 1)[r])
                    last.then_inc(q_kept.sem, 1)
                for t in range(TILES + 1):
                    if t < TILES:
                        act.wait_ge(s_shifted.sem, s_shifted.at(g, t + 1))
                        act.activation(st[:, t % 2, :], st[:, t % 2, :], ACT.Exp).then_inc(s_exp.sem, 1)
                    if t >= 1:
                        act.wait_ge(z_made.sem, z_made.at(g, t))
                        act.activation(zta[(t - 1) % 2].rearrange("p a n -> p (a n)"), pb[:, :],
                                       ACT.Copy).then_inc(z_kept.sem, 1)
                act.wait_ge(stat1.sem, stat1.at(g, 1))
                own(act.activation(lnv, mv[:, :, 1], ACT.Ln, bias=k("eps5")))
                act.activation(rstd, lnv, ACT.Exp, scale=-0.5).then_inc(rstd1.sem, 1)
                act.wait_ge(qx_made.sem, qx_made.at(g, 1))
                for j in range(4):
                    last = act.activation(qg[:, j, :], pa[:, 0:512], ACT.Identity, scale=mqs[:, j:j + 1],
                                          bias=bxqm[:, j:j + 1])
                last.then_inc(qx_kept.sem, 1)
                for t in range(TILES + 1):
                    if t < TILES:
                        act.wait_ge(sx_shifted.sem, sx_shifted.at(g, t + 1))
                        act.activation(st[:, t % 2, :], st[:, t % 2, :], ACT.Exp).then_inc(sx_exp.sem, 1)
                    if t >= 1:
                        act.wait_ge(px_turned.sem, px_turned.at(g, t))
                        act.activation(pt[(t - 1) % 2][:, 0:4, :].rearrange("p a n -> p (a n)"), pa[:, 0:512],
                                       ACT.Copy).then_inc(px_a.sem, 1)
                act.wait_ge(zx_turned.sem, zx_turned.at(g, 1))
                act.activation(tT[:, :], pe_[:, :], ACT.Copy).then_inc(zxt_ready.sem, 1)
                act.wait_ge(r2_ready.sem, r2_ready.at(g, 1))
                own(act.activation(lnv, mv[:, :, 1], ACT.Ln, bias=k("eps5")))
                act.activation(rstd, lnv, ACT.Exp, scale=-0.5).then_inc(rstd2.sem, 1)
                act.wait_ge(stat3.sem, stat3.at(g, 1))
                own(act.activation(lnv, mv[:, :, 1], ACT.Ln, bias=k("eps3")))
                act.activation(rstdf, lnv, ACT.Exp, scale=-0.5).then_inc(rstd3.sem, 1)
                own.done()
            act.activation(fold[:, D:2 * D], w("ffn"), ACT.Abs, accum_out=ffs[:, 0:1]).then_inc(weight_sum.sem, 1)
            with act.Fori(0, G) as g:
                own = Chain(act, act_own)

                def root(before, eps, signal, dst=rstd):
                    act.wait_ge(before.sem, before.at(g, 1))
                    own(act.activation(lnv, mv[:, :, 1], ACT.Ln, bias=k(eps)))
                    act.activation(dst, lnv, ACT.Exp, scale=-0.5).then_inc(signal.sem, 1)

                root(cn_stat, "eps5", cn_rstd)
                act.wait_ge(cn_turned.sem, cn_turned.at(g, 1))
                act.activation(kvt[:, :, 0:S], hview(pd[:, :]), ACT.Identity, scale=w("gx"),
                               bias=w("bx")).then_inc(cn_kept.sem, 1)
                root(x3_stat, "eps5", x3_rstd)
                act.wait_ge(lat_made.sem, lat_made.at(g, 1))
                act.activation(latt[:, :], pb[0:R, 0:512], ACT.Copy).then_inc(lat_kept.sem, 1)
                act.wait_ge(s1_shifted.sem, s1_shifted.at(g, 1))
                act.activation(st[:, 0, 0:512], st[:, 0, 0:512], ACT.Exp, scale=R ** -0.5).then_inc(s1_exp.sem, 1)
                act.wait_ge(p1_turned.sem, p1_turned.at(g, 1))
                act.activation(st[:, 1, 0:512], pe_[:, :], ACT.Copy).then_inc(p1t_ready.sem, 1)
                act.wait_ge(z1_made.sem, z1_made.at(g, 1))
                act.activation(st[:, 1, 512:1024], pb[:, 512:1024], ACT.Identity,
                               bias=w("bv1")).then_inc(z1_kept.sem, 1)
                root(x4_stat, "eps5", x4_rstd)
                root(ln_stat, "eps5", ln_rstd)
                act.wait_ge(ln_turned.sem, ln_turned.at(g, 1))
                act.activation(tT[:, :], pe_[:, :], ACT.Identity, scale=w("gl"),
                               bias=w("bl")).then_inc(ln_kept.sem, 1)
                for t in range(TILES + 1):
                    if t < TILES:
                        src = (pa, pc)[t % 2]
                        act.wait_ge(yq_made.sem, yq_made.at(g, t + 1))
                        act.activation(sqt, src[:, :], ACT.Square).then_inc(yq_squared.sem, 1)
                        act.wait_ge(yq_sum.sem, yq_sum.at(g, t + 1))
                        own(act.activation(rq, mx[:, t % 2, :], ACT.Ln))
                        act.activation(rq, rq, ACT.Exp, scale=-0.5).then_inc(yq_root.sem, 1)
                    if t >= 1:
                        act.wait_ge(yq_turned.sem, yq_turned.at(g, t))
                        act.activation(qblk[0:DH, :, 0, (t - 1) * P:t * P], hview(pb[0:DH, :], P), ACT.Copy,
                                       scale=gqk[0:DH]).then_inc(yq_a.sem, 1)
                for c in range(2):
                    for p in range(NP):
                        act.wait_ge(yk_made.sem, yk_made.at(g, NP * c + p + 1))
                        act.activation(kt[:, p, :], pb[:, 512 * (p % 2):512 * (p % 2) + 512],
                                       ACT.Copy).then_inc(yk_kept.sem, 1)
                    act.wait_ge(yk_summed.sem, yk_summed.at(g, NP * c + NP))
                    act.activation(st[:, 0, 0:512], pd[:, :], ACT.Copy).then_inc(yk_sum_kept.sem, 1)
                    act.wait_ge(yk_mean.sem, yk_mean.at(g, c + 1))
                    own(act.activation(rkl, rk, ACT.Ln))
                    act.activation(rk, rkl, ACT.Exp, scale=-0.5).then_inc(yk_root.sem, 1)
                    for i in range(4):
                        b = 4 * c + i
                        act.wait_ge(yv_made.sem, yv_made.at(g, b + 1))
                        if b >= 2:
                            act.wait_ge(yz_made.sem, yz_made.at(g, b - 1))
                        act.activation(v[:, b % 2, :], pa[:, :], ACT.Copy).then_inc(yv_kept.sem, 1)
                        act.wait_ge(ys_scaled.sem, ys_scaled.at(g, b + 1))
                        act.activation(st[:, b % 2, :], st[:, b % 2, :], ACT.Exp,
                                       bias=mbl[:, b:b + 1]).then_inc(yp_ready.sem, 1)
                root(x5_stat, "eps5", x5_rstd)
                act.wait_ge(gap_ready.sem, gap_ready.at(g, 1))
                act.activation(p2, p2, ACT.Exp).then_inc(gap_exp.sem, 1)
                act.wait_ge(cw_turned.sem, cw_turned.at(g, 1))
                act.activation(cwt[:, :], pc[0:E8, 512:1024], ACT.Copy).then_inc(cwt_ready.sem, 1)
                root(x6_stat, "eps5", x6_rstd)
                own.done()

        @block.gpsimd
        def _(pool):
            pool.memset(qblk[:, :, :, :], 0.0)
            pool.memset(pblk[:, :, :, :], 0.0)
            pool.memset(peaks, 0.0)
            pool.memset(y[:, :, :], 0.0).then_inc(setup.sem, 1)
            pool.wait_ge(loaded.sem, 80)
            pool.wait_ge(setup.sem, 2)
            with pool.Fori(0, G) as g:
                own = Chain(pool, pool_own)
                pool.wait_ge(x_loaded.sem, x_loaded.at(g, 16))
                pool.tensor_tensor(xb[:, :, :], x_in[:, :, :], tiled(w("ro0"), TILES), ALU.add).then_inc(xb_ready.sem, 1)
                pool.wait_ge(xb_ready.sem, xb_ready.at(g, 1))
                for t in range(TILES):
                    pool.wait_ge(s_norm.sem, s_norm.at(g, t + 1))
                    if t >= 1:
                        pool.wait_ge(z_made.sem, z_made.at(g, t))
                    for b in range(2):
                        r = slice(S * b, S * b + S)
                        pool.tensor_tensor(pblk[r, :, b, :], hview(st[r, t % 2, :]), over(rs[r, t % 2, :], S),
                                           ALU.mult).then_inc(p_ready.sem, 1)
                        pool.wait_ge(p_ready.sem, p_ready.at(g, 2 * t + b + 1))
                pool.wait_ge(x1_ready.sem, x1_ready.at(g, 1))
                pool.tensor_tensor(xb[:, :, :], x1[:, :, :], tiled(w("rxo"), TILES), ALU.add).then_inc(x1b_ready.sem, 1)
                pool.wait_ge(vx_masked.sem, vx_masked.at(g, 1))
                pool.tensor_tensor(vdata, vdata, tiled(vbias, SEQ).rearrange("p b (i n) -> p b i n", n=16),
                                   ALU.add).then_inc(vx_ready.sem, 1)
                pool.wait_ge(rstd3.sem, rstd3.at(g, 1))
                pool.wait_ge(peak_kept.sem, peak_kept.at(g, 1))
                pool.sem_inc(pool_hold, 1)
                pool.tensor_copy(state[:, bass.ds(g * GT, GT)], flat(x2))
                pool.tensor_copy(fstat[:, bass.ds(g * 8, 4)], mv[:, :, 0])
                pool.tensor_copy(fstat[:, bass.ds(g * 8 + 4, 4)], rstdf)
                for t in range(TILES):
                    last = pool.tensor_scalar(y[:, t, :], x2[:, t, :], mv[:, t, 0:1], rstdf[:, t:t + 1],
                                              ALU.subtract, ALU.mult)
                own(last)
                own(pool.tensor_tensor(y[:, :, :], y[:, :, :], tiled(w("rfg"), TILES), ALU.mult))
                pool.tensor_tensor(y[:, :, :], y[:, :, :], tiled(w("rfb"), TILES), ALU.add).then_inc(peak_done.sem, 1)
                own.done()
            pool.wait_ge(peak_local.sem, 1)
            pool.wait_ge(weight_sum.sem, 1)
            pool.partition_all_reduce(ffs[:, 1:2], ffs[:, 3:4], P, bass.bass_isa.ReduceOp.max)
            pool.partition_all_reduce(ffs[:, 2:3], ffs[:, 0:1], P, bass.bass_isa.ReduceOp.add).then_inc(peak_all.sem, 1)
            with pool.Fori(0, G) as g:
                own = Chain(pool, pool_own)
                pool.wait_ge(z1_made.sem, z1_made.at(g, 0))
                pool.wait_ge(yp_ready.sem, yp_ready.at(g, 0))
                pool.sem_inc(pool_hold, 1)
                pool.tensor_copy(flat(x2), state[:, bass.ds(g * GT, GT)])
                pool.tensor_copy(mbl, maskb[:, bass.ds(g * SEQ, SEQ)])
                own(pool.tensor_copy(fstl, fstat[:, bass.ds(g * 8, 8)]))
                pool.wait_ge(ln_turned.sem, ln_turned.at(g, 0))
                for t in range(TILES):
                    last = pool.tensor_scalar(nrm[:, t, :], x2[:, t, :], fstl[:, t:t + 1], fstl[:, 4 + t:5 + t],
                                              ALU.subtract, ALU.mult)
                own(last)
                own(pool.tensor_tensor(nrm[:, :, :], nrm[:, :, :], tiled(w("rfg"), TILES), ALU.mult))
                pool.tensor_tensor(nrm[:, :, :], nrm[:, :, :], tiled(w("rfb"), TILES), ALU.add).then_inc(xn_ready.sem, 1)
                pool.wait_ge(x3_ready.sem, x3_ready.at(g, 1))
                pool.tensor_tensor(xb[:, :, :], x1[:, :, :], tiled(w("ro1"), TILES), ALU.add).then_inc(x3b_ready.sem, 1)
                pool.wait_ge(x4_ready.sem, x4_ready.at(g, 1))
                pool.tensor_tensor(xb[:, :, :], zx[:, :, :], tiled(w("ryo"), TILES), ALU.add).then_inc(x4b_ready.sem, 1)
                pool.wait_ge(ln_kept.sem, ln_kept.at(g, 1))
                pool.sem_inc(pool_hold, 1)
                pool.tensor_copy(kvt[:, :, S:2 * S], hview(tT[:, :])).then_inc(lat_placed.sem, 1)
                for p in range(2 * NP):
                    pool.wait_ge(yk_kept.sem, yk_kept.at(g, p + 1))
                    if p == 0:
                        pool.wait_ge(yq_turned.sem, yq_turned.at(g, TILES))
                    if p == NP:
                        pool.wait_ge(yl_inv.sem, yl_inv.at(g, 4))
                        pool.wait_ge(yz_kept.sem, yz_kept.at(g, 4))
                    if p % NP >= 2:
                        pool.wait_ge(yk_summed.sem, yk_summed.at(g, p - 1))
                    pool.tensor_tensor(sqk[p % 2], kt[:, p % NP, :], kt[:, p % NP, :],
                                       ALU.mult).then_inc(yk_squared.sem, 1)
                own.done()

        @block.vector
        def _(dve):
            dve.wait_ge(loaded.sem, 80)
            dve.tensor_scalar(mqs, k("maskq"), float(DX) ** -0.5, None, ALU.mult).then_inc(gap_s.sem, 1)
            dve.wait_ge(gap_s.sem, 1)
            dve.tensor_scalar(bxqm, mqs, w("bxq"), None, ALU.mult)
            dve.tensor_tensor(vbias, k("mask2"), w("rxv"), ALU.mult)
            dve.tensor_copy(vblk[:, :, :, 16:18].rearrange("p b i n -> p (b i) n"), tiled(k("half"), SEQ * NP))
            dve.tensor_scalar(gqk, w("qg"), w("kg"), float(DH) ** -0.5, ALU.mult, ALU.mult)
            dve.memset(maskb[S:P, :], 0.0)
            dve.tensor_scalar(maskb[0:S, :], mask8[:, :], -1.0, 1e30, ALU.add, ALU.mult).then_inc(setup.sem, 1)

            with dve.Fori(0, G) as g:
                own = Chain(dve, dve_own)

                def norm_stats(src, signal):
                    for t in range(TILES):
                        last = dve.bn_stats(stats[:, t, :], src[:, t, :])
                    own(last)
                    for t in range(TILES):
                        last = dve.bn_aggr(mv[:, t, :], stats[:, t, :])
                    last.then_inc(signal.sem, 1)

                def norm_apply(dst, src, before, signal):
                    dve.wait_ge(before.sem, before.at(g, 1))
                    for t in range(TILES):
                        last = dve.tensor_scalar(dst[:, t, :], src[:, t, :], mv[:, t, 0:1], rstd[:, t:t + 1],
                                                 ALU.subtract, ALU.mult)
                    last.then_inc(signal.sem, 1)

                dve.wait_ge(rms_ready.sem, rms_ready.at(g, 1))
                dve.tensor_tensor(nrm[:, :, :], x_in[:, :, :], over(rms, D), ALU.mult).then_inc(n_ready.sem, 1)
                dve.wait_ge(n_turned.sem, n_turned.at(g, 1))
                dve.tensor_copy(tT[:, :], pe_[:, :]).then_inc(nt_ready.sem, 1)
                for p in range(NP):
                    dve.wait_ge(k_made.sem, k_made.at(g, p + 1))
                    dve.tensor_scalar(kt[:, p, :], pb[:, 512 * (p % 2):512 * (p % 2) + 512], w("bk0", p, p + 1), None,
                                      ALU.add).then_inc(k_kept.sem, 1)
                for t in range(TILES + 1):
                    if t < TILES:
                        dve.wait_ge(v_made.sem, v_made.at(g, t + 1))
                        dve.tensor_tensor(v[:, t % 2, :], pa[:, :], w("rv0"), ALU.add).then_inc(v_kept.sem, 1)
                        dve.wait_ge(s_made.sem, s_made.at(g, t + 1))
                        own(dve.tensor_reduce(mx[:, t % 2, :], hview(pc[:, :]), AX.X, ALU.max))
                        if t >= 2:
                            dve.wait_ge(p_ready.sem, p_ready.at(g, 2 * t - 2))
                        dve.tensor_tensor(hview(st[:, t % 2, :]), hview(pc[:, :]), over(mx[:, t % 2, :], S),
                                          ALU.subtract).then_inc(s_shifted.sem, 1)
                    if t >= 1:
                        u = t - 1
                        dve.wait_ge(s_exp.sem, s_exp.at(g, u + 1))
                        own(dve.tensor_reduce(sm[:, u % 2, :], hview(st[:, u % 2, :]), AX.X, ALU.add))
                        if u >= 2:
                            dve.wait_ge(p_ready.sem, p_ready.at(g, 2 * u - 2))
                        dve.reciprocal(rs[:, u % 2, :], sm[:, u % 2, :]).then_inc(s_norm.sem, 1)
                dve.wait_ge(o_made.sem, o_made.at(g, 1))
                dve.wait_ge(xb_ready.sem, xb_ready.at(g, 1))
                dve.wait_ge(peak_done.sem, peak_done.at(g, 0))
                dve.tensor_reduce(peak[:, 0:1], flat(y), AX.X, ALU.max)
                own(dve.tensor_reduce(peak[:, 1:2], flat(y), AX.X, ALU.min))
                dve.tensor_tensor(peaks[:, 0:1], peaks[:, 0:1], peak[:, 0:1], ALU.max)
                dve.tensor_tensor(peaks[:, 1:2], peaks[:, 1:2], peak[:, 1:2], ALU.min).then_inc(peak_kept.sem, 1)
                own(dve.tensor_tensor(flat(res), pd[:, :], flat(xb), ALU.add))
                norm_stats(res, stat1)
                norm_apply(x1, res, rstd1, x1_ready)
                dve.wait_ge(x1_turned.sem, x1_turned.at(g, 1))
                dve.tensor_copy(tT[:, :], pe_[:, :]).then_inc(x1t_ready.sem, 1)
                dve.wait_ge(kx_made.sem, kx_made.at(g, 1))
                for j in range(4):
                    last = dve.tensor_scalar(kj[:, j, :], pa[:, 512:1024], w("bxk"), k("mask4", j, j + 1), ALU.add,
                                             ALU.mult)
                last.then_inc(kx_kept.sem, 1)
                dve.wait_ge(vx_made.sem, vx_made.at(g, 1))
                dve.tensor_tensor(vdata, pb[:, :].rearrange("p (b i n) -> p b i n", b=SEQ, n=16),
                                  tiled(k("mask2"), SEQ).rearrange("p b (i n) -> p b i n", n=16),
                                  ALU.mult).then_inc(vx_masked.sem, 1)
                for t in range(TILES + 2):
                    if t < TILES:
                        dve.wait_ge(sx_made.sem, sx_made.at(g, t + 1))
                        own(dve.tensor_reduce(mx[:, t % 2, :], hview(pc[:, :]), AX.X, ALU.max))
                        dve.tensor_tensor(hview(st[:, t % 2, :]), hview(pc[:, :]), over(mx[:, t % 2, :], S),
                                          ALU.subtract).then_inc(sx_shifted.sem, 1)
                    if 1 <= t <= TILES:
                        dve.wait_ge(px_turned.sem, px_turned.at(g, t))
                        dve.tensor_copy(pt[(t - 1) % 2][:, 4:8, :].rearrange("p a n -> p (a n)"),
                                        pa[:, 512:1024]).then_inc(px_v.sem, 1)
                    if t >= 2:
                        u = t - 2
                        dve.wait_ge(zx_made.sem, zx_made.at(g, u + 1))
                        for b in range(2):
                            r = slice(S * b, S * b + S)
                            col = pd[r, 0:36 * NP].rearrange("p (i n) -> p i n", n=36)
                            last = dve.reciprocal(rz[r], col[:, :, 18 * b + 16:18 * b + 18])
                        own(last)
                        for b in range(2):
                            r = slice(S * b, S * b + S)
                            col = pd[r, 0:36 * NP].rearrange("p (i n) -> p i n", n=36)
                            last = dve.tensor_tensor(
                                zx[r, u, :].rearrange("p (i e d) -> p i e d", e=2, d=DX),
                                col[:, :, 18 * b:18 * b + 16].rearrange("p i (e d) -> p i e d", d=DX),
                                rz[r].unsqueeze(3).broadcast_to([S, NP, 2, DX]), ALU.mult)
                        last.then_inc(zx_ready.sem, 1)
                dve.wait_ge(ox_made.sem, ox_made.at(g, 1))
                dve.wait_ge(x1b_ready.sem, x1b_ready.at(g, 1))
                own(dve.tensor_tensor(flat(res), pa[:, 0:512], flat(xb), ALU.add))
                norm_stats(res, r2_ready)
                norm_apply(x2, res, rstd2, x2_ready)
                dve.wait_ge(x2_ready.sem, x2_ready.at(g, 1))
                norm_stats(x2, stat3)
                own.done()

            dve.wait_ge(peak_done.sem, G + peak_done.lead)
            steps = [0]

            def link(ins):
                steps[0] += 1
                ins.then_inc(gap_v.sem, 1)
                dve.wait_ge(gap_v.sem, steps[0])

            dve.tensor_reduce(peak[:, 0:1], flat(y), AX.X, ALU.max)
            link(dve.tensor_reduce(peak[:, 1:2], flat(y), AX.X, ALU.min))
            link(dve.tensor_tensor(ffs[:, 4:5], peaks[:, 0:1], peak[:, 0:1], ALU.max))
            link(dve.tensor_tensor(ffs[:, 5:6], peaks[:, 1:2], peak[:, 1:2], ALU.min))
            dve.scalar_tensor_tensor(ffs[:, 3:4], ffs[:, 5:6], -1.0, ffs[:, 4:5], ALU.mult,
                                     ALU.max).then_inc(peak_local.sem, 1)
            dve.wait_ge(peak_all.sem, 1)
            link(dve.reciprocal(ffs[:, 4:5], ffs[:, 1:2]))
            link(dve.tensor_scalar(ffs[:, 4:5], ffs[:, 4:5], QB, None, ALU.mult))
            link(dve.tensor_scalar(ffs[:, 5:6], ffs[:, 2:3], 1.0 / (D * D), None, ALU.mult))
            link(dve.tensor_scalar(ffs[:, 6:7], ffs[:, 5:6], ffs[:, 1:2], 1.0 / QB, ALU.mult, ALU.mult))
            link(dve.tensor_scalar(ffs[:, 7:8], ffs[:, 5:6], 1e-5, None, ALU.add))
            link(dve.reciprocal(ffs[:, 7:8], ffs[:, 7:8]))
            link(dve.tensor_scalar(wq[:, :], w("ffn"), ffs[:, 7:8], None, ALU.mult))
            link(dve.tensor_scalar(wq[:, :], wq[:, :], 12582912.0, None, ALU.add))
            link(dve.tensor_scalar(wq[:, :], wq[:, :], -12582912.0, None, ALU.add))
            dve.tensor_scalar(wq[:, :], wq[:, :], 1.0, -1.0, ALU.min, ALU.max).then_inc(between.sem, 1)
            dve.wait_ge(between.sem, 1)

            with dve.Fori(0, G) as g:
                own = Chain(dve, dve_own)

                def norm_stats(src, signal):
                    for t in range(TILES):
                        last = dve.bn_stats(stats[:, t, :], src[:, t, :])
                    own(last)
                    for t in range(TILES):
                        last = dve.bn_aggr(mv[:, t, :], stats[:, t, :])
                    last.then_inc(signal.sem, 1)

                def norm_apply(dst, src, before, signal):
                    dve.wait_ge(before.sem, before.at(g, 1))
                    for t in range(TILES):
                        last = dve.tensor_scalar(dst[:, t, :], src[:, t, :], mv[:, t, 0:1], rstd[:, t:t + 1],
                                                 ALU.subtract, ALU.mult)
                    last.then_inc(signal.sem, 1)

                dve.wait_ge(cb_loaded.sem, cb_loaded.at(g, 16))
                norm_stats(c_in, cn_stat)
                norm_apply(y, c_in, cn_rstd, cn_ready)
                dve.wait_ge(xn_turned.sem, xn_turned.at(g, 1))
                own(dve.tensor_scalar(tT[:, :], pe_[:, :], ffs[:, 4:5], QB - 1e-5, ALU.mult, ALU.min))
                dve.tensor_scalar(tT[:, :], tT[:, :], -QB + 1e-5, None, ALU.max).then_inc(xq_ready.sem, 1)
                dve.wait_ge(f_made.sem, f_made.at(g, 1))
                own(dve.scalar_tensor_tensor(flat(res), pa[:, 0:512], ffs[:, 6:7], flat(x2), ALU.mult, ALU.add))
                norm_stats(res, x3_stat)
                norm_apply(x1, res, x3_rstd, x3_ready)
                dve.wait_ge(x3_turned.sem, x3_turned.at(g, 1))
                dve.tensor_copy(tT[:, :], pe_[:, :]).then_inc(x3t_ready.sem, 1)
                dve.wait_ge(v1_made.sem, v1_made.at(g, 1))
                dve.tensor_copy(flat(x2), pa[:, 512:1024]).then_inc(v1_kept.sem, 1)
                dve.wait_ge(s1_made.sem, s1_made.at(g, 1))
                own(dve.tensor_reduce(mx[:, 0, 0:TILES], hview(pc[:, 0:512], P), AX.X, ALU.max))
                dve.tensor_tensor(hview(st[:, 0, 0:512], P), hview(pc[:, 0:512], P), over(mx[:, 0, 0:TILES], P),
                                  ALU.subtract).then_inc(s1_shifted.sem, 1)
                dve.wait_ge(s1_exp.sem, s1_exp.at(g, 1))
                own(dve.tensor_reduce(sm[:, 0, 0:TILES], hview(st[:, 0, 0:512], P), AX.X, ALU.add))
                own(dve.reciprocal(sm[:, 0, 0:TILES], sm[:, 0, 0:TILES]))
                dve.tensor_tensor(hview(st[:, 0, 0:512], P), hview(st[:, 0, 0:512], P), over(sm[:, 0, 0:TILES], P),
                                  ALU.mult).then_inc(p1_ready.sem, 1)
                dve.wait_ge(o1_made.sem, o1_made.at(g, 1))
                dve.wait_ge(x3b_ready.sem, x3b_ready.at(g, 1))
                own(dve.tensor_tensor(flat(res), pa[:, 0:512], flat(xb), ALU.add))
                norm_stats(res, x4_stat)
                dve.wait_ge(stored.sem, stored.at(g, 0))
                norm_apply(zx, res, x4_rstd, x4_ready)
                dve.wait_ge(x4_ready.sem, x4_ready.at(g, 1))
                norm_stats(zx, ln_stat)
                norm_apply(nrm, zx, ln_rstd, ln_ready)
                for t in range(TILES + 1):
                    if t < TILES:
                        src = (pa, pc)[t % 2]
                        dve.wait_ge(yq_squared.sem, yq_squared.at(g, t + 1))
                        own(dve.tensor_reduce(sm[:, t % 2, :], hview(sqt), AX.X, ALU.add))
                        dve.tensor_scalar(mx[:, t % 2, :], sm[:, t % 2, :], 1.0 / DH, 1e-16, ALU.mult, ALU.max).then_inc(yq_sum.sem, 1)
                    if t >= 1:
                        dve.wait_ge(yq_turned.sem, yq_turned.at(g, t))
                        dve.tensor_scalar(qblk[DH:P, :, 1, (t - 1) * P:t * P], hview(pb[DH:P, :], P), gqk[DH:P],
                                          None, ALU.mult).then_inc(yq_v.sem, 1)
                    if t < TILES:
                        dve.wait_ge(yq_root.sem, yq_root.at(g, t + 1))
                        dve.tensor_tensor(hview(qs), hview(src[:, :]), over(rq, DH),
                                          ALU.mult).then_inc(yq_scaled.sem, 1)
                for c in range(2):
                    dve.wait_ge(yk_sum_turned.sem, yk_sum_turned.at(g, c + 1))
                    dve.tensor_scalar(rk.rearrange("p b (r n) -> p b r n", n=4),
                                      pd[:, :].rearrange("p (b r n) -> p b r n", b=4, n=32)[:, :, :, 0:4],
                                      1.0 / DH, 1e-16, ALU.mult, ALU.max).then_inc(yk_mean.sem, 1)
                    dve.wait_ge(yk_root.sem, yk_root.at(g, c + 1))
                    for i in range(5):
                        b = 4 * c + i
                        if i < 4:
                            dve.wait_ge(ys_made.sem, ys_made.at(g, b + 1))
                            if b >= 2:
                                dve.wait_ge(yz_made.sem, yz_made.at(g, b - 1))
                            dve.tensor_tensor(hview(st[:, b % 2, :]), hview(pc[:, :]), over(rk[:, i, :], S),
                                              ALU.mult).then_inc(ys_scaled.sem, 1)
                        if i >= 1:
                            u = b - 1
                            dve.wait_ge(yl_made.sem, yl_made.at(g, u + 1))
                            dve.reciprocal(sqk[u % 2], pd[:, :]).then_inc(yl_inv.sem, 1)
                            dve.wait_ge(yl_inv.sem, yl_inv.at(g, u + 1))
                            dve.wait_ge(yz_made.sem, yz_made.at(g, u + 1))
                            for e in range(2):
                                r = slice(DH * e, DH * e + DH)
                                last = dve.tensor_tensor(
                                    zt[r, :, S * u:S * u + S],
                                    pb[r, :].rearrange("p (a e n) -> p a e n", e=2, n=S)[:, :, e, :],
                                    hview(sqk[u % 2][r]), ALU.mult)
                            last.then_inc(yz_kept.sem, 1)
                dve.wait_ge(yo_made.sem, yo_made.at(g, 1))
                dve.wait_ge(x4b_ready.sem, x4b_ready.at(g, 1))
                own(dve.tensor_tensor(flat(res), pe_[:, :], flat(xb), ALU.add))
                norm_stats(res, x5_stat)
                norm_apply(x1, res, x5_rstd, x5_ready)
                dve.wait_ge(x5_turned.sem, x5_turned.at(g, 1))
                dve.tensor_copy(tT[:, :], pd[:, :]).then_inc(x5t_ready.sem, 1)
                dve.wait_ge(gate_made.sem, gate_made.at(g, 1))
                own(dve.tensor_copy(lg.rearrange("p t e -> p (t e)"), pc[:, 0:TILES * E8]))
                for t in range(TILES):
                    last = dve.max(top[:, t, :], lg[:, t, :])
                own(last)
                for t in range(TILES):
                    last = dve.max_index(topu[:, t, :], top[:, t, :], lg[:, t, :])
                own(last)
                dve.tensor_tensor(p2, top[:, :, 1], top[:, :, 0], ALU.subtract).then_inc(gap_ready.sem, 1)
                own(dve.tensor_copy(ix, topu[:, :, 0:2]))
                own(dve.tensor_tensor(selc, tiled(k("iota"), TILES), over(ix[:, :, 0], E8), ALU.is_equal))
                own(dve.tensor_tensor(selc2, tiled(k("iota"), TILES), over(ix[:, :, 1], E8), ALU.is_equal))
                dve.wait_ge(gap_exp.sem, gap_exp.at(g, 1))
                own(dve.tensor_scalar(p1, p2, 1.0, None, ALU.add))
                own(dve.reciprocal(p1, p1))
                own(dve.tensor_tensor(ix[:, :, 1], p2, p1, ALU.mult))
                own(dve.tensor_tensor(selc, selc, over(p1, E8), ALU.mult))
                own(dve.tensor_tensor(selc2, selc2, over(ix[:, :, 1], E8), ALU.mult))
                dve.tensor_tensor(cw, selc, selc2, ALU.add).then_inc(cw_ready.sem, 1)
                dve.wait_ge(cw_ready.sem, cw_ready.at(g, 1))
                for t in range(TILES):
                    dve.wait_ge(e_made.sem, e_made.at(g, t + 1))
                    dve.tensor_tensor(hview(st[:, t % 2, :], D), hview((pa, pb)[t % 2][:, :], D), over(cw[:, t, :], D),
                                      ALU.mult).then_inc(e_scaled.sem, 1)
                    dve.wait_ge(e_scaled.sem, e_scaled.at(g, t + 1))
                    own(dve.tensor_reduce(y[:, t, :], st[:, t % 2, :].rearrange("p (e n) -> p n e", e=E8), AX.X,
                                          ALU.add))
                dve.wait_ge(be_made.sem, be_made.at(g, 1))
                own(dve.tensor_tensor(flat(res), pd[:, :], flat(x1), ALU.add))
                own(dve.tensor_tensor(flat(res), flat(res), flat(y), ALU.add))
                norm_stats(res, x6_stat)
                norm_apply(zx, res, x6_rstd, x6_ready)
                own.done()


def pack(table, parts):
    rows = [np.asarray(parts[name]).reshape(P, width) for name, width in table]
    return np.ascontiguousarray(np.concatenate(rows, axis=1))


def constants():
    i, j = np.arange(P)[:, None], np.arange(P)[None, :]
    f = np.float32
    sel = np.zeros((P, 64), f)
    for e in range(2):
        sel[DH * e:DH * e + DH, e] = 1.0
        sel[DH * e:DH * e + DH, 32 + 2 + e] = 1.0
    parts = {
        "ident": (i == j).astype(f), "ones": np.ones((P, P), f), "sel": sel,
        "mask4": ((i % 32) // DX == np.arange(4)[None, :]).astype(f),
        "maskq": (i // 32 == np.arange(4)[None, :]).astype(f),
        "mask2": ((i < S) == ((j // DX) % 2 == 0)).astype(f),
        "half": np.concatenate([(i < S), (i >= S)], axis=1).astype(f),
        "eps0": np.full((P, 1), 1.1920929e-07, f), "eps5": np.full((P, 1), 1e-5, f), "eps3": np.full((P, 1), 1e-3, f),
        "iota": np.broadcast_to(np.arange(E8, dtype=f), (P, E8)), "zero": np.zeros((P, 1), f),
    }
    low = -60000.0
    m0 = np.where(np.arange(S)[None, :] >= i % S, 0.0, low)
    m1 = np.where((i // S == j // S) & (j <= i), 0.0, low)
    wide = np.concatenate([np.eye(P), np.tile(m0, (1, 8)), np.tile(m1, (1, 4))], axis=1)
    return pack(CONSTS, parts), wide.astype(np.float16)


def kernel(**a):
    from concourse import bacc
    from concourse.bass_utils import run_bass_kernel_spmd

    a = {name: np.asarray(value) for name, value in a.items()}
    ctx = a["ctx_1024"].reshape(B * S, D)
    wqkv = a["L0_attn_W_qkv"].reshape(NH, DH, 3, D)
    bqkv = a["L0_attn_b_qkv"].reshape(NH, DH, 3)

    def by_pair(m):
        return m.reshape(NP, P, D).transpose(1, 0, 2)

    def rows(r):
        return np.broadcast_to(r.reshape(1, -1), (P, r.size))

    def twice(r):
        return np.concatenate([r, r])

    wkv = a["L1_xattn_Wkv"]
    weights = pack(WEIGHTS, {
        "q0": wqkv[:, :, 0].reshape(INNER, D).T, "k0": wqkv[:, :, 1].reshape(INNER, D).T,
        "v0": wqkv[:, :, 2].reshape(INNER, D).T, "o0": by_pair(a["L0_attn_W_o"].T),
        "xq": a["L0_xattn_Wq"], "xk": a["L0_xattn_Wk"], "xv": a["L0_xattn_Wv"], "xo": a["L0_xattn_Wo"],
        "ffn": a["L0_ffn_weight"], "basis": a["L1_attn_W_basis"].T, "v1": a["L1_attn_W_v"].T,
        "o1": a["L1_attn_W_o"].T, "yq": a["L1_xattn_Wq"], "yk": wkv[:, :INNER], "yv": wkv[:, INNER:],
        "yo": by_pair(a["L1_xattn_Wout"]), "gate": a["L1_ffn_Wg"].T,
        "exp": a["L1_ffn_We"].transpose(2, 0, 1),
        "bq0": bqkv[:, :, 0].reshape(NP, P).T, "bk0": bqkv[:, :, 1].reshape(NP, P).T,
        "bxq": a["L0_xattn_bq"], "bxk": a["L0_xattn_bk"], "bv1": a["L1_attn_b_v"],
        "gx": a["L1_xattn_ln_x_g"], "bx": a["L1_xattn_ln_x_b"], "gl": a["L1_xattn_ln_l_g"],
        "bl": a["L1_xattn_ln_l_b"], "qg": twice(a["L1_xattn_qn_g"]), "kg": twice(a["L1_xattn_kn_g"]),
        "rv0": rows(bqkv[:, :, 2]), "ro0": rows(a["L0_attn_b_o"]), "rxv": rows(a["L0_xattn_bv"]),
        "rxo": rows(a["L0_xattn_bo"]), "rfg": rows(a["L0_ffn_ln_gamma"]), "rfb": rows(a["L0_ffn_ln_beta"]),
        "ro1": rows(a["L1_attn_b_o"]), "ryo": rows(a["L1_xattn_bout"]),
    })
    consts, consts16 = constants()
    arrays = {
        "x": np.ascontiguousarray(a["x"].reshape(B * S, D)),
        "ctx_t": np.ascontiguousarray(ctx.T),
        "ctx": np.ascontiguousarray(ctx),
        "mask_t": np.ascontiguousarray(a["mask_BxS2_bf1"].T).view(np.uint8),
        "weights": weights,
        "be": np.ascontiguousarray(a["L1_ffn_be"]),
        "consts": consts,
        "consts16": consts16,
    }
    nc = bacc.Bacc("TRN2", target_bir_lowering=False, num_devices=1)
    args = [nc.dram_tensor(name, v.shape, mybir.dt.from_np(v.dtype), kind="ExternalInput").ap()
            for name, v in arrays.items()]
    args.append(nc.dram_tensor("out", (B * S, D), F32, kind="ExternalOutput").ap())
    decoder(nc, *args)
    r = run_bass_kernel_spmd(nc, [arrays], core_ids=[0])
    return r.results[0]["out"].reshape(B, S, D)
```

```python
from contextlib import ExitStack

import numpy as np

import concourse.bass as bass
from concourse import mybir

F32, F16, U32, U8 = mybir.dt.float32, mybir.dt.float16, mybir.dt.uint32, mybir.dt.uint8
ALU = mybir.AluOpType
ACT = mybir.ActivationFunctionType
AX = mybir.AxisListType

P = 128
B, S, D = 128, 64, 128
NH, DH = 16, 64
NP = NH // 2
INNER = NH * DH
TILES = 4
G = B * S // (TILES * P)
GT = TILES * P
SEQ = GT // S
NX = 16
DX = D // NX
R = 64
E8 = 8
QB = 128.0

WEIGHTS_A = [
    ("q0", INNER), ("k0", INNER), ("v0", INNER), ("o0", INNER),
    ("xq", D), ("xk", D), ("xv", D), ("xo", D), ("bq0", NP), ("bk0", NP), ("bxq", 1), ("bxk", 1),
    ("rv0", INNER), ("ro0", D), ("rxv", D), ("rxo", D),
]
WEIGHTS_B = [
    ("basis", R), ("v1", D), ("o1", D),
    ("yq", INNER), ("yk", INNER), ("yv", INNER), ("yo", INNER),
    ("gate", E8), ("exp", E8 * D), ("bv1", 1), ("gx", 1), ("bx", 1), ("gl", 1), ("bl", 1),
    ("qg", 1), ("kg", 1), ("ro1", D), ("ryo", D),
]
WEIGHTS_AB = [("ffn", D), ("rfg", D), ("rfb", D)]
CONSTS = [
    ("ident", P), ("ones", P), ("sel", 64), ("mask4", 4), ("maskq", 4), ("mask2", P), ("half", 2),
    ("eps0", 1), ("eps5", 1), ("eps3", 1), ("iota", E8), ("zero", 1),
]


def columns(table):
    at, out = 0, {}
    for name, width in table:
        out[name] = slice(at, at + width)
        at += width
    return out, at


ACOL, AN = columns(WEIGHTS_A)
BCOL, BN = columns(WEIGHTS_B)
ABCOL, ABN = columns(WEIGHTS_AB)
CCOL, CN = columns(CONSTS)


class Signal:

    def __init__(self, sem, per, lead=0):
        self.sem, self.per, self.lead = sem, per, lead

    def at(self, g, n):
        return g * self.per + (n + self.lead)


class Chain:

    def __init__(self, eng, sem):
        self.eng, self.sem, self.n = eng, sem, 0

    def __call__(self, ins):
        self.n += 1
        ins.then_inc(self.sem, 1)
        self.eng.wait_ge(self.sem, self.n)

    def done(self):
        self.eng.sem_clear(self.sem)
        self.n = 0


def decoder(nc, x, ctx_t, ctx, mask_t, weights_a, weights_b, weights_ab, be, consts, consts16, out):
    x_v = x.rearrange("(g t p) c -> g p t c", t=TILES, p=P)
    ctx_v = ctx.rearrange("(g t p) c -> g p t c", t=TILES, p=P)
    ctxt_v = ctx_t.rearrange("c (g n) -> g c n", n=GT)
    out_v = out.rearrange("(g t p) c -> g p t c", t=TILES, p=P)

    with ExitStack() as stack:
        def sb(name, shape, dt=F32):
            return stack.enter_context(nc.sbuf_tensor(name, shape, dt))

        def ps(name, shape):
            return stack.enter_context(nc.psum_tensor(name, shape, F32))

        def sig(name, per=1, lead=0):
            return Signal(stack.enter_context(nc.semaphore(name)), per, lead)

        pa = ps("pa", [P, 1024])
        pb = ps("pb", [P, 1024])
        pc = ps("pc", [P, 1024])
        pd = ps("pd", [P, 512])
        pe_ = ps("pe", [P, 512])

        wts = sb("wts", [P, max(AN, BN)])
        wts_ab = sb("wts_ab", [P, ABN])
        cst = sb("cst", [P, CN])
        cst16 = sb("cst16", [P, P + 1024], F16)
        be_sb = sb("be_sb", [E8, D])
        ident16, causal_t, causal_1 = cst16[:, 0:P], cst16[:, P:P + 512], cst16[:, P + 512:P + 1024]

        def w(name, a=0, b=None):
            c, buffer = ((ACOL, wts) if name in ACOL else (BCOL, wts) if name in BCOL else (ABCOL, wts_ab))
            c = c[name]
            return buffer[:, c.start + a:c.start + b if b is not None else c.stop]

        def k(name, a=0, b=None):
            c = CCOL[name]
            return cst[:, c.start + a:c.start + b if b is not None else c.stop]

        ident = k("ident")
        state = sb("state", [P, G * GT])
        fstat = sb("fstat", [P, G * 2 * TILES])
        qblk = sb("qblk", [P, NP, 2, GT])
        kt = sb("kt", [P, NP, GT])
        v = sb("v", [P, 2, INNER])
        st = sb("st", [P, 2, 1024])
        zt = sb("zt", [P, NP, GT])
        pblk = sb("pblk", [P, NH, 2, S])
        x_in = sb("x_in", [P, TILES, D])
        c_in = sb("c_in", [P, TILES, D])
        nrm = sb("nrm", [P, TILES, D])
        tT = sb("tT", [P, GT])
        res = sb("res", [P, TILES, D])
        x1 = sb("x1", [P, TILES, D])
        xb = sb("xb", [P, TILES, D])
        zx = sb("zx", [P, TILES, D])
        y = sb("y", [P, TILES, D])
        x2 = sb("x2", [P, TILES, D])
        kq = sb("kq", [P, 8 * GT])
        stx = sb("stx", [P, 1024])
        tx = sb("tx", [P, GT])
        resx = sb("resx", [P, TILES, D])
        xbx = sb("xbx", [P, TILES, D])
        vblk = sb("vblk", [P, SEQ, NP, 18])
        small = sb("small", [P, 704])
        used = [0]

        def tiny(*shape):
            n = int(np.prod(shape))
            a = small[:, used[0]:used[0] + n]
            used[0] += n
            names = "abc"[:len(shape)]
            if len(shape) > 1:
                a = a.rearrange(f"p ({' '.join(names)}) -> p {' '.join(names)}", **dict(zip(names[1:], shape[1:])))
            return a

        ssq, lnv, rms = tiny(TILES), tiny(TILES), tiny(TILES)
        mx, sm, rs = tiny(2, NH), tiny(2, NH), tiny(2, NH)
        stats, mv = tiny(TILES, 6), tiny(TILES, 2)
        statsx, mvx = tiny(TILES, 6), tiny(TILES, 2)
        lnx, rstdx = tiny(TILES), tiny(TILES)
        mxx, smx = tiny(NH), tiny(TILES)
        rstd, rstdf = tiny(TILES), tiny(TILES)
        fstl = tiny(8)
        rq = tiny(NH)
        mbl = tiny(SEQ)
        peaks, peak = tiny(2), tiny(2)
        bxqm = tiny(4)
        mqs = tiny(4)
        rz = tiny(NP, 2)
        rk = tiny(4, NH)
        rkl = tiny(4, NH)
        gqk = tiny(1)
        ffs = tiny(8)
        lg = tiny(TILES, E8)
        top = tiny(TILES, E8)
        topi = tiny(TILES, E8)
        selc = tiny(TILES, E8)
        selc2 = tiny(TILES, E8)
        cw = tiny(TILES, E8)
        p1, p2 = tiny(TILES), tiny(TILES)
        ix = tiny(TILES, 2)
        maskb = sb("maskb", [P, B])
        mask8 = sb("mask8", [S, B], U8)
        topu = sb("topu", [P, TILES, E8], U32)
        wq = sb("wq", [P, D])
        fold = sb("fold", [P, 2 * D])

        qg = kq[:, 0:4 * GT].rearrange("p (j n) -> p j n", n=GT)
        kj = kq[:, 4 * GT:8 * GT].rearrange("p (j n) -> p j n", n=GT)
        latt, cwt, tl = kq[0:R, 0:GT], kq[0:E8, GT:2 * GT], kq[:, 2 * GT:3 * GT]
        x4 = kq[:, 3 * GT:4 * GT].rearrange("p (t c) -> p t c", c=D)
        ztf = zt[:, :, :].rearrange("p a n -> p (a n)")
        zta = [ztf[:, 1024 * i:1024 * i + 1024].rearrange("p (a n) -> p a n", n=P) for i in range(2)]
        pt = [ztf[:, 2048 + 1024 * i:3072 + 1024 * i].rearrange("p (a n) -> p a n", n=P) for i in range(2)]
        pflat = pblk[:, :, :, :].rearrange("p h a n -> p (h a n)")
        sqt, qs = pflat[:, 0:1024], pflat[:, 1024:2048]
        kvt = vblk[:, :, :, :].rearrange("p b i n -> p (b i n)")[:, 0:SEQ * P].rearrange("p (b n) -> p b n", n=P)
        vdata = vblk[:, :, :, 0:16]
        vbias = fold[:, 0:D]
        sqk = [pflat[:, 512 * i:512 * i + 512] for i in range(2)]

        def flat(a):
            return a[:, :, :].rearrange("p t c -> p (t c)")

        def hview(a, n=S):
            return a.rearrange("p (h n) -> p h n", n=n)

        def over(a, n):
            return a.unsqueeze(2).broadcast_to([a.shape[0], a.shape[1], n])

        def tiled(a, n):
            return a.unsqueeze(1).broadcast_to([a.shape[0], n, a.shape[1]])

        loaded = sig("loaded")
        setup = sig("setup")
        x_loaded, c_loaded = sig("x_loaded", 16), sig("c_loaded", 16)
        xb_ready, rms_ready, n_ready, n_turned, nt_ready = (
            sig("xb_ready", 1, 1), sig("rms_ready", 1), sig("n_ready", 1, 1), sig("n_turned", 1, 1), sig("nt_ready", 1))
        q_made, k_made, q_kept, k_kept = sig("q_made", NP), sig("k_made", NP), sig("q_kept", NP), sig("k_kept", NP)
        v_made, v_kept = sig("v_made", TILES), sig("v_kept", TILES)
        s_made, s_shifted, s_exp, s_norm = (
            sig("s_made", TILES), sig("s_shifted", TILES), sig("s_exp", TILES), sig("s_norm", TILES))
        p_ready, v_scaled = sig("p_ready", TILES), sig("v_scaled", TILES)
        z_made, z_kept, o_made = sig("z_made", TILES), sig("z_kept", TILES), sig("o_made", 1)
        stat1, rstd1, x1_ready, x1_turned, x1t_ready = (
            sig("stat1", 1, 1), sig("rstd1"), sig("x1_ready"), sig("x1_turned"), sig("x1t_ready"))
        kx_made, vx_made, vx_masked, vx_ready, qx_made, kx_kept, qx_kept = (
            sig("kx_made"), sig("vx_made", 1, 1), sig("vx_masked"), sig("vx_ready"), sig("qx_made"), sig("kx_kept"), sig("qx_kept"))
        sx_made, sx_shifted, sx_exp, px_turned = (
            sig("sx_made", TILES), sig("sx_shifted", TILES), sig("sx_exp", TILES), sig("px_turned", TILES))
        px_a, px_v = sig("px_a", TILES), sig("px_v", TILES)
        zx_made, zx_ready, zx_turned, zxt_ready, ox_made = (
            sig("zx_made", TILES), sig("zx_ready", TILES), sig("zx_turned"), sig("zxt_ready"), sig("ox_made"))
        x1b_ready, r2_ready, rstd2, x2_ready, stat3, rstd3, peak_done = (
            sig("x1b_ready"), sig("r2_ready", 1, 1), sig("rstd2"), sig("x2_ready"), sig("stat3"), sig("rstd3"), sig("peak_done", 1, 1))

        peak_local, weight_sum, peak_all, between = sig("peak_local"), sig("weight_sum"), sig("peak_all"), sig("between")
        cb_loaded, xn_ready, xn_turned, xq_ready, f_made = (
            sig("cb_loaded", 16), sig("xn_ready"), sig("xn_turned"), sig("xq_ready"), sig("f_made"))
        cn_stat, cn_rstd, cn_ready, cn_turned, cn_kept = (
            sig("cn_stat"), sig("cn_rstd"), sig("cn_ready", 1, 1), sig("cn_turned"), sig("cn_kept"))
        x3_stat, x3_rstd, x3_ready, x3_turned, x3t_ready, x3b_ready = (
            sig("x3_stat"), sig("x3_rstd"), sig("x3_ready"), sig("x3_turned"), sig("x3t_ready"), sig("x3b_ready"))
        lat_made, lat_kept, v1_made, v1_kept = sig("lat_made"), sig("lat_kept"), sig("v1_made"), sig("v1_kept")
        s1_made, s1_shifted, s1_exp, p1_ready, p1_turned, p1t_ready, z1_made, z1_kept, o1_made = (
            sig("s1_made"), sig("s1_shifted"), sig("s1_exp"), sig("p1_ready"), sig("p1_turned"), sig("p1t_ready"),
            sig("z1_made", 1, 1), sig("z1_kept"), sig("o1_made"))
        x4_stat, x4_rstd, x4_ready, x4b_ready, ln_stat, ln_rstd, ln_ready, ln_turned, ln_kept = (
            sig("x4_stat"), sig("x4_rstd"), sig("x4_ready"), sig("x4b_ready"), sig("ln_stat"), sig("ln_rstd"),
            sig("ln_ready"), sig("ln_turned", 1, 1), sig("ln_kept"))
        yq_made, yq_squared, yq_sum, yq_root, yq_scaled, yq_turned, yq_a, yq_v = (
            sig("yq_made", TILES), sig("yq_squared", TILES), sig("yq_sum", TILES), sig("yq_root", TILES),
            sig("yq_scaled", TILES), sig("yq_turned", TILES), sig("yq_a", TILES), sig("yq_v", TILES))
        yk_made, yk_kept, yk_squared, yk_summed = (
            sig("yk_made", 2 * NP), sig("yk_kept", 2 * NP), sig("yk_squared", 2 * NP), sig("yk_summed", 2 * NP))
        yk_sum_kept, yk_sum_turned, yk_mean, yk_root = (
            sig("yk_sum_kept", 2), sig("yk_sum_turned", 2), sig("yk_mean", 2), sig("yk_root", 2))
        yv_made, yv_kept, ys_made, ys_scaled, yp_ready, yl_made, yl_inv, yz_made, yz_kept, yo_made = (
            sig("yv_made", SEQ), sig("yv_kept", SEQ), sig("ys_made", SEQ), sig("ys_scaled", SEQ), sig("yp_ready", SEQ, 1),
            sig("yl_made", SEQ), sig("yl_inv", SEQ), sig("yz_made", SEQ), sig("yz_kept", SEQ), sig("yo_made"))
        x5_stat, x5_rstd, x5_ready, x5_turned, x5t_ready = (
            sig("x5_stat"), sig("x5_rstd"), sig("x5_ready"), sig("x5_turned"), sig("x5t_ready"))
        gate_made, gap_ready, gap_exp, cw_ready, cw_turned, cwt_ready, be_made = (
            sig("gate_made"), sig("gap_ready"), sig("gap_exp"), sig("cw_ready"), sig("cw_turned"), sig("cwt_ready"),
            sig("be_made"))
        e_made, e_scaled = sig("e_made", TILES), sig("e_scaled", TILES)
        x6_stat, x6_rstd, x6_ready, stored = sig("x6_stat"), sig("x6_rstd"), sig("x6_ready"), sig("stored", 16, 16)
        x2_copied = sig("x2_copied")
        lat_placed, peak_kept = sig("lat_placed"), sig("peak_kept")
        act_own, dve_own, pool_own, pool_hold = [stack.enter_context(nc.semaphore(n))
                                                 for n in ("act_own", "dve_own", "pool_own", "pool_hold")]
        gap_a, gap_v, gap_s = sig("gap_a"), sig("gap_v"), sig("gap_s")
        LOADED_A, LOADED_B = 6 * 16, 7 * 16
        block = stack.enter_context(nc.Block())

        @block.sync
        def _(sp):
            for ahead in (xb_ready, n_ready, n_turned, stat1, vx_made, r2_ready, peak_done, cn_ready, stored, z1_made,
                          yp_ready, ln_turned):
                sp.sem_inc(ahead.sem, ahead.lead)
            for dst, src in ((wts[:, 0:AN], weights_a), (wts_ab[:, :], weights_ab), (cst[:, :], consts),
                             (cst16[:, :], consts16), (be_sb[:, :], be), (mask8[:, :], mask_t)):
                sp.dma_start(dst, src).then_inc(loaded.sem, 16)
            def load(a, x):
                if a is not None:
                    sp.wait_ge(xb_ready.sem, xb_ready.at(a, 0))
                    sp.wait_ge(n_ready.sem, n_ready.at(a, 0))
                    sp.dma_start(x_in[:, :, :], x_v[a]).then_inc(x_loaded.sem, 16)
                if x is not None:
                    sp.wait_ge(vx_made.sem, vx_made.at(x, 0))
                    sp.dma_start(flat(c_in), ctxt_v[x]).then_inc(c_loaded.sem, 16)

            load(0, 0)
            with sp.Fori(1, G) as g:
                load(g, g)
            sp.wait_ge(peak_done.sem, G + peak_done.lead)
            sp.dma_start(wts[:, 0:BN], weights_b).then_inc(loaded.sem, 16)
            with sp.Fori(0, G) as g:
                sp.wait_ge(cn_ready.sem, cn_ready.at(g, 0))
                sp.dma_start(c_in[:, :, :], ctx_v[g]).then_inc(cb_loaded.sem, 16)
                sp.wait_ge(x6_ready.sem, x6_ready.at(g, 1))
                sp.dma_start(out_v[g], zx[:, :, :]).then_inc(stored.sem, 16)
            sp.wait_ge(stored.sem, 16 * G + stored.lead)

        @block.tensor
        def _(pe):
            pe.wait_ge(loaded.sem, LOADED_A)
            pe.wait_ge(setup.sem, 2)

            def turn(dst, src, signal):
                for t in range(TILES):
                    last = pe.transpose(dst[:, t * P:(t + 1) * P], src[:, t, :], ident)
                last.then_inc(signal.sem, 1)

            def pass_a(a, x):
                def context():
                    pe.wait_ge(c_loaded.sem, c_loaded.at(x, 16))
                    ctxt = flat(c_in)
                    pe.matmul(pc[:, 512:1024], w("xk"), ctxt, start=True, stop=True).then_inc(kx_made.sem, 1)
                    for b in range(SEQ):
                        for e in range(2):
                            last = pe.matmul(pb[S * e:S * e + S, P * b:P * b + P], ctxt[:, S * b:S * b + S], w("xv"),
                                             start=True, stop=True)
                    last.then_inc(vx_made.sem, 1)

                def turn_x1():
                    pe.wait_ge(x1_ready.sem, x1_ready.at(x, 1))
                    pe.wait_ge(r2_ready.sem, r2_ready.at(x, 0))
                    turn(pe_, x1, x1_turned)

                def turn_n():
                    pe.wait_ge(n_ready.sem, n_ready.at(a, 1))
                    turn(pd, nrm, n_turned)

                def queries_x():
                    pe.wait_ge(x1t_ready.sem, x1t_ready.at(x, 1))
                    pe.matmul(pe_[:, :], w("xq"), tx[:, :], start=True, stop=True).then_inc(qx_made.sem, 1)

                def queries_keys(p):
                    if p == 0:
                        pe.wait_ge(nt_ready.sem, nt_ready.at(a, 1))
                    if p >= 2:
                        pe.wait_ge(q_kept.sem, q_kept.at(a, p - 1))
                    pe.matmul(pa[:, 512 * (p % 2):512 * (p % 2) + 512], w("q0", P * p, P * p + P), tT[:, :],
                              start=True, stop=True).then_inc(q_made.sem, 1)
                    if p == 1 and x is not None:
                        pe.wait_ge(kx_kept.sem, kx_kept.at(x, 1))
                    if p >= 2:
                        pe.wait_ge(k_kept.sem, k_kept.at(a, p - 1))
                    pe.matmul(pc[:, 512 * (p % 2):512 * (p % 2) + 512], w("k0", P * p, P * p + P), tT[:, :],
                              start=True, stop=True).then_inc(k_made.sem, 1)

                def values(t):
                    if t == 0:
                        pe.wait_ge(q_kept.sem, q_kept.at(a, NP))
                    else:
                        pe.wait_ge(v_kept.sem, v_kept.at(a, t))
                    if t >= 2:
                        pe.wait_ge(z_kept.sem, z_kept.at(a, t - 1))
                    for c in range(2):
                        last = pe.matmul(pa[:, 512 * c:512 * c + 512], tT[:, t * P:(t + 1) * P],
                                         w("v0", 512 * c, 512 * c + 512), start=True, stop=True)
                    last.then_inc(v_made.sem, 1)

                def scores(t):
                    if t == 0:
                        pe.wait_ge(k_kept.sem, k_kept.at(a, NP))
                    else:
                        pe.wait_ge(s_shifted.sem, s_shifted.at(a, t))
                    for c in range(2):
                        pe.matmul(pc[:, 512 * c:512 * c + 512], ident16, causal_t, start=True, stop=False,
                                  skip_group_check=True)
                    for p in range(NP):
                        for b in range(2):
                            at = t * P + b * S
                            last = pe.matmul(pc[S * b:S * b + S, P * p:P * p + P], kt[:, p, at:at + S],
                                             qblk[:, p, :, at:at + S], start=False, stop=(p % 4 == 3),
                                             skip_group_check=True)
                    last.then_inc(s_made.sem, 1)

                def attend(t):
                    pe.wait_ge(p_ready.sem, p_ready.at(a, t + 1))
                    pe.wait_ge(v_scaled.sem, v_scaled.at(a, t + 1))
                    pe.wait_ge(v_kept.sem, v_kept.at(a, min(t + 2, TILES)))
                    if t >= 1:
                        pe.wait_ge(z_kept.sem, z_kept.at(a, t))
                    for h in range(NH):
                        last = pe.matmul(pa[S * (h % 2):S * (h % 2) + S, P * (h // 2):P * (h // 2) + P],
                                         v[:, t % 2, DH * h:DH * h + DH],
                                         pblk[:, h, :, :], start=True, stop=True)
                    last.then_inc(z_made.sem, 1)

                def project(t):
                    pe.wait_ge(z_kept.sem, z_kept.at(a, t + 1))
                    for p in range(NP):
                        last = pe.matmul(pd[:, t * P:t * P + P], zta[t % 2][:, p, :], w("o0", P * p, P * p + P),
                                         start=(p == 0), stop=(p == NP - 1))
                    if t == TILES - 1:
                        last.then_inc(o_made.sem, 1)

                def scores_x(t):
                    if t == 0:
                        pe.wait_ge(qx_kept.sem, qx_kept.at(x, 1))
                        pe.wait_ge(kx_kept.sem, kx_kept.at(x, 1))
                        pe.wait_ge(vx_masked.sem, vx_masked.at(x, 1))
                    else:
                        pe.wait_ge(px_a.sem, px_a.at(x, t))
                        pe.wait_ge(px_v.sem, px_v.at(x, t))
                    for q in range(4):
                        for b in range(2):
                            at = t * P + b * S
                            last = pe.matmul(pb[S * b:S * b + S, 256 * q:256 * q + 256], qg[:, q, at:at + S],
                                             kj[:, :, at:at + S], start=True, stop=True)
                    last.then_inc(sx_made.sem, 1)

                def turn_x(t):
                    pe.wait_ge(sx_exp.sem, sx_exp.at(x, t + 1))
                    for i in range(NP):
                        last = pe.transpose(pb[:, P * i:P * i + P], stx[:, P * i:P * i + P], ident)
                    last.then_inc(px_turned.sem, 1)

                def attend_x(t):
                    if t == 0:
                        pe.wait_ge(vx_ready.sem, vx_ready.at(x, 1))
                    else:
                        pe.wait_ge(zx_ready.sem, zx_ready.at(x, t))
                    pe.wait_ge(px_a.sem, px_a.at(x, t + 1))
                    pe.wait_ge(px_v.sem, px_v.at(x, t + 1))
                    for i in range(NP):
                        last = pe.matmul(pe_[:, 36 * i:36 * i + 36], pt[t % 2][:, i, :],
                                         vblk[:, 2 * t:2 * t + 2, i, :], start=True, stop=True)
                    last.then_inc(zx_made.sem, 1)

                def turn_zx():
                    pe.wait_ge(zx_ready.sem, zx_ready.at(x, TILES))
                    turn(pe_, zx, zx_turned)

                def project_x():
                    pe.wait_ge(zxt_ready.sem, zxt_ready.at(x, 1))
                    for t in range(TILES):
                        last = pe.matmul(pe_[:, t * P:(t + 1) * P], tx[:, t * P:(t + 1) * P], w("xo"),
                                         start=True, stop=True)
                    last.then_inc(ox_made.sem, 1)

                if x is not None:
                    context()
                    turn_x1()
                if a is not None:
                    turn_n()
                if x is not None:
                    queries_x()
                if a is not None:
                    for p in range(5):
                        queries_keys(p)
                if x is not None:
                    scores_x(0)
                if a is not None:
                    for p in range(5, NP):
                        queries_keys(p)
                if x is not None:
                    turn_x(0)
                for t in range(TILES + 2):
                    if a is not None and t < TILES:
                        values(t)
                        scores(t)
                    if x is not None and t < TILES:
                        attend_x(t)
                        if t + 1 < TILES:
                            scores_x(t + 1)
                    if x is not None and t == TILES:
                        turn_zx()
                    if a is not None and 1 <= t <= TILES:
                        attend(t - 1)
                    if x is not None and t + 1 < TILES:
                        turn_x(t + 1)
                    if x is not None and t == TILES:
                        project_x()
                    if a is not None and t >= 2:
                        project(t - 2)

            pass_a(0, None)
            with pe.Fori(1, G) as g:
                pass_a(g, g - 1)
            pass_a(None, G - 1)
            pe.wait_ge(loaded.sem, LOADED_B)
            with pe.Fori(0, G) as g:
                pe.wait_ge(cn_ready.sem, cn_ready.at(g, 1))
                turn(pd, y, cn_turned)
                pe.wait_ge(xn_ready.sem, xn_ready.at(g, 1))
                turn(pe_, nrm, xn_turned)
                pe.wait_ge(xq_ready.sem, xq_ready.at(g, 1))
                pe.wait_ge(between.sem, 1)
                for t in range(TILES):
                    last = pe.matmul(pa[:, t * P:(t + 1) * P], tT[:, t * P:(t + 1) * P], wq[:, :],
                                     start=True, stop=True)
                last.then_inc(f_made.sem, 1)
                pe.wait_ge(x3_ready.sem, x3_ready.at(g, 1))
                turn(pe_, x1, x3_turned)
                pe.wait_ge(x3t_ready.sem, x3t_ready.at(g, 1))
                pe.matmul(pb[0:R, 0:512], w("basis"), tT[:, :], start=True, stop=True).then_inc(lat_made.sem, 1)
                for t in range(TILES):
                    last = pe.matmul(pa[:, 512 + t * P:512 + (t + 1) * P], tT[:, t * P:(t + 1) * P], w("v1"),
                                     start=True, stop=True)
                last.then_inc(v1_made.sem, 1)
                pe.matmul(pc[:, 0:512], ident16, causal_1, start=True, stop=False, skip_group_check=True)
                pe.wait_ge(lat_kept.sem, lat_kept.at(g, 1))
                for t in range(TILES):
                    a = slice(t * P, (t + 1) * P)
                    last = pe.matmul(pc[:, a], latt[:, a], latt[:, a], start=False, stop=(t == TILES - 1),
                                     skip_group_check=True)
                last.then_inc(s1_made.sem, 1)
                pe.wait_ge(p1_ready.sem, p1_ready.at(g, 1))
                for t in range(TILES):
                    last = pe.transpose(pe_[:, t * P:(t + 1) * P], st[:, 0, t * P:(t + 1) * P], ident)
                last.then_inc(p1_turned.sem, 1)
                pe.wait_ge(p1t_ready.sem, p1t_ready.at(g, 1))
                pe.wait_ge(v1_kept.sem, v1_kept.at(g, 1))
                for t in range(TILES):
                    last = pe.matmul(pb[:, 512 + t * P:512 + (t + 1) * P], x2[:, t, :], st[:, 1, t * P:(t + 1) * P],
                                     start=True, stop=True)
                last.then_inc(z1_made.sem, 1)
                pe.wait_ge(z1_kept.sem, z1_kept.at(g, 1))
                for t in range(TILES):
                    last = pe.matmul(pa[:, t * P:(t + 1) * P], st[:, 1, 512 + t * P:512 + (t + 1) * P], w("o1"),
                                     start=True, stop=True)
                last.then_inc(o1_made.sem, 1)

                pe.wait_ge(ln_ready.sem, ln_ready.at(g, 1))
                turn(pe_, nrm, ln_turned)
                pe.wait_ge(ln_kept.sem, ln_kept.at(g, 1))

                def queries(t):
                    dst = (pa, pc)[t % 2]
                    if t >= 2:
                        pe.wait_ge(yq_scaled.sem, yq_scaled.at(g, t - 1))
                    for c in range(2):
                        last = pe.matmul(dst[:, 512 * c:512 * c + 512], tT[:, t * P:(t + 1) * P],
                                         w("yq", 512 * c, 512 * c + 512), start=True, stop=True)
                    last.then_inc(yq_made.sem, 1)

                def turn_q(t):
                    pe.wait_ge(yq_scaled.sem, yq_scaled.at(g, t + 1))
                    if t >= 1:
                        pe.wait_ge(yq_a.sem, yq_a.at(g, t))
                        pe.wait_ge(yq_v.sem, yq_v.at(g, t))
                    for p in range(NP):
                        last = pe.transpose(pb[:, P * p:P * p + P], qs[:, P * p:P * p + P], ident)
                    last.then_inc(yq_turned.sem, 1)

                for t in range(TILES + 1):
                    if t < TILES:
                        queries(t)
                    if t >= 1:
                        turn_q(t - 1)

                for c in range(2):
                    if c == 0:
                        pe.wait_ge(yq_a.sem, yq_a.at(g, TILES))
                        pe.wait_ge(yq_v.sem, yq_v.at(g, TILES))
                        pe.wait_ge(lat_placed.sem, lat_placed.at(g, 1))
                        pe.wait_ge(cn_kept.sem, cn_kept.at(g, 1))
                    else:
                        pe.wait_ge(yz_kept.sem, yz_kept.at(g, 4))
                    for p in range(NP + 2):
                        if p < NP:
                            if p >= 2:
                                pe.wait_ge(yk_kept.sem, yk_kept.at(g, NP * c + p - 1))
                            pe.matmul(pb[:, 512 * (p % 2):512 * (p % 2) + 512], w("yk", P * p, P * p + P),
                                      kvt[:, 4 * c:4 * c + 4, :], start=True, stop=True).then_inc(yk_made.sem, 1)
                        if p >= 2:
                            u = p - 2
                            pe.wait_ge(yk_squared.sem, yk_squared.at(g, NP * c + u + 1))
                            row = 32 * (u // 2)
                            pe.matmul(pd[row:row + 32, :], k("sel", 32 * (u % 2), 32 * (u % 2) + 32), sqk[u % 2],
                                      start=(u % 2 == 0), stop=(u % 2 == 1),
                                      skip_group_check=True).then_inc(yk_summed.sem, 1)
                    pe.wait_ge(yk_sum_kept.sem, yk_sum_kept.at(g, c + 1))
                    for i in range(4):
                        last = pe.transpose(pd[:, P * i:P * i + P], st[:, 0, P * i:P * i + P], ident)
                    last.then_inc(yk_sum_turned.sem, 1)
                    pe.wait_ge(yk_kept.sem, yk_kept.at(g, NP * c + NP))

                    def values_y(b):
                        if b >= 1:
                            pe.wait_ge(yv_kept.sem, yv_kept.at(g, b))
                        for h in range(2):
                            last = pe.matmul(pa[:, 512 * h:512 * h + 512], kvt[:, b, :],
                                             w("yv", 512 * h, 512 * h + 512), start=True, stop=True)
                        last.then_inc(yv_made.sem, 1)

                    def scores_y(b):
                        if b >= 1:
                            pe.wait_ge(ys_scaled.sem, ys_scaled.at(g, b))
                        at = P * (b % 4)
                        for p in range(NP):
                            last = pe.matmul(pc[:, P * p:P * p + P], kt[:, p, at:at + P],
                                             qblk[:, p, :, S * b:S * b + S], start=True, stop=True)
                        last.then_inc(ys_made.sem, 1)

                    def attend_y(b):
                        pe.wait_ge(yp_ready.sem, yp_ready.at(g, b + 1))
                        pr = hview(st[:, b % 2, :])
                        if b % 4 == 0:
                            pe.wait_ge(yk_mean.sem, yk_mean.at(g, b // 4 + 1))
                        if b >= 1:
                            pe.wait_ge(yl_inv.sem, yl_inv.at(g, b))
                        for e in range(2):
                            last = pe.matmul(pd[S * e:S * e + S, :], k("ones", 0, S), pr[:, e:NH:2, :],
                                             start=True, stop=True)
                        last.then_inc(yl_made.sem, 1)
                        pe.wait_ge(yv_kept.sem, yv_kept.at(g, b + 1))
                        if b >= 1:
                            pe.wait_ge(yz_kept.sem, yz_kept.at(g, b))
                        for p in range(NP):
                            last = pe.matmul(pb[:, P * p:P * p + P], v[:, b % 2, P * p:P * p + P],
                                             st[:, b % 2, P * p:P * p + P], start=True, stop=True)
                        last.then_inc(yz_made.sem, 1)

                    def project_y(t):
                        pe.wait_ge(yz_kept.sem, yz_kept.at(g, 2 * t + 2))
                        for p in range(NP):
                            last = pe.matmul(pe_[:, t * P:t * P + P], zt[:, p, t * P:t * P + P],
                                             w("yo", P * p, P * p + P), start=(p == 0), stop=(p == NP - 1))
                        if t == TILES - 1:
                            last.then_inc(yo_made.sem, 1)

                    for i in range(6):
                        b = 4 * c + i
                        if i < 4:
                            values_y(b)
                            scores_y(b)
                        if 1 <= i <= 4:
                            attend_y(b - 1)
                        if i in (3, 5):
                            project_y((b - 2) // 2)

                pe.wait_ge(x5_ready.sem, x5_ready.at(g, 1))
                turn(pd, x1, x5_turned)
                pe.wait_ge(x5t_ready.sem, x5t_ready.at(g, 1))
                for t in range(TILES):
                    last = pe.matmul(pc[:, E8 * t:E8 * t + E8], tT[:, t * P:(t + 1) * P], w("gate"),
                                     start=True, stop=True)
                last.then_inc(gate_made.sem, 1)

                def experts(t):
                    dst = (pa, pb)[t % 2]
                    if t >= 2:
                        pe.wait_ge(e_scaled.sem, e_scaled.at(g, t - 1))
                    for c in range(2):
                        last = pe.matmul(dst[:, 512 * c:512 * c + 512], tT[:, t * P:(t + 1) * P],
                                         w("exp", 512 * c, 512 * c + 512), start=True, stop=True)
                    last.then_inc(e_made.sem, 1)

                experts(0)
                experts(1)
                pe.wait_ge(cw_ready.sem, cw_ready.at(g, 1))
                for t in range(TILES):
                    last = pe.transpose(pc[0:E8, 512 + t * P:512 + (t + 1) * P], cw[:, t, :], ident)
                last.then_inc(cw_turned.sem, 1)
                pe.wait_ge(cwt_ready.sem, cwt_ready.at(g, 1))
                for t in range(TILES):
                    last = pe.matmul(pd[:, t * P:(t + 1) * P], cwt[:, t * P:(t + 1) * P], be_sb[:, :],
                                     start=True, stop=True)
                last.then_inc(be_made.sem, 1)
                experts(2)
                experts(3)
                pe.wait_ge(x6_stat.sem, x6_stat.at(g, 1))

        @block.scalar
        def _(act):
            act.preload_act_table_set("natural_log_exp_and_others")
            act.wait_ge(loaded.sem, LOADED_A)
            act.wait_ge(setup.sem, 2)

            def pass_a(a, x):
                own = Chain(act, act_own)

                def rms_root():
                    act.wait_ge(x_loaded.sem, x_loaded.at(a, 16))
                    act.wait_ge(n_turned.sem, n_turned.at(a, 0))
                    for t in range(TILES):
                        last = act.activation(nrm[:, t, :], x_in[:, t, :], ACT.Square, accum_out=ssq[:, t:t + 1])
                    own(last)
                    own(act.activation(lnv, ssq, ACT.Ln, scale=1.0 / D, bias=k("eps0")))
                    act.activation(rms, lnv, ACT.Exp, scale=-0.5).then_inc(rms_ready.sem, 1)

                def keep_q(p):
                    act.wait_ge(q_made.sem, q_made.at(a, p + 1))
                    for e in range(2):
                        r = slice(DH * e, DH * e + DH)
                        last = act.activation(qblk[r, p, e, :], pa[r, 512 * (p % 2):512 * (p % 2) + 512],
                                              ACT.Identity, bias=w("bq0", p, p + 1)[r])
                    last.then_inc(q_kept.sem, 1)

                def exps(t):
                    act.wait_ge(s_shifted.sem, s_shifted.at(a, t + 1))
                    act.activation(st[:, t % 2, :], st[:, t % 2, :], ACT.Exp).then_inc(s_exp.sem, 1)

                def place_p(t):
                    act.wait_ge(s_exp.sem, s_exp.at(a, t + 1))
                    if t >= 1:
                        act.wait_ge(z_made.sem, z_made.at(a, t))
                    for b in range(2):
                        r = slice(S * b, S * b + S)
                        last = act.activation(pblk[r, :, b, :], hview(st[r, t % 2, :]), ACT.Copy)
                    last.then_inc(p_ready.sem, 1)

                def keep_z(t):
                    act.wait_ge(z_made.sem, z_made.at(a, t + 1))
                    act.activation(zta[t % 2].rearrange("p a n -> p (a n)"), pa[:, :],
                                   ACT.Copy).then_inc(z_kept.sem, 1)

                def keep_x1t():
                    act.wait_ge(x1_turned.sem, x1_turned.at(x, 1))
                    act.activation(tx[:, :], pe_[:, :], ACT.Copy).then_inc(x1t_ready.sem, 1)

                def keep_qx():
                    act.wait_ge(qx_made.sem, qx_made.at(x, 1))
                    for j in range(4):
                        last = act.activation(qg[:, j, :], pe_[:, :], ACT.Identity, scale=mqs[:, j:j + 1],
                                              bias=bxqm[:, j:j + 1])
                    last.then_inc(qx_kept.sem, 1)

                def exps_x(t):
                    act.wait_ge(sx_shifted.sem, sx_shifted.at(x, t + 1))
                    act.activation(stx[:, :], stx[:, :], ACT.Exp).then_inc(sx_exp.sem, 1)

                def keep_px(t):
                    act.wait_ge(px_turned.sem, px_turned.at(x, t + 1))
                    act.activation(pt[t % 2][:, 0:4, :].rearrange("p a n -> p (a n)"), pb[:, 0:512],
                                   ACT.Copy).then_inc(px_a.sem, 1)

                def keep_zxt():
                    act.wait_ge(zx_turned.sem, zx_turned.at(x, 1))
                    act.activation(tx[:, :], pe_[:, :], ACT.Copy).then_inc(zxt_ready.sem, 1)

                def root(n, before, eps, log, means, dst, signal):
                    act.wait_ge(before.sem, before.at(n, 1))
                    own(act.activation(log, means[:, :, 1], ACT.Ln, bias=k(eps)))
                    act.activation(dst, log, ACT.Exp, scale=-0.5).then_inc(signal.sem, 1)

                if a is not None:
                    rms_root()
                if x is not None:
                    keep_x1t()
                    keep_qx()
                if a is not None:
                    for p in range(5):
                        keep_q(p)
                if x is not None:
                    exps_x(0)
                if a is not None:
                    for p in range(5, NP):
                        keep_q(p)
                if x is not None:
                    keep_px(0)
                for t in range(TILES + 1):
                    if a is not None and t < TILES:
                        exps(t)
                    if x is not None and t + 1 < TILES:
                        exps_x(t + 1)
                    if x is not None and t == TILES:
                        keep_zxt()
                    if a is not None and t >= 1:
                        keep_z(t - 1)
                    if x is not None and t + 1 < TILES:
                        keep_px(t + 1)
                    if a is not None and t < TILES:
                        place_p(t)
                if a is not None:
                    root(a, stat1, "eps5", lnv, mv, rstd, rstd1)
                if x is not None:
                    root(x, r2_ready, "eps5", lnx, mvx, rstdx, rstd2)
                    root(x, stat3, "eps3", lnx, mvx, rstdf, rstd3)
                own.done()

            pass_a(0, None)
            with act.Fori(1, G) as g:
                pass_a(g, g - 1)
            pass_a(None, G - 1)
            act.wait_ge(loaded.sem, LOADED_B)
            act.activation(fold[:, D:2 * D], w("ffn"), ACT.Abs, accum_out=ffs[:, 0:1]).then_inc(weight_sum.sem, 1)
            with act.Fori(0, G) as g:
                own = Chain(act, act_own)

                def root(before, eps, signal, dst=rstd):
                    act.wait_ge(before.sem, before.at(g, 1))
                    own(act.activation(lnv, mv[:, :, 1], ACT.Ln, bias=k(eps)))
                    act.activation(dst, lnv, ACT.Exp, scale=-0.5).then_inc(signal.sem, 1)

                root(cn_stat, "eps5", cn_rstd)
                act.wait_ge(cn_turned.sem, cn_turned.at(g, 1))
                act.activation(kvt[:, :, 0:S], hview(pd[:, :]), ACT.Identity, scale=w("gx"),
                               bias=w("bx")).then_inc(cn_kept.sem, 1)
                root(x3_stat, "eps5", x3_rstd)
                act.wait_ge(lat_made.sem, lat_made.at(g, 1))
                act.activation(latt[:, :], pb[0:R, 0:512], ACT.Copy).then_inc(lat_kept.sem, 1)
                act.wait_ge(s1_shifted.sem, s1_shifted.at(g, 1))
                act.activation(st[:, 0, 0:512], st[:, 0, 0:512], ACT.Exp, scale=R ** -0.5).then_inc(s1_exp.sem, 1)
                act.wait_ge(p1_turned.sem, p1_turned.at(g, 1))
                act.activation(st[:, 1, 0:512], pe_[:, :], ACT.Copy).then_inc(p1t_ready.sem, 1)
                act.wait_ge(z1_made.sem, z1_made.at(g, 1))
                act.activation(st[:, 1, 512:1024], pb[:, 512:1024], ACT.Identity,
                               bias=w("bv1")).then_inc(z1_kept.sem, 1)
                root(x4_stat, "eps5", x4_rstd)
                root(ln_stat, "eps5", ln_rstd)
                act.wait_ge(ln_turned.sem, ln_turned.at(g, 1))
                act.activation(tT[:, :], pe_[:, :], ACT.Identity, scale=w("gl"),
                               bias=w("bl")).then_inc(ln_kept.sem, 1)
                for t in range(TILES + 1):
                    if t < TILES:
                        src = (pa, pc)[t % 2]
                        act.wait_ge(yq_made.sem, yq_made.at(g, t + 1))
                        act.activation(sqt, src[:, :], ACT.Square).then_inc(yq_squared.sem, 1)
                        act.wait_ge(yq_sum.sem, yq_sum.at(g, t + 1))
                        own(act.activation(rq, mx[:, t % 2, :], ACT.Ln))
                        act.activation(rq, rq, ACT.Exp, scale=-0.5).then_inc(yq_root.sem, 1)
                    if t >= 1:
                        act.wait_ge(yq_turned.sem, yq_turned.at(g, t))
                        act.activation(qblk[0:DH, :, 0, (t - 1) * P:t * P], hview(pb[0:DH, :], P), ACT.Copy,
                                       scale=gqk[0:DH]).then_inc(yq_a.sem, 1)
                for c in range(2):
                    for p in range(NP):
                        act.wait_ge(yk_made.sem, yk_made.at(g, NP * c + p + 1))
                        act.activation(kt[:, p, :], pb[:, 512 * (p % 2):512 * (p % 2) + 512],
                                       ACT.Copy).then_inc(yk_kept.sem, 1)
                    act.wait_ge(yk_summed.sem, yk_summed.at(g, NP * c + NP))
                    act.activation(st[:, 0, 0:512], pd[:, :], ACT.Copy).then_inc(yk_sum_kept.sem, 1)
                    act.wait_ge(yk_mean.sem, yk_mean.at(g, c + 1))
                    own(act.activation(rkl, rk, ACT.Ln))
                    act.activation(rk, rkl, ACT.Exp, scale=-0.5).then_inc(yk_root.sem, 1)
                    for i in range(4):
                        b = 4 * c + i
                        act.wait_ge(yv_made.sem, yv_made.at(g, b + 1))
                        if b >= 2:
                            act.wait_ge(yz_made.sem, yz_made.at(g, b - 1))
                        act.activation(v[:, b % 2, :], pa[:, :], ACT.Copy).then_inc(yv_kept.sem, 1)
                        act.wait_ge(ys_scaled.sem, ys_scaled.at(g, b + 1))
                        act.activation(st[:, b % 2, :], st[:, b % 2, :], ACT.Exp,
                                       bias=mbl[:, b:b + 1]).then_inc(yp_ready.sem, 1)
                root(x5_stat, "eps5", x5_rstd)
                act.wait_ge(gap_ready.sem, gap_ready.at(g, 1))
                act.activation(p2, p2, ACT.Exp).then_inc(gap_exp.sem, 1)
                act.wait_ge(cw_turned.sem, cw_turned.at(g, 1))
                act.activation(cwt[:, :], pc[0:E8, 512:1024], ACT.Copy).then_inc(cwt_ready.sem, 1)
                root(x6_stat, "eps5", x6_rstd)
                own.done()

        @block.gpsimd
        def _(pool):
            pool.memset(qblk[:, :, :, :], 0.0)
            pool.memset(pblk[:, :, :, :], 0.0)
            pool.memset(peaks, 0.0)
            pool.memset(y[:, :, :], 0.0).then_inc(setup.sem, 1)
            pool.wait_ge(loaded.sem, LOADED_A)
            pool.wait_ge(setup.sem, 2)

            def pass_a(a, x):
                own = Chain(pool, pool_own)

                def residual():
                    pool.wait_ge(x_loaded.sem, x_loaded.at(a, 16))
                    pool.wait_ge(stat1.sem, stat1.at(a, 0))
                    pool.tensor_tensor(xb[:, :, :], x_in[:, :, :], tiled(w("ro0"), TILES),
                                       ALU.add).then_inc(xb_ready.sem, 1)

                def residual_x():
                    pool.wait_ge(x1_ready.sem, x1_ready.at(x, 1))
                    pool.wait_ge(r2_ready.sem, r2_ready.at(x, 0))
                    pool.tensor_tensor(xbx[:, :, :], x1[:, :, :], tiled(w("rxo"), TILES),
                                       ALU.add).then_inc(x1b_ready.sem, 1)

                def bias_vx():
                    pool.wait_ge(vx_masked.sem, vx_masked.at(x, 1))
                    pool.tensor_tensor(vdata, vdata, tiled(vbias, SEQ).rearrange("p b (i n) -> p b i n", n=16),
                                       ALU.add).then_inc(vx_ready.sem, 1)

                def scale_v(t):
                    pool.wait_ge(s_norm.sem, s_norm.at(a, t + 1))
                    pool.wait_ge(v_kept.sem, v_kept.at(a, t + 1))
                    pool.tensor_tensor(hview(v[:, t % 2, :]), hview(v[:, t % 2, :]), over(rs[:, t % 2, :], DH),
                                       ALU.mult).then_inc(v_scaled.sem, 1)

                def ffn_input():
                    pool.wait_ge(rstd3.sem, rstd3.at(x, 1))
                    pool.wait_ge(peak_kept.sem, peak_kept.at(x, 1))
                    pool.sem_inc(pool_hold, 1)
                    pool.tensor_copy(state[:, bass.ds(x * GT, GT)], flat(x2))
                    pool.tensor_copy(fstat[:, bass.ds(x * 8, 4)], mvx[:, :, 0])
                    pool.tensor_copy(fstat[:, bass.ds(x * 8 + 4, 4)], rstdf)
                    for t in range(TILES):
                        last = pool.tensor_scalar(y[:, t, :], x2[:, t, :], mvx[:, t, 0:1], rstdf[:, t:t + 1],
                                                  ALU.subtract, ALU.mult)
                    own(last)
                    own(pool.tensor_tensor(y[:, :, :], y[:, :, :], tiled(w("rfg"), TILES), ALU.mult))
                    pool.tensor_tensor(y[:, :, :], y[:, :, :], tiled(w("rfb"), TILES), ALU.add).then_inc(peak_done.sem, 1)

                if a is not None:
                    residual()
                if x is not None:
                    bias_vx()
                    residual_x()
                if a is not None:
                    for t in range(TILES):
                        scale_v(t)
                if x is not None:
                    ffn_input()
                own.done()

            pass_a(0, None)
            with pool.Fori(1, G) as g:
                pass_a(g, g - 1)
            pass_a(None, G - 1)
            pool.wait_ge(loaded.sem, LOADED_B)
            pool.wait_ge(peak_local.sem, 1)
            pool.wait_ge(weight_sum.sem, 1)
            pool.partition_all_reduce(ffs[:, 1:2], ffs[:, 3:4], P, bass.bass_isa.ReduceOp.max)
            pool.partition_all_reduce(ffs[:, 2:3], ffs[:, 0:1], P, bass.bass_isa.ReduceOp.add).then_inc(peak_all.sem, 1)
            with pool.Fori(0, G) as g:
                own = Chain(pool, pool_own)
                pool.wait_ge(z1_made.sem, z1_made.at(g, 0))
                pool.wait_ge(yp_ready.sem, yp_ready.at(g, 0))
                pool.sem_inc(pool_hold, 1)
                pool.tensor_copy(flat(x2), state[:, bass.ds(g * GT, GT)])
                pool.tensor_copy(mbl, maskb[:, bass.ds(g * SEQ, SEQ)])
                own(pool.tensor_copy(fstl, fstat[:, bass.ds(g * 8, 8)]))
                pool.wait_ge(ln_turned.sem, ln_turned.at(g, 0))
                for t in range(TILES):
                    last = pool.tensor_scalar(nrm[:, t, :], x2[:, t, :], fstl[:, t:t + 1], fstl[:, 4 + t:5 + t],
                                              ALU.subtract, ALU.mult)
                own(last)
                own(pool.tensor_tensor(nrm[:, :, :], nrm[:, :, :], tiled(w("rfg"), TILES), ALU.mult))
                pool.tensor_tensor(nrm[:, :, :], nrm[:, :, :], tiled(w("rfb"), TILES), ALU.add).then_inc(xn_ready.sem, 1)
                pool.wait_ge(x3_ready.sem, x3_ready.at(g, 1))
                pool.tensor_tensor(xb[:, :, :], x1[:, :, :], tiled(w("ro1"), TILES), ALU.add).then_inc(x3b_ready.sem, 1)
                pool.wait_ge(x4_ready.sem, x4_ready.at(g, 1))
                pool.tensor_tensor(xb[:, :, :], zx[:, :, :], tiled(w("ryo"), TILES), ALU.add).then_inc(x4b_ready.sem, 1)
                pool.wait_ge(ln_kept.sem, ln_kept.at(g, 1))
                pool.sem_inc(pool_hold, 1)
                pool.tensor_copy(kvt[:, :, S:2 * S], hview(tT[:, :])).then_inc(lat_placed.sem, 1)
                for p in range(2 * NP):
                    pool.wait_ge(yk_kept.sem, yk_kept.at(g, p + 1))
                    if p == 0:
                        pool.wait_ge(yq_turned.sem, yq_turned.at(g, TILES))
                    if p == NP:
                        pool.wait_ge(yl_inv.sem, yl_inv.at(g, 4))
                        pool.wait_ge(yz_kept.sem, yz_kept.at(g, 4))
                    if p % NP >= 2:
                        pool.wait_ge(yk_summed.sem, yk_summed.at(g, p - 1))
                    pool.tensor_tensor(sqk[p % 2], kt[:, p % NP, :], kt[:, p % NP, :],
                                       ALU.mult).then_inc(yk_squared.sem, 1)
                own.done()

        @block.vector
        def _(dve):
            dve.wait_ge(loaded.sem, LOADED_A)
            dve.tensor_scalar(mqs, k("maskq"), float(DX) ** -0.5, None, ALU.mult).then_inc(gap_s.sem, 1)
            dve.wait_ge(gap_s.sem, 1)
            dve.tensor_scalar(bxqm, mqs, w("bxq"), None, ALU.mult)
            dve.tensor_tensor(vbias, k("mask2"), w("rxv"), ALU.mult)
            dve.tensor_copy(vblk[:, :, :, 16:18].rearrange("p b i n -> p (b i) n"), tiled(k("half"), SEQ * NP))
            dve.memset(maskb[S:P, :], 0.0)
            dve.tensor_scalar(maskb[0:S, :], mask8[:, :], -1.0, 1e30, ALU.add, ALU.mult).then_inc(setup.sem, 1)

            def pass_a(a, x):
                own = Chain(dve, dve_own)

                def norm_stats(src, stats, means, signal):
                    for t in range(TILES):
                        last = dve.bn_stats(stats[:, t, :], src[:, t, :])
                    own(last)
                    for t in range(TILES):
                        last = dve.bn_aggr(means[:, t, :], stats[:, t, :])
                    last.then_inc(signal.sem, 1)

                def norm_apply(n, dst, src, means, root, before, signal):
                    dve.wait_ge(before.sem, before.at(n, 1))
                    for t in range(TILES):
                        last = dve.tensor_scalar(dst[:, t, :], src[:, t, :], means[:, t, 0:1], root[:, t:t + 1],
                                                 ALU.subtract, ALU.mult)
                    last.then_inc(signal.sem, 1)

                def normalise():
                    dve.wait_ge(rms_ready.sem, rms_ready.at(a, 1))
                    dve.tensor_tensor(nrm[:, :, :], x_in[:, :, :], over(rms, D), ALU.mult).then_inc(n_ready.sem, 1)

                def keep_nt():
                    dve.wait_ge(n_turned.sem, n_turned.at(a, 1))
                    dve.tensor_copy(tT[:, :], pd[:, :]).then_inc(nt_ready.sem, 1)

                def keep_k(p):
                    dve.wait_ge(k_made.sem, k_made.at(a, p + 1))
                    dve.tensor_scalar(kt[:, p, :], pc[:, 512 * (p % 2):512 * (p % 2) + 512], w("bk0", p, p + 1), None,
                                      ALU.add).then_inc(k_kept.sem, 1)

                def keep_v(t):
                    dve.wait_ge(v_made.sem, v_made.at(a, t + 1))
                    dve.tensor_tensor(v[:, t % 2, :], pa[:, :], w("rv0"), ALU.add).then_inc(v_kept.sem, 1)

                def shift(t):
                    dve.wait_ge(s_made.sem, s_made.at(a, t + 1))
                    own(dve.tensor_reduce(mx[:, t % 2, :], hview(pc[:, :]), AX.X, ALU.max))
                    if t >= 2:
                        dve.wait_ge(p_ready.sem, p_ready.at(a, t - 1))
                    dve.tensor_tensor(hview(st[:, t % 2, :]), hview(pc[:, :]), over(mx[:, t % 2, :], S),
                                      ALU.subtract).then_inc(s_shifted.sem, 1)

                def sums(t):
                    dve.wait_ge(s_exp.sem, s_exp.at(a, t + 1))
                    own(dve.tensor_reduce(sm[:, t % 2, :], hview(st[:, t % 2, :]), AX.X, ALU.add))
                    if t >= 2:
                        dve.wait_ge(v_scaled.sem, v_scaled.at(a, t - 1))
                    dve.reciprocal(rs[:, t % 2, :], sm[:, t % 2, :]).then_inc(s_norm.sem, 1)

                def keep_kx():
                    dve.wait_ge(kx_made.sem, kx_made.at(x, 1))
                    for j in range(4):
                        last = dve.tensor_scalar(kj[:, j, :], pc[:, 512:1024], w("bxk"), k("mask4", j, j + 1), ALU.add,
                                                 ALU.mult)
                    last.then_inc(kx_kept.sem, 1)

                def keep_vx():
                    dve.wait_ge(vx_made.sem, vx_made.at(x, 1))
                    dve.tensor_tensor(vdata, pb[:, :].rearrange("p (b i n) -> p b i n", b=SEQ, n=16),
                                      tiled(k("mask2"), SEQ).rearrange("p b (i n) -> p b i n", n=16),
                                      ALU.mult).then_inc(vx_masked.sem, 1)

                def last_peak():
                    dve.wait_ge(peak_done.sem, peak_done.at(x, 0))
                    dve.tensor_reduce(peak[:, 0:1], flat(y), AX.X, ALU.max)
                    own(dve.tensor_reduce(peak[:, 1:2], flat(y), AX.X, ALU.min))
                    dve.tensor_tensor(peaks[:, 0:1], peaks[:, 0:1], peak[:, 0:1], ALU.max)
                    dve.tensor_tensor(peaks[:, 1:2], peaks[:, 1:2], peak[:, 1:2], ALU.min).then_inc(peak_kept.sem, 1)

                def shift_x(t):
                    dve.wait_ge(sx_made.sem, sx_made.at(x, t + 1))
                    own(dve.tensor_reduce(mxx, hview(pb[:, :]), AX.X, ALU.max))
                    dve.tensor_tensor(hview(stx[:, :]), hview(pb[:, :]), over(mxx, S),
                                      ALU.subtract).then_inc(sx_shifted.sem, 1)

                def keep_px(t):
                    dve.wait_ge(px_turned.sem, px_turned.at(x, t + 1))
                    dve.tensor_copy(pt[t % 2][:, 4:8, :].rearrange("p a n -> p (a n)"),
                                    pb[:, 512:1024]).then_inc(px_v.sem, 1)

                def keep_zx(t):
                    dve.wait_ge(zx_made.sem, zx_made.at(x, t + 1))
                    for b in range(2):
                        r = slice(S * b, S * b + S)
                        col = pe_[r, 0:36 * NP].rearrange("p (i n) -> p i n", n=36)
                        last = dve.reciprocal(rz[r], col[:, :, 18 * b + 16:18 * b + 18])
                    own(last)
                    for b in range(2):
                        r = slice(S * b, S * b + S)
                        col = pe_[r, 0:36 * NP].rearrange("p (i n) -> p i n", n=36)
                        last = dve.tensor_tensor(
                            zx[r, t, :].rearrange("p (i e d) -> p i e d", e=2, d=DX),
                            col[:, :, 18 * b:18 * b + 16].rearrange("p i (e d) -> p i e d", d=DX),
                            rz[r].unsqueeze(3).broadcast_to([S, NP, 2, DX]), ALU.mult)
                    last.then_inc(zx_ready.sem, 1)

                if a is not None:
                    normalise()
                if x is not None:
                    keep_kx()
                if a is not None:
                    keep_nt()
                    keep_k(0)
                if x is not None:
                    keep_vx()
                if a is not None:
                    for p in range(1, 5):
                        keep_k(p)
                if x is not None:
                    shift_x(0)
                if a is not None:
                    for p in range(5, NP):
                        keep_k(p)
                if x is not None:
                    keep_px(0)
                for t in range(TILES + 1):
                    if a is not None and t >= 1:
                        sums(t - 1)
                    if a is not None and t < TILES:
                        keep_v(t)
                        shift(t)
                    if x is not None and t < TILES:
                        keep_zx(t)
                        if t + 1 < TILES:
                            shift_x(t + 1)
                            keep_px(t + 1)
                if x is not None:
                    last_peak()
                if a is not None:
                    dve.wait_ge(o_made.sem, o_made.at(a, 1))
                    dve.wait_ge(xb_ready.sem, xb_ready.at(a, 1))
                    own(dve.tensor_tensor(flat(res), pd[:, :], flat(xb), ALU.add))
                    norm_stats(res, stats, mv, stat1)
                if x is not None:
                    dve.wait_ge(ox_made.sem, ox_made.at(x, 1))
                    dve.wait_ge(x1b_ready.sem, x1b_ready.at(x, 1))
                    own(dve.tensor_tensor(flat(resx), pe_[:, :], flat(xbx), ALU.add))
                    norm_stats(resx, statsx, mvx, r2_ready)
                if a is not None:
                    norm_apply(a, x1, res, mv, rstd, rstd1, x1_ready)
                if x is not None:
                    norm_apply(x, x2, resx, mvx, rstdx, rstd2, x2_ready)
                    dve.wait_ge(x2_ready.sem, x2_ready.at(x, 1))
                    norm_stats(x2, statsx, mvx, stat3)
                own.done()

            pass_a(0, None)
            with dve.Fori(1, G) as g:
                pass_a(g, g - 1)
            pass_a(None, G - 1)
            dve.wait_ge(loaded.sem, LOADED_B)
            dve.tensor_scalar(gqk, w("qg"), w("kg"), float(DH) ** -0.5, ALU.mult, ALU.mult)

            dve.wait_ge(peak_done.sem, G + peak_done.lead)
            steps = [0]

            def link(ins):
                steps[0] += 1
                ins.then_inc(gap_v.sem, 1)
                dve.wait_ge(gap_v.sem, steps[0])

            dve.tensor_reduce(peak[:, 0:1], flat(y), AX.X, ALU.max)
            link(dve.tensor_reduce(peak[:, 1:2], flat(y), AX.X, ALU.min))
            link(dve.tensor_tensor(ffs[:, 4:5], peaks[:, 0:1], peak[:, 0:1], ALU.max))
            link(dve.tensor_tensor(ffs[:, 5:6], peaks[:, 1:2], peak[:, 1:2], ALU.min))
            dve.scalar_tensor_tensor(ffs[:, 3:4], ffs[:, 5:6], -1.0, ffs[:, 4:5], ALU.mult,
                                     ALU.max).then_inc(peak_local.sem, 1)
            dve.wait_ge(peak_all.sem, 1)
            link(dve.reciprocal(ffs[:, 4:5], ffs[:, 1:2]))
            link(dve.tensor_scalar(ffs[:, 4:5], ffs[:, 4:5], QB, None, ALU.mult))
            link(dve.tensor_scalar(ffs[:, 5:6], ffs[:, 2:3], 1.0 / (D * D), None, ALU.mult))
            link(dve.tensor_scalar(ffs[:, 6:7], ffs[:, 5:6], ffs[:, 1:2], 1.0 / QB, ALU.mult, ALU.mult))
            link(dve.tensor_scalar(ffs[:, 7:8], ffs[:, 5:6], 1e-5, None, ALU.add))
            link(dve.reciprocal(ffs[:, 7:8], ffs[:, 7:8]))
            link(dve.tensor_scalar(wq[:, :], w("ffn"), ffs[:, 7:8], None, ALU.mult))
            link(dve.tensor_scalar(wq[:, :], wq[:, :], 12582912.0, None, ALU.add))
            link(dve.tensor_scalar(wq[:, :], wq[:, :], -12582912.0, None, ALU.add))
            dve.tensor_scalar(wq[:, :], wq[:, :], 1.0, -1.0, ALU.min, ALU.max).then_inc(between.sem, 1)
            dve.wait_ge(between.sem, 1)

            with dve.Fori(0, G) as g:
                own = Chain(dve, dve_own)

                def norm_stats(src, signal):
                    for t in range(TILES):
                        last = dve.bn_stats(stats[:, t, :], src[:, t, :])
                    own(last)
                    for t in range(TILES):
                        last = dve.bn_aggr(mv[:, t, :], stats[:, t, :])
                    last.then_inc(signal.sem, 1)

                def norm_apply(dst, src, before, signal):
                    dve.wait_ge(before.sem, before.at(g, 1))
                    for t in range(TILES):
                        last = dve.tensor_scalar(dst[:, t, :], src[:, t, :], mv[:, t, 0:1], rstd[:, t:t + 1],
                                                 ALU.subtract, ALU.mult)
                    last.then_inc(signal.sem, 1)

                dve.wait_ge(cb_loaded.sem, cb_loaded.at(g, 16))
                norm_stats(c_in, cn_stat)
                norm_apply(y, c_in, cn_rstd, cn_ready)
                dve.wait_ge(xn_turned.sem, xn_turned.at(g, 1))
                own(dve.tensor_scalar(tT[:, :], pe_[:, :], ffs[:, 4:5], QB - 1e-5, ALU.mult, ALU.min))
                dve.tensor_scalar(tT[:, :], tT[:, :], -QB + 1e-5, None, ALU.max).then_inc(xq_ready.sem, 1)
                dve.wait_ge(f_made.sem, f_made.at(g, 1))
                own(dve.scalar_tensor_tensor(flat(res), pa[:, 0:512], ffs[:, 6:7], flat(x2), ALU.mult, ALU.add))
                norm_stats(res, x3_stat)
                norm_apply(x1, res, x3_rstd, x3_ready)
                dve.wait_ge(x3_turned.sem, x3_turned.at(g, 1))
                dve.tensor_copy(tT[:, :], pe_[:, :]).then_inc(x3t_ready.sem, 1)
                dve.wait_ge(v1_made.sem, v1_made.at(g, 1))
                dve.tensor_copy(flat(x2), pa[:, 512:1024]).then_inc(v1_kept.sem, 1)
                dve.wait_ge(s1_made.sem, s1_made.at(g, 1))
                own(dve.tensor_reduce(mx[:, 0, 0:TILES], hview(pc[:, 0:512], P), AX.X, ALU.max))
                dve.tensor_tensor(hview(st[:, 0, 0:512], P), hview(pc[:, 0:512], P), over(mx[:, 0, 0:TILES], P),
                                  ALU.subtract).then_inc(s1_shifted.sem, 1)
                dve.wait_ge(s1_exp.sem, s1_exp.at(g, 1))
                own(dve.tensor_reduce(sm[:, 0, 0:TILES], hview(st[:, 0, 0:512], P), AX.X, ALU.add))
                own(dve.reciprocal(sm[:, 0, 0:TILES], sm[:, 0, 0:TILES]))
                dve.tensor_tensor(hview(st[:, 0, 0:512], P), hview(st[:, 0, 0:512], P), over(sm[:, 0, 0:TILES], P),
                                  ALU.mult).then_inc(p1_ready.sem, 1)
                dve.wait_ge(o1_made.sem, o1_made.at(g, 1))
                dve.wait_ge(x3b_ready.sem, x3b_ready.at(g, 1))
                own(dve.tensor_tensor(flat(res), pa[:, 0:512], flat(xb), ALU.add))
                norm_stats(res, x4_stat)
                dve.wait_ge(stored.sem, stored.at(g, 0))
                norm_apply(zx, res, x4_rstd, x4_ready)
                dve.wait_ge(x4_ready.sem, x4_ready.at(g, 1))
                norm_stats(zx, ln_stat)
                norm_apply(nrm, zx, ln_rstd, ln_ready)
                for t in range(TILES + 1):
                    if t < TILES:
                        src = (pa, pc)[t % 2]
                        dve.wait_ge(yq_squared.sem, yq_squared.at(g, t + 1))
                        own(dve.tensor_reduce(sm[:, t % 2, :], hview(sqt), AX.X, ALU.add))
                        dve.tensor_scalar(mx[:, t % 2, :], sm[:, t % 2, :], 1.0 / DH, 1e-16, ALU.mult, ALU.max).then_inc(yq_sum.sem, 1)
                    if t >= 1:
                        dve.wait_ge(yq_turned.sem, yq_turned.at(g, t))
                        dve.tensor_scalar(qblk[DH:P, :, 1, (t - 1) * P:t * P], hview(pb[DH:P, :], P), gqk[DH:P],
                                          None, ALU.mult).then_inc(yq_v.sem, 1)
                    if t < TILES:
                        dve.wait_ge(yq_root.sem, yq_root.at(g, t + 1))
                        dve.tensor_tensor(hview(qs), hview(src[:, :]), over(rq, DH),
                                          ALU.mult).then_inc(yq_scaled.sem, 1)
                for c in range(2):
                    dve.wait_ge(yk_sum_turned.sem, yk_sum_turned.at(g, c + 1))
                    dve.tensor_scalar(rk.rearrange("p b (r n) -> p b r n", n=4),
                                      pd[:, :].rearrange("p (b r n) -> p b r n", b=4, n=32)[:, :, :, 0:4],
                                      1.0 / DH, 1e-16, ALU.mult, ALU.max).then_inc(yk_mean.sem, 1)
                    dve.wait_ge(yk_root.sem, yk_root.at(g, c + 1))
                    for i in range(5):
                        b = 4 * c + i
                        if i < 4:
                            dve.wait_ge(ys_made.sem, ys_made.at(g, b + 1))
                            if b >= 2:
                                dve.wait_ge(yz_made.sem, yz_made.at(g, b - 1))
                            dve.tensor_tensor(hview(st[:, b % 2, :]), hview(pc[:, :]), over(rk[:, i, :], S),
                                              ALU.mult).then_inc(ys_scaled.sem, 1)
                        if i >= 1:
                            u = b - 1
                            dve.wait_ge(yl_made.sem, yl_made.at(g, u + 1))
                            dve.reciprocal(sqk[u % 2], pd[:, :]).then_inc(yl_inv.sem, 1)
                            dve.wait_ge(yl_inv.sem, yl_inv.at(g, u + 1))
                            dve.wait_ge(yz_made.sem, yz_made.at(g, u + 1))
                            for e in range(2):
                                r = slice(DH * e, DH * e + DH)
                                last = dve.tensor_tensor(
                                    zt[r, :, S * u:S * u + S],
                                    pb[r, :].rearrange("p (a e n) -> p a e n", e=2, n=S)[:, :, e, :],
                                    hview(sqk[u % 2][r]), ALU.mult)
                            last.then_inc(yz_kept.sem, 1)
                dve.wait_ge(yo_made.sem, yo_made.at(g, 1))
                dve.wait_ge(x4b_ready.sem, x4b_ready.at(g, 1))
                own(dve.tensor_tensor(flat(res), pe_[:, :], flat(xb), ALU.add))
                norm_stats(res, x5_stat)
                norm_apply(x1, res, x5_rstd, x5_ready)
                dve.wait_ge(x5_turned.sem, x5_turned.at(g, 1))
                dve.tensor_copy(tT[:, :], pd[:, :]).then_inc(x5t_ready.sem, 1)
                dve.wait_ge(gate_made.sem, gate_made.at(g, 1))
                own(dve.tensor_copy(lg.rearrange("p t e -> p (t e)"), pc[:, 0:TILES * E8]))
                for t in range(TILES):
                    last = dve.max(top[:, t, :], lg[:, t, :])
                own(last)
                for t in range(TILES):
                    last = dve.max_index(topu[:, t, :], top[:, t, :], lg[:, t, :])
                own(last)
                dve.tensor_tensor(p2, top[:, :, 1], top[:, :, 0], ALU.subtract).then_inc(gap_ready.sem, 1)
                own(dve.tensor_copy(ix, topu[:, :, 0:2]))
                own(dve.tensor_tensor(selc, tiled(k("iota"), TILES), over(ix[:, :, 0], E8), ALU.is_equal))
                own(dve.tensor_tensor(selc2, tiled(k("iota"), TILES), over(ix[:, :, 1], E8), ALU.is_equal))
                dve.wait_ge(gap_exp.sem, gap_exp.at(g, 1))
                own(dve.tensor_scalar(p1, p2, 1.0, None, ALU.add))
                own(dve.reciprocal(p1, p1))
                own(dve.tensor_tensor(ix[:, :, 1], p2, p1, ALU.mult))
                own(dve.tensor_tensor(selc, selc, over(p1, E8), ALU.mult))
                own(dve.tensor_tensor(selc2, selc2, over(ix[:, :, 1], E8), ALU.mult))
                dve.tensor_tensor(cw, selc, selc2, ALU.add).then_inc(cw_ready.sem, 1)
                dve.wait_ge(cw_ready.sem, cw_ready.at(g, 1))
                for t in range(TILES):
                    dve.wait_ge(e_made.sem, e_made.at(g, t + 1))
                    dve.tensor_tensor(hview(st[:, t % 2, :], D), hview((pa, pb)[t % 2][:, :], D), over(cw[:, t, :], D),
                                      ALU.mult).then_inc(e_scaled.sem, 1)
                    dve.wait_ge(e_scaled.sem, e_scaled.at(g, t + 1))
                    own(dve.tensor_reduce(y[:, t, :], st[:, t % 2, :].rearrange("p (e n) -> p n e", e=E8), AX.X,
                                          ALU.add))
                dve.wait_ge(be_made.sem, be_made.at(g, 1))
                own(dve.tensor_tensor(flat(res), pd[:, :], flat(x1), ALU.add))
                own(dve.tensor_tensor(flat(res), flat(res), flat(y), ALU.add))
                norm_stats(res, x6_stat)
                norm_apply(zx, res, x6_rstd, x6_ready)
                own.done()


def pack(table, parts):
    rows = [np.asarray(parts[name]).reshape(P, width) for name, width in table]
    return np.ascontiguousarray(np.concatenate(rows, axis=1))


def constants():
    i, j = np.arange(P)[:, None], np.arange(P)[None, :]
    f = np.float32
    sel = np.zeros((P, 64), f)
    for e in range(2):
        sel[DH * e:DH * e + DH, e] = 1.0
        sel[DH * e:DH * e + DH, 32 + 2 + e] = 1.0
    parts = {
        "ident": (i == j).astype(f), "ones": np.ones((P, P), f), "sel": sel,
        "mask4": ((i % 32) // DX == np.arange(4)[None, :]).astype(f),
        "maskq": (i // 32 == np.arange(4)[None, :]).astype(f),
        "mask2": ((i < S) == ((j // DX) % 2 == 0)).astype(f),
        "half": np.concatenate([(i < S), (i >= S)], axis=1).astype(f),
        "eps0": np.full((P, 1), 1.1920929e-07, f), "eps5": np.full((P, 1), 1e-5, f), "eps3": np.full((P, 1), 1e-3, f),
        "iota": np.broadcast_to(np.arange(E8, dtype=f), (P, E8)), "zero": np.zeros((P, 1), f),
    }
    low = -60000.0
    m0 = np.where(np.arange(S)[None, :] >= i % S, 0.0, low)
    m1 = np.where((i // S == j // S) & (j <= i), 0.0, low)
    wide = np.concatenate([np.eye(P), np.tile(m0, (1, 8)), np.tile(m1, (1, 4))], axis=1)
    return pack(CONSTS, parts), wide.astype(np.float16)


def kernel(**a):
    from concourse import bacc
    from concourse.bass_utils import run_bass_kernel_spmd

    a = {name: np.asarray(value) for name, value in a.items()}
    ctx = a["ctx_1024"].reshape(B * S, D)
    wqkv = a["L0_attn_W_qkv"].reshape(NH, DH, 3, D)
    bqkv = a["L0_attn_b_qkv"].reshape(NH, DH, 3)

    def by_pair(m):
        return m.reshape(NP, P, D).transpose(1, 0, 2)

    def rows(r):
        return np.broadcast_to(r.reshape(1, -1), (P, r.size))

    def twice(r):
        return np.concatenate([r, r])

    wkv = a["L1_xattn_Wkv"]
    parts = {
        "q0": wqkv[:, :, 0].reshape(INNER, D).T, "k0": wqkv[:, :, 1].reshape(INNER, D).T,
        "v0": wqkv[:, :, 2].reshape(INNER, D).T, "o0": by_pair(a["L0_attn_W_o"].T),
        "xq": a["L0_xattn_Wq"], "xk": a["L0_xattn_Wk"], "xv": a["L0_xattn_Wv"], "xo": a["L0_xattn_Wo"],
        "ffn": a["L0_ffn_weight"], "basis": a["L1_attn_W_basis"].T, "v1": a["L1_attn_W_v"].T,
        "o1": a["L1_attn_W_o"].T, "yq": a["L1_xattn_Wq"], "yk": wkv[:, :INNER], "yv": wkv[:, INNER:],
        "yo": by_pair(a["L1_xattn_Wout"]), "gate": a["L1_ffn_Wg"].T,
        "exp": a["L1_ffn_We"].transpose(2, 0, 1),
        "bq0": bqkv[:, :, 0].reshape(NP, P).T, "bk0": bqkv[:, :, 1].reshape(NP, P).T,
        "bxq": a["L0_xattn_bq"], "bxk": a["L0_xattn_bk"], "bv1": a["L1_attn_b_v"],
        "gx": a["L1_xattn_ln_x_g"], "bx": a["L1_xattn_ln_x_b"], "gl": a["L1_xattn_ln_l_g"],
        "bl": a["L1_xattn_ln_l_b"], "qg": twice(a["L1_xattn_qn_g"]), "kg": twice(a["L1_xattn_kn_g"]),
        "rv0": rows(bqkv[:, :, 2]), "ro0": rows(a["L0_attn_b_o"]), "rxv": rows(a["L0_xattn_bv"]),
        "rxo": rows(a["L0_xattn_bo"]), "rfg": rows(a["L0_ffn_ln_gamma"]), "rfb": rows(a["L0_ffn_ln_beta"]),
        "ro1": rows(a["L1_attn_b_o"]), "ryo": rows(a["L1_xattn_bout"]),
    }
    consts, consts16 = constants()
    arrays = {
        "x": np.ascontiguousarray(a["x"].reshape(B * S, D)),
        "ctx_t": np.ascontiguousarray(ctx.T),
        "ctx": np.ascontiguousarray(ctx),
        "mask_t": np.ascontiguousarray(a["mask_BxS2_bf1"].T).view(np.uint8),
        "weights_a": pack(WEIGHTS_A, parts),
        "weights_b": pack(WEIGHTS_B, parts),
        "weights_ab": pack(WEIGHTS_AB, parts),
        "be": np.ascontiguousarray(a["L1_ffn_be"]),
        "consts": consts,
        "consts16": consts16,
    }
    nc = bacc.Bacc("TRN2", target_bir_lowering=False, num_devices=1)
    args = [nc.dram_tensor(name, v.shape, mybir.dt.from_np(v.dtype), kind="ExternalInput").ap()
            for name, v in arrays.items()]
    args.append(nc.dram_tensor("out", (B * S, D), F32, kind="ExternalOutput").ap())
    decoder(nc, *args)
    r = run_bass_kernel_spmd(nc, [arrays], core_ids=[0])
    return r.results[0]["out"].reshape(B, S, D)
```

```python
from contextlib import ExitStack

import numpy as np

import concourse.bass as bass
from concourse import mybir

F32, F16, U32, U8 = mybir.dt.float32, mybir.dt.float16, mybir.dt.uint32, mybir.dt.uint8
ALU = mybir.AluOpType
ACT = mybir.ActivationFunctionType
AX = mybir.AxisListType

P = 128
B, S, D = 128, 64, 128
NH, DH = 16, 64
NP = NH // 2
INNER = NH * DH
TILES = 4
G = B * S // (TILES * P)
GT = TILES * P
SEQ = GT // S
NX = 16
DX = D // NX
R = 64
E8 = 8
QB = 128.0

WEIGHTS_A = [
    ("q0", INNER), ("k0", INNER), ("v0", INNER), ("o0", INNER),
    ("xq", D), ("xk", D), ("xv", D), ("xo", D), ("bq0", NP), ("bk0", NP), ("bxq", 1), ("bxk", 1),
    ("rv0", INNER), ("ro0", D), ("rxv", D), ("rxo", D),
]
WEIGHTS_B = [
    ("yq", INNER), ("yk", INNER), ("yv", INNER), ("yo", INNER),
    ("basis", R), ("v1", D), ("o1", D),
    ("gate", E8), ("exp", E8 * D), ("bv1", 1), ("gx", 1), ("bx", 1), ("gl", 1), ("bl", 1),
    ("qg", 1), ("kg", 1), ("ro1", D), ("ryo", D),
]
WIDE = 4 * INNER
WEIGHTS_AB = [("ffn", D), ("rfg", D), ("rfb", D)]
CONSTS = [
    ("ident", P), ("ones", P), ("sel", 64), ("mask4", 4), ("maskq", 4), ("mask2", P), ("half", 2),
    ("eps0", 1), ("eps5", 1), ("eps3", 1), ("iota", E8),
]


def columns(table):
    at, out = 0, {}
    for name, width in table:
        out[name] = slice(at, at + width)
        at += width
    return out, at


ACOL, AN = columns(WEIGHTS_A)
BCOL, BN = columns(WEIGHTS_B)
ABCOL, ABN = columns(WEIGHTS_AB)
CCOL, CN = columns(CONSTS)


class Signal:

    def __init__(self, sem, per, lead=0):
        self.sem, self.per, self.lead = sem, per, lead

    def at(self, g, n):
        return g * self.per + (n + self.lead)


class Chain:

    def __init__(self, eng, sem):
        self.eng, self.sem, self.n = eng, sem, 0

    def __call__(self, ins):
        self.n += 1
        ins.then_inc(self.sem, 1)
        self.eng.wait_ge(self.sem, self.n)

    def done(self):
        self.eng.sem_clear(self.sem)
        self.n = 0


def decoder(nc, x, ctx_t, ctx, mask_t, weights_a, weights_b, weights_ab, be, consts, consts16, out):
    x_v = x.rearrange("(g t p) c -> g p t c", t=TILES, p=P)
    ctx_v = ctx.rearrange("(g t p) c -> g p t c", t=TILES, p=P)
    ctxt_v = ctx_t.rearrange("c (g n) -> g c n", n=GT)
    out_v = out.rearrange("(g t p) c -> g p t c", t=TILES, p=P)

    with ExitStack() as stack:
        def sb(name, shape, dt=F32):
            return stack.enter_context(nc.sbuf_tensor(name, shape, dt))

        def ps(name, shape):
            return stack.enter_context(nc.psum_tensor(name, shape, F32))

        def sig(name, per=1, lead=0):
            return Signal(stack.enter_context(nc.semaphore(name)), per, lead)

        pa = ps("pa", [P, 1024])
        pb = ps("pb", [P, 1024])
        pc = ps("pc", [P, 1024])
        pd = ps("pd", [P, 512])
        pe_ = ps("pe", [P, 512])

        wts = sb("wts", [P, max(AN, BN)])
        wts_ab = sb("wts_ab", [P, ABN])
        cst = sb("cst", [P, CN])
        cst16 = sb("cst16", [P, P + 1024], F16)
        be_sb = sb("be_sb", [E8, D])
        ident16, causal_t, causal_1 = cst16[:, 0:P], cst16[:, P:P + 512], cst16[:, P + 512:P + 1024]

        def w(name, a=0, b=None):
            c, buffer = ((ACOL, wts) if name in ACOL else (BCOL, wts) if name in BCOL else (ABCOL, wts_ab))
            c = c[name]
            return buffer[:, c.start + a:c.start + b if b is not None else c.stop]

        def k(name, a=0, b=None):
            c = CCOL[name]
            return cst[:, c.start + a:c.start + b if b is not None else c.stop]

        ident = k("ident")
        state = sb("state", [P, G * GT])
        fstat = sb("fstat", [P, G * 2 * TILES])
        qblk = sb("qblk", [P, NP, 2, GT])
        kt = sb("kt", [P, NP, GT])
        v = sb("v", [P, 2, INNER])
        st = sb("st", [P, 2, 1024])
        zt = sb("zt", [P, NP, GT])
        pblk = sb("pblk", [P, NH, 2, S])
        x_in = sb("x_in", [P, TILES, D])
        c_in = sb("c_in", [P, TILES, D])
        nrm = sb("nrm", [P, TILES, D])
        tT = sb("tT", [P, GT])
        res = sb("res", [P, TILES, D])
        x1 = sb("x1", [P, TILES, D])
        xb = sb("xb", [P, TILES, D])
        zx = sb("zx", [P, TILES, D])
        y = sb("y", [P, TILES, D])
        x2 = sb("x2", [P, TILES, D])
        kq = sb("kq", [P, 8 * GT])
        stx = sb("stx", [P, 1024])
        tx = sb("tx", [P, GT])
        resx = sb("resx", [P, TILES, D])
        xbx = sb("xbx", [P, TILES, D])
        vblk = sb("vblk", [P, SEQ, NP, 18])
        small = sb("small", [P, 704])
        used = [0]

        def tiny(*shape):
            n = int(np.prod(shape))
            a = small[:, used[0]:used[0] + n]
            used[0] += n
            names = "abc"[:len(shape)]
            if len(shape) > 1:
                a = a.rearrange(f"p ({' '.join(names)}) -> p {' '.join(names)}", **dict(zip(names[1:], shape[1:])))
            return a

        ssq, lnv, rms = tiny(TILES), tiny(TILES), tiny(TILES)
        mx, sm, rs = tiny(2, NH), tiny(2, NH), tiny(2, NH)
        stats, mv = tiny(TILES, 6), tiny(TILES, 2)
        statsx, mvx = tiny(TILES, 6), tiny(TILES, 2)
        lnx, rstdx = tiny(TILES), tiny(TILES)
        mxx, smx = tiny(NH), tiny(TILES)
        rstd, rstdf = tiny(TILES), tiny(TILES)
        fstl = tiny(8)
        rq = tiny(2, NH)
        mbl = tiny(SEQ)
        peaks, peak = tiny(2), tiny(2)
        bxqm = tiny(4)
        mqs = tiny(4)
        rz = tiny(NP, 2)
        rk = tiny(4, NH)
        rkl = tiny(4, NH)
        gqk = tiny(1)
        ffs = tiny(8)
        lg = tiny(TILES, E8)
        top = tiny(TILES, E8)
        selc = tiny(TILES, E8)
        selc2 = tiny(TILES, E8)
        cw = tiny(TILES, E8)
        p1, p2 = tiny(TILES), tiny(TILES)
        ix = tiny(TILES, 2)
        maskb = sb("maskb", [P, B])
        mask8 = sb("mask8", [S, B], U8)
        topu = sb("topu", [P, TILES, E8], U32)
        wq = sb("wq", [P, D])
        fold = sb("fold", [P, 2 * D])

        qg = kq[:, 0:4 * GT].rearrange("p (j n) -> p j n", n=GT)
        kj = kq[:, 4 * GT:8 * GT].rearrange("p (j n) -> p j n", n=GT)
        latt, cwt, tl = kq[0:R, 0:GT], kq[0:E8, GT:2 * GT], kq[:, 2 * GT:3 * GT]
        x4 = kq[:, 3 * GT:4 * GT].rearrange("p (t c) -> p t c", c=D)
        cn = kq[:, 4 * GT:5 * GT].rearrange("p (t c) -> p t c", c=D)
        v1, z1 = kq[:, 5 * GT:6 * GT], kq[:, 6 * GT:7 * GT]
        s1, p1t = stx[:, 0:GT], stx[:, GT:2 * GT]
        x3, x5, x6 = x1, x_in, zx
        ztf = zt[:, :, :].rearrange("p a n -> p (a n)")
        zta = [ztf[:, 1024 * i:1024 * i + 1024].rearrange("p (a n) -> p a n", n=P) for i in range(2)]
        pt = [ztf[:, 2048 + 1024 * i:3072 + 1024 * i].rearrange("p (a n) -> p a n", n=P) for i in range(2)]
        pflat = pblk[:, :, :, :].rearrange("p h a n -> p (h a n)")
        mixed = pflat[:, 1024:2048]
        kvt = vblk[:, :, :, :].rearrange("p b i n -> p (b i n)")[:, 0:SEQ * P].rearrange("p (b n) -> p b n", n=P)
        vdata = vblk[:, :, :, 0:16]
        vbias = fold[:, 0:D]
        sqk = [pflat[:, 512 * i:512 * i + 512] for i in range(2)]

        def flat(a):
            return a[:, :, :].rearrange("p t c -> p (t c)")

        def hview(a, n=S):
            return a.rearrange("p (h n) -> p h n", n=n)

        def over(a, n):
            return a.unsqueeze(2).broadcast_to([a.shape[0], a.shape[1], n])

        def tiled(a, n):
            return a.unsqueeze(1).broadcast_to([a.shape[0], n, a.shape[1]])

        loaded, loaded_late = sig("loaded"), sig("loaded_late")
        setup = sig("setup")
        x_loaded, c_loaded = sig("x_loaded", 16), sig("c_loaded", 16)
        xb_ready, rms_ready, n_ready, n_turned, nt_ready = (
            sig("xb_ready", 1, 1), sig("rms_ready", 1), sig("n_ready", 1, 1), sig("n_turned", 1, 1), sig("nt_ready", 1))
        q_made, k_made, q_kept, k_kept = sig("q_made", NP), sig("k_made", NP), sig("q_kept", NP), sig("k_kept", NP)
        v_made, v_kept = sig("v_made", TILES), sig("v_kept", TILES)
        s_made, s_shifted, s_exp, s_norm = (
            sig("s_made", TILES), sig("s_shifted", TILES), sig("s_exp", TILES), sig("s_norm", TILES))
        p_ready, v_scaled = sig("p_ready", TILES), sig("v_scaled", TILES)
        z_made, z_kept, o_made = sig("z_made", TILES), sig("z_kept", TILES), sig("o_made", 1)
        stat1, rstd1, x1_ready, x1_turned, x1t_ready = (
            sig("stat1", 1, 1), sig("rstd1"), sig("x1_ready"), sig("x1_turned"), sig("x1t_ready"))
        kx_made, vx_made, vx_masked, vx_ready, qx_made, kx_kept, qx_kept = (
            sig("kx_made"), sig("vx_made", 1, 1), sig("vx_masked"), sig("vx_ready"), sig("qx_made"), sig("kx_kept"), sig("qx_kept"))
        sx_made, sx_shifted, sx_exp, px_turned = (
            sig("sx_made", TILES), sig("sx_shifted", TILES), sig("sx_exp", TILES), sig("px_turned", TILES))
        px_a, px_v = sig("px_a", TILES), sig("px_v", TILES)
        zx_made, zx_ready, zx_turned, zxt_ready, ox_made = (
            sig("zx_made", TILES), sig("zx_ready", TILES), sig("zx_turned"), sig("zxt_ready"), sig("ox_made"))
        x1b_ready, r2_ready, rstd2, x2_ready, stat3, rstd3, peak_done = (
            sig("x1b_ready"), sig("r2_ready", 1, 1), sig("rstd2"), sig("x2_ready"), sig("stat3"), sig("rstd3"), sig("peak_done", 1, 1))

        peak_local, weight_sum, peak_all, between = sig("peak_local"), sig("weight_sum"), sig("peak_all"), sig("between")
        cb_loaded, xn_ready, xn_turned, xq_ready, f_made = (
            sig("cb_loaded", 16), sig("xn_ready"), sig("xn_turned"), sig("xq_ready"), sig("f_made"))
        cn_stat, cn_rstd, cn_ready, cn_turned, cn_kept = (
            sig("cn_stat"), sig("cn_rstd"), sig("cn_ready", 1, 1), sig("cn_turned"), sig("cn_kept"))
        x3_stat, x3_rstd, x3_ready, x3_turned, x3t_ready, x3b_ready = (
            sig("x3_stat"), sig("x3_rstd"), sig("x3_ready"), sig("x3_turned"), sig("x3t_ready"), sig("x3b_ready"))
        lat_made, lat_kept, v1_made, v1_kept = sig("lat_made"), sig("lat_kept"), sig("v1_made"), sig("v1_kept")
        s1_made, s1_shifted, s1_exp, p1_ready, p1_turned, p1t_ready, z1_made, z1_kept, o1_made = (
            sig("s1_made"), sig("s1_shifted"), sig("s1_exp"), sig("p1_ready"), sig("p1_turned"), sig("p1t_ready"),
            sig("z1_made"), sig("z1_kept"), sig("o1_made"))
        x4_stat, x4_rstd, x4_ready, x4b_ready, ln_stat, ln_rstd, ln_ready, ln_turned, ln_kept = (
            sig("x4_stat"), sig("x4_rstd"), sig("x4_ready"), sig("x4b_ready"), sig("ln_stat"), sig("ln_rstd"),
            sig("ln_ready"), sig("ln_turned"), sig("ln_kept"))
        yq_made, yq_squared, yq_sum, yq_root, yq_scaled, yq_turned, yq_a, yq_v = (
            sig("yq_made", TILES), sig("yq_squared", TILES), sig("yq_sum", TILES), sig("yq_root", TILES),
            sig("yq_scaled", TILES), sig("yq_turned", TILES), sig("yq_a", TILES), sig("yq_v", TILES))
        yk_made, yk_kept, yk_squared_p, yk_squared_v, yk_summed = (
            sig("yk_made", 2 * NP), sig("yk_kept", 2 * NP), sig("yk_squared_p", NP), sig("yk_squared_v", NP), sig("yk_summed", 2 * NP))
        yk_sum_kept, yk_sum_turned, yk_mean, yk_root = (
            sig("yk_sum_kept", 2), sig("yk_sum_turned", 2), sig("yk_mean", 2), sig("yk_root", 2))
        yv_made, yv_kept, ys_made, ys_scaled, yp_ready, yl_made, yl_inv, yz_made, yz_kept, yo_made = (
            sig("yv_made", SEQ), sig("yv_kept", SEQ), sig("ys_made", SEQ), sig("ys_scaled", SEQ), sig("yp_ready", SEQ, 1),
            sig("yl_made", SEQ), sig("yl_inv", SEQ), sig("yz_made", SEQ), sig("yz_kept", SEQ), sig("yo_made"))
        x5_stat, x5_rstd, x5_ready, x5_turned, x5t_ready = (
            sig("x5_stat", 1, 1), sig("x5_rstd"), sig("x5_ready"), sig("x5_turned"), sig("x5t_ready"))
        gate_made, gap_ready, gap_exp, cw_ready, cw_turned, cwt_ready, be_made = (
            sig("gate_made"), sig("gap_ready"), sig("gap_exp"), sig("cw_ready"), sig("cw_turned"), sig("cwt_ready"),
            sig("be_made"))
        e_made, e_scaled, be_kept = sig("e_made", 2 * TILES), sig("e_scaled", 2 * TILES), sig("be_kept")
        x6_stat, x6_rstd, x6_ready, stored = sig("x6_stat"), sig("x6_rstd"), sig("x6_ready"), sig("stored", 16, 16)
        lat_placed, peak_kept = sig("lat_placed"), sig("peak_kept")
        act_own, dve_own, pool_own, pool_hold = [stack.enter_context(nc.semaphore(n))
                                                 for n in ("act_own", "dve_own", "pool_own", "pool_hold")]
        scale_step, setup_scale = sig("scale_step"), sig("setup_scale")
        LOADED_A = 7 * 16
        LOADED_B = LOADED_A + 2 * 16

        block = stack.enter_context(nc.Block())

        @block.sync
        def _(sp):
            for ahead in (xb_ready, n_ready, n_turned, stat1, vx_made, r2_ready, peak_done, cn_ready, stored, yp_ready,
                          x5_stat):
                sp.sem_inc(ahead.sem, ahead.lead)
            for dst, src in ((cst[:, :], consts), (cst16[:, :], consts16), (be_sb[:, :], be), (mask8[:, :], mask_t),
                             (wts[:, WIDE:AN], weights_a[:, WIDE:AN]), (wts_ab[:, :], weights_ab),
                             (wts[:, 0:2 * INNER], weights_a[:, 0:2 * INNER])):
                sp.dma_start(dst, src).then_inc(loaded.sem, 16)
            sp.dma_start(wts[:, 2 * INNER:WIDE], weights_a[:, 2 * INNER:WIDE]).then_inc(loaded_late.sem, 16)
            with sp.Fori(0, G) as g:
                sp.wait_ge(xb_ready.sem, xb_ready.at(g, 0))
                sp.wait_ge(n_ready.sem, n_ready.at(g, 0))
                sp.dma_start(x_in[:, :, :], x_v[g]).then_inc(x_loaded.sem, 16)
                sp.wait_ge(vx_made.sem, vx_made.at(g, 0))
                sp.dma_start(flat(c_in), ctxt_v[g]).then_inc(c_loaded.sem, 16)
            sp.wait_ge(o_made.sem, G)
            sp.dma_start(wts[:, 0:WIDE], weights_b[:, 0:WIDE]).then_inc(loaded.sem, 16)
            sp.wait_ge(peak_done.sem, G + peak_done.lead)
            sp.dma_start(wts[:, WIDE:BN], weights_b[:, WIDE:BN]).then_inc(loaded.sem, 16)

            def load_context(n):
                sp.wait_ge(cn_ready.sem, cn_ready.at(n, 0))
                sp.dma_start(c_in[:, :, :], ctx_v[n]).then_inc(cb_loaded.sem, 16)

            def store(f):
                sp.wait_ge(x6_ready.sem, x6_ready.at(f, 1))
                sp.dma_start(out_v[f], x6[:, :, :]).then_inc(stored.sem, 16)

            load_context(0)
            load_context(1)
            with sp.Fori(1, G - 1) as g:
                load_context(g + 1)
                store(g - 1)
            store(G - 2)
            store(G - 1)
            sp.wait_ge(stored.sem, 16 * G + stored.lead)

        @block.tensor
        def _(pe):
            pe.wait_ge(loaded.sem, LOADED_A)
            pe.wait_ge(setup.sem, 2)

            def turn(dst, src, signal):
                for t in range(TILES):
                    last = pe.transpose(dst[:, t * P:(t + 1) * P], src[:, t, :], ident)
                last.then_inc(signal.sem, 1)

            def pass_a(b, a, x):
                def context():
                    pe.wait_ge(c_loaded.sem, c_loaded.at(a, 16))
                    pe.wait_ge(s_shifted.sem, s_shifted.at(a, TILES))
                    ctxt = flat(c_in)
                    pe.matmul(pc[:, 512:1024], w("xk"), ctxt, start=True, stop=True).then_inc(kx_made.sem, 1)
                    for b in range(SEQ):
                        for e in range(2):
                            last = pe.matmul(pb[S * e:S * e + S, P * b:P * b + P], ctxt[:, S * b:S * b + S], w("xv"),
                                             start=True, stop=True)
                    last.then_inc(vx_made.sem, 1)

                def turn_x1():
                    pe.wait_ge(x1_ready.sem, x1_ready.at(x, 1))
                    pe.wait_ge(r2_ready.sem, r2_ready.at(x, 0))
                    turn(pe_, x1, x1_turned)

                def turn_n():
                    pe.wait_ge(n_ready.sem, n_ready.at(b, 1))
                    if a is not None:
                        pe.wait_ge(z_kept.sem, z_kept.at(a, TILES))
                    turn(pa[:, 512:1024], nrm, n_turned)

                def queries_x():
                    pe.wait_ge(x1t_ready.sem, x1t_ready.at(x, 1))
                    pe.matmul(pe_[:, :], w("xq"), tx[:, :], start=True, stop=True).then_inc(qx_made.sem, 1)

                def queries_keys(p):
                    if p == 0:
                        pe.wait_ge(nt_ready.sem, nt_ready.at(a, 1))
                    if p >= 2:
                        pe.wait_ge(q_kept.sem, q_kept.at(a, p - 1))
                    pe.matmul(pa[:, 512 * (p % 2):512 * (p % 2) + 512], w("q0", P * p, P * p + P), tT[:, :],
                              start=True, stop=True).then_inc(q_made.sem, 1)
                    if p == 1 and x is not None:
                        pe.wait_ge(kx_kept.sem, kx_kept.at(x, 1))
                    if p >= 2:
                        pe.wait_ge(k_kept.sem, k_kept.at(a, p - 1))
                    pe.matmul(pc[:, 512 * (p % 2):512 * (p % 2) + 512], w("k0", P * p, P * p + P), tT[:, :],
                              start=True, stop=True).then_inc(k_made.sem, 1)

                def values(t):
                    if t == 0:
                        pe.wait_ge(q_kept.sem, q_kept.at(a, NP))
                    else:
                        pe.wait_ge(v_kept.sem, v_kept.at(a, t))
                    if t >= 2:
                        pe.wait_ge(z_kept.sem, z_kept.at(a, t - 1))
                    for c in range(2):
                        last = pe.matmul(pa[:, 512 * c:512 * c + 512], tT[:, t * P:(t + 1) * P],
                                         w("v0", 512 * c, 512 * c + 512), start=True, stop=True)
                    last.then_inc(v_made.sem, 1)

                def scores(t):
                    if t == 0:
                        pe.wait_ge(k_kept.sem, k_kept.at(a, NP))
                    else:
                        pe.wait_ge(s_shifted.sem, s_shifted.at(a, t))
                    for c in range(2):
                        pe.matmul(pc[:, 512 * c:512 * c + 512], ident16, causal_t, start=True, stop=False,
                                  skip_group_check=True)
                    for p in range(NP):
                        for b in range(2):
                            at = t * P + b * S
                            last = pe.matmul(pc[S * b:S * b + S, P * p:P * p + P], kt[:, p, at:at + S],
                                             qblk[:, p, :, at:at + S], start=False, stop=(p % 4 == 3),
                                             skip_group_check=True)
                    last.then_inc(s_made.sem, 1)

                def attend(t):
                    pe.wait_ge(p_ready.sem, p_ready.at(a, t + 1))
                    pe.wait_ge(v_scaled.sem, v_scaled.at(a, t + 1))
                    pe.wait_ge(v_kept.sem, v_kept.at(a, min(t + 2, TILES)))
                    if t >= 1:
                        pe.wait_ge(z_kept.sem, z_kept.at(a, t))
                    for h in range(NH):
                        last = pe.matmul(pa[S * (h % 2):S * (h % 2) + S, P * (h // 2):P * (h // 2) + P],
                                         v[:, t % 2, DH * h:DH * h + DH],
                                         pblk[:, h, :, :], start=True, stop=True)
                    last.then_inc(z_made.sem, 1)

                def project(t):
                    if t == 0:
                        pe.wait_ge(stat1.sem, stat1.at(a, 0))
                    pe.wait_ge(z_kept.sem, z_kept.at(a, t + 1))
                    for p in range(NP):
                        last = pe.matmul(pd[:, t * P:t * P + P], zta[t % 2][:, p, :], w("o0", P * p, P * p + P),
                                         start=(p == 0), stop=(p == NP - 1))
                    if t == TILES - 1:
                        last.then_inc(o_made.sem, 1)

                def scores_x(t):
                    if t == 0:
                        pe.wait_ge(qx_kept.sem, qx_kept.at(x, 1))
                        pe.wait_ge(kx_kept.sem, kx_kept.at(x, 1))
                        pe.wait_ge(vx_masked.sem, vx_masked.at(x, 1))
                    else:
                        pe.wait_ge(px_a.sem, px_a.at(x, t))
                        pe.wait_ge(px_v.sem, px_v.at(x, t))
                    for q in range(4):
                        for b in range(2):
                            at = t * P + b * S
                            last = pe.matmul(pb[S * b:S * b + S, 256 * q:256 * q + 256], qg[:, q, at:at + S],
                                             kj[:, :, at:at + S], start=True, stop=True)
                    last.then_inc(sx_made.sem, 1)

                def turn_x(t):
                    pe.wait_ge(sx_exp.sem, sx_exp.at(x, t + 1))
                    for i in range(NP):
                        last = pe.transpose(pb[:, P * i:P * i + P], stx[:, P * i:P * i + P], ident)
                    last.then_inc(px_turned.sem, 1)

                def attend_x(t):
                    if t == 0:
                        pe.wait_ge(vx_ready.sem, vx_ready.at(x, 1))
                    else:
                        pe.wait_ge(zx_ready.sem, zx_ready.at(x, t))
                    pe.wait_ge(px_a.sem, px_a.at(x, t + 1))
                    pe.wait_ge(px_v.sem, px_v.at(x, t + 1))
                    for i in range(NP):
                        last = pe.matmul(pe_[:, 36 * i:36 * i + 36], pt[t % 2][:, i, :],
                                         vblk[:, 2 * t:2 * t + 2, i, :], start=True, stop=True)
                    last.then_inc(zx_made.sem, 1)

                def turn_zx():
                    pe.wait_ge(zx_ready.sem, zx_ready.at(x, TILES))
                    turn(pe_, zx, zx_turned)

                def project_x():
                    pe.wait_ge(zxt_ready.sem, zxt_ready.at(x, 1))
                    for t in range(TILES):
                        last = pe.matmul(pe_[:, t * P:(t + 1) * P], tx[:, t * P:(t + 1) * P], w("xo"),
                                         start=True, stop=True)
                    last.then_inc(ox_made.sem, 1)

                for p in range(NP):
                    if a is not None:
                        queries_keys(p)
                    if x is not None:
                        if p == 2:
                            turn_x1()
                        if p == 4:
                            queries_x()
                        if p == 6:
                            scores_x(0)
                for t in range(TILES + 2):
                    if a is not None and t < TILES:
                        values(t)
                    if x is not None and t < TILES:
                        turn_x(t)
                    if a is not None and t < TILES:
                        scores(t)
                    if x is not None and t < TILES:
                        attend_x(t)
                        if t + 1 < TILES:
                            scores_x(t + 1)
                    if x is not None and t == TILES:
                        turn_zx()
                    if a is not None and t == TILES:
                        context()
                    if x is not None and t == TILES:
                        project_x()
                    if a is not None and 1 <= t <= TILES:
                        attend(t - 1)
                    if b is not None and t == TILES + 1:
                        turn_n()
                    if a is not None and t >= 2:
                        project(t - 2)

            pass_a(0, None, None)
            pe.wait_ge(loaded_late.sem, 16)
            pass_a(1, 0, None)
            with pe.Fori(1, G - 1) as g:
                pass_a(g + 1, g, g - 1)
            pass_a(None, G - 1, G - 2)
            pass_a(None, None, G - 1)
            pe.wait_ge(loaded.sem, LOADED_B)
            def pass_b(f, m, n):
                def bank_free(signal, i, count=1):
                    if i is not None:
                        pe.wait_ge(signal.sem, signal.at(i, count))

                def turn_xn():
                    pe.wait_ge(xn_ready.sem, xn_ready.at(n, 1))
                    bank_free(gap_ready, f)
                    bank_free(cn_kept, m)
                    turn(pe_, nrm, xn_turned)

                def quantised():
                    pe.wait_ge(xq_ready.sem, xq_ready.at(n, 1))
                    pe.wait_ge(between.sem, 1)
                    for t in range(TILES):
                        last = pe.matmul(pe_[:, t * P:(t + 1) * P], tT[:, t * P:(t + 1) * P], wq[:, :],
                                         start=True, stop=True)
                    last.then_inc(f_made.sem, 1)

                def turn_x3():
                    pe.wait_ge(x3_ready.sem, x3_ready.at(n, 1))
                    bank_free(be_kept, f)
                    turn(pe_, x3, x3_turned)

                def latents_1():
                    pe.wait_ge(x3t_ready.sem, x3t_ready.at(n, 1))
                    pe.matmul(pe_[0:R, :], w("basis"), tT[:, :], start=True, stop=True).then_inc(lat_made.sem, 1)

                def values_1():
                    pe.wait_ge(lat_kept.sem, lat_kept.at(n, 1))
                    bank_free(e_scaled, f, 1)
                    for t in range(TILES):
                        last = pe.matmul(pe_[:, t * P:(t + 1) * P], tT[:, t * P:(t + 1) * P], w("v1"),
                                         start=True, stop=True)
                    last.then_inc(v1_made.sem, 1)

                def scores_1():
                    pe.wait_ge(v1_kept.sem, v1_kept.at(n, 1))
                    bank_free(e_scaled, f, 2)
                    pe.matmul(pe_[:, :], ident16, causal_1, start=True, stop=False, skip_group_check=True)
                    for t in range(TILES):
                        a = slice(t * P, (t + 1) * P)
                        last = pe.matmul(pe_[:, a], latt[:, a], latt[:, a], start=False, stop=(t == TILES - 1),
                                         skip_group_check=True)
                    last.then_inc(s1_made.sem, 1)

                def turn_p1():
                    pe.wait_ge(p1_ready.sem, p1_ready.at(n, 1))
                    bank_free(e_scaled, f, 4)
                    for t in range(TILES):
                        last = pe.transpose(pe_[:, t * P:(t + 1) * P], s1[:, t * P:(t + 1) * P], ident)
                    last.then_inc(p1_turned.sem, 1)

                def attend_1():
                    pe.wait_ge(p1t_ready.sem, p1t_ready.at(n, 1))
                    bank_free(e_scaled, f, 5)
                    for t in range(TILES):
                        last = pe.matmul(pe_[:, t * P:(t + 1) * P], v1[:, t * P:(t + 1) * P],
                                         p1t[:, t * P:(t + 1) * P], start=True, stop=True)
                    last.then_inc(z1_made.sem, 1)

                def project_1():
                    pe.wait_ge(z1_kept.sem, z1_kept.at(n, 1))
                    bank_free(e_scaled, f, 6)
                    for t in range(TILES):
                        last = pe.matmul(pe_[:, t * P:(t + 1) * P], z1[:, t * P:(t + 1) * P], w("o1"),
                                         start=True, stop=True)
                    last.then_inc(o1_made.sem, 1)

                def turn_ln():
                    pe.wait_ge(ln_ready.sem, ln_ready.at(n, 1))
                    bank_free(e_scaled, f, 8)
                    turn(pe_, nrm, ln_turned)

                def turn_cn():
                    pe.wait_ge(cn_ready.sem, cn_ready.at(n, 1))
                    bank_free(ln_kept, n)
                    turn(pe_, cn, cn_turned)

                def queries(i, t):
                    dst = (pc, pa)[t % 2]
                    if t == 0:
                        pe.wait_ge(ln_kept.sem, ln_kept.at(i, 1))
                    if t == 1:
                        pe.wait_ge(x5_stat.sem, x5_stat.at(m, 0))
                    if t >= 2:
                        pe.wait_ge(yq_a.sem, yq_a.at(m, t - 1))
                        pe.wait_ge(yq_v.sem, yq_v.at(m, t - 1))
                    for c in range(2):
                        last = pe.matmul(dst[:, 512 * c:512 * c + 512], tl[:, t * P:(t + 1) * P],
                                         w("yq", 512 * c, 512 * c + 512), start=True, stop=True)
                    last.then_inc(yq_made.sem, 1)

                def turn_q(t):
                    pe.wait_ge(yq_scaled.sem, yq_scaled.at(m, t + 1))
                    for p in range(NP):
                        last = pe.transpose((pc, pa)[t % 2][:, P * p:P * p + P], st[:, t % 2, P * p:P * p + P], ident)
                    last.then_inc(yq_turned.sem, 1)

                def keys(c, p):
                    if p == 0 and c == 0:
                        pe.wait_ge(lat_placed.sem, lat_placed.at(m, 1))
                        pe.wait_ge(cn_kept.sem, cn_kept.at(m, 1))
                    if p == 0 and c == 1:
                        pe.wait_ge(ys_scaled.sem, ys_scaled.at(m, 4))
                    if p >= 2:
                        pe.wait_ge(yk_kept.sem, yk_kept.at(m, NP * c + p - 1))
                    pe.matmul((pb, pc)[c][:, 512 * (p % 2):512 * (p % 2) + 512], w("yk", P * p, P * p + P),
                              kvt[:, 4 * c:4 * c + 4, :], start=True, stop=True).then_inc(yk_made.sem, 1)

                def key_sums(c, u):
                    if c == 1 and u == 0:
                        pe.wait_ge(yl_inv.sem, yl_inv.at(m, 4))
                    squared = (yk_squared_p, yk_squared_v)[u % 2]
                    pe.wait_ge(squared.sem, squared.at(m, NP // 2 * c + u // 2 + 1))
                    row = 32 * (u // 2)
                    pe.matmul(pd[row:row + 32, :], k("sel", 32 * (u % 2), 32 * (u % 2) + 32), sqk[u % 2],
                              start=(u % 2 == 0), stop=(u % 2 == 1), skip_group_check=True).then_inc(yk_summed.sem, 1)

                def turn_sums(c):
                    pe.wait_ge(yk_sum_kept.sem, yk_sum_kept.at(m, c + 1))
                    for i in range(4):
                        last = pe.transpose(pd[:, P * i:P * i + P], st[:, 0, P * i:P * i + P], ident)
                    last.then_inc(yk_sum_turned.sem, 1)

                def values_y(b):
                    if b == 0:
                        pe.wait_ge(yq_a.sem, yq_a.at(m, TILES))
                        pe.wait_ge(yq_v.sem, yq_v.at(m, TILES))
                    else:
                        pe.wait_ge(yv_kept.sem, yv_kept.at(m, b))
                    for h in range(2):
                        last = pe.matmul(pa[:, 512 * h:512 * h + 512], kvt[:, b, :],
                                         w("yv", 512 * h, 512 * h + 512), start=True, stop=True)
                    last.then_inc(yv_made.sem, 1)

                def scores_y(b):
                    if b % 4 == 0:
                        pe.wait_ge(yk_kept.sem, yk_kept.at(m, NP * (b // 4) + NP))
                    if b == 0:
                        pe.wait_ge(yq_a.sem, yq_a.at(m, TILES))
                        pe.wait_ge(yq_v.sem, yq_v.at(m, TILES))
                    else:
                        pe.wait_ge(ys_scaled.sem, ys_scaled.at(m, b))
                    at = P * (b % 4)
                    for p in range(NP):
                        last = pe.matmul(pc[:, P * p:P * p + P], kt[:, p, at:at + P],
                                         qblk[:, p, :, S * b:S * b + S], start=True, stop=True)
                    last.then_inc(ys_made.sem, 1)

                def attend_y(b):
                    pe.wait_ge(yp_ready.sem, yp_ready.at(m, b + 1))
                    pr = hview(st[:, b % 2, :])
                    if b % 4 == 0:
                        pe.wait_ge(yk_mean.sem, yk_mean.at(m, b // 4 + 1))
                    if b >= 1:
                        pe.wait_ge(yl_inv.sem, yl_inv.at(m, b))
                    for e in range(2):
                        last = pe.matmul(pd[S * e:S * e + S, :], k("ones", 0, S), pr[:, e:NH:2, :],
                                         start=True, stop=True)
                    last.then_inc(yl_made.sem, 1)
                    pe.wait_ge(yv_kept.sem, yv_kept.at(m, b + 1))
                    if b >= 1:
                        pe.wait_ge(yz_kept.sem, yz_kept.at(m, b))
                    for p in range(NP):
                        last = pe.matmul(pb[:, P * p:P * p + P], v[:, b % 2, P * p:P * p + P],
                                         st[:, b % 2, P * p:P * p + P], start=True, stop=True)
                    last.then_inc(yz_made.sem, 1)

                def project_y(t):
                    if t == 0:
                        pe.wait_ge(yv_kept.sem, yv_kept.at(m, SEQ))
                    pe.wait_ge(yz_kept.sem, yz_kept.at(m, 2 * t + 2))
                    for p in range(NP):
                        last = pe.matmul(pa[:, t * P:t * P + P], zt[:, p, t * P:t * P + P],
                                         w("yo", P * p, P * p + P), start=(p == 0), stop=(p == NP - 1))
                    if t == TILES - 1:
                        last.then_inc(yo_made.sem, 1)

                def turn_x5():
                    pe.wait_ge(x5_ready.sem, x5_ready.at(f, 1))
                    bank_free(cn_kept, m)
                    turn(pe_, x5, x5_turned)

                def gate():
                    pe.wait_ge(x5t_ready.sem, x5t_ready.at(f, 1))
                    for t in range(TILES):
                        last = pe.matmul(pe_[:, E8 * t:E8 * t + E8], tx[:, t * P:(t + 1) * P], w("gate"),
                                         start=True, stop=True)
                    last.then_inc(gate_made.sem, 1)

                def turn_cw():
                    pe.wait_ge(cw_ready.sem, cw_ready.at(f, 1))
                    bank_free(x3_stat, n)
                    for t in range(TILES):
                        last = pe.transpose(pe_[0:E8, t * P:(t + 1) * P], cw[:, t, :], ident)
                    last.then_inc(cw_turned.sem, 1)

                def expert_bias():
                    pe.wait_ge(cwt_ready.sem, cwt_ready.at(f, 1))
                    for t in range(TILES):
                        last = pe.matmul(pe_[:, t * P:(t + 1) * P], cwt[:, t * P:(t + 1) * P], be_sb[:, :],
                                         start=True, stop=True)
                    last.then_inc(be_made.sem, 1)

                def experts(i, before=None):
                    t, c = i // 2, i % 2
                    if i == 0:
                        bank_free(be_kept, f)
                    else:
                        bank_free(e_scaled, f, i)
                    if before is not None:
                        bank_free(before, n)
                    pe.matmul(pe_[:, :], tx[:, t * P:(t + 1) * P], w("exp", 512 * c, 512 * c + 512),
                              start=True, stop=True).then_inc(e_made.sem, 1)

                for c in range(2):
                    for p in range(NP + 2):
                        if m is not None and p < NP:
                            keys(c, p)
                        if m is not None and p >= 2:
                            key_sums(c, p - 2)
                        if m is not None and c == 0:
                            if p == 1:
                                queries(m, 1)
                                turn_q(0)
                            if p == 3:
                                turn_q(1)
                                queries(m, 2)
                            if p == 5:
                                queries(m, 3)
                            if p == 6:
                                turn_q(2)
                            if p == 8:
                                turn_q(3)
                        if f is not None and c == 0:
                            if p == 2:
                                turn_x5()
                            if p == 3:
                                gate()
                        if n is not None and c == 0:
                            if p == 5:
                                turn_xn()
                            if p == 6:
                                quantised()
                        if n is not None and c == 1:
                            if p == 3:
                                turn_p1()
                            if p == 6:
                                attend_1()
                        if f is not None and c == 1:
                            if p == 5:
                                experts(4, p1t_ready)
                            if p == 8:
                                experts(5, z1_kept)
                        if m is not None and p == 9:
                            values_y(4 * c)
                        if f is not None and c == 0 and p == 9:
                            turn_cw()
                        if n is not None and c == 1 and p == 9:
                            project_1()
                    if m is not None:
                        turn_sums(c)
                        scores_y(4 * c)
                    if f is not None:
                        if c == 0:
                            expert_bias()
                        else:
                            experts(6, x4_stat)
                    for i in range(1, 5):
                        if m is not None and i < 4:
                            values_y(4 * c + i)
                        if n is not None and c == 0 and i == 1:
                            turn_x3()
                        if m is not None and i < 4:
                            scores_y(4 * c + i)
                        if n is not None and c == 0:
                            if i == 1:
                                latents_1()
                            if i == 2:
                                values_1()
                            if i == 3:
                                scores_1()
                        if m is not None and c == 1 and i == 4:
                            for t in range(TILES - 1):
                                project_y(t)
                        if m is not None:
                            attend_y(4 * c + i - 1)
                        if f is not None and c == 0:
                            experts(i - 1, (lat_kept, v1_kept, s1_shifted, None)[i - 1])
                        if f is not None and c == 1 and i == 1:
                            experts(7)
                        if n is not None and c == 1:
                            if i == 2:
                                turn_ln()
                            if i == 3:
                                turn_cn()
                if n is not None:
                    queries(n, 0)
                if m is not None:
                    project_y(TILES - 1)

            pass_b(None, None, 0)
            pass_b(None, 0, 1)
            with pe.Fori(1, G - 1) as g:
                pass_b(g - 1, g, g + 1)
            pass_b(G - 2, G - 1, None)
            pass_b(G - 1, None, None)

        @block.scalar
        def _(act):
            act.preload_act_table_set("natural_log_exp_and_others")
            act.wait_ge(loaded.sem, LOADED_A)
            act.wait_ge(setup.sem, 2)

            def pass_a(b, a, x):
                own = Chain(act, act_own)

                def rms_root():
                    act.wait_ge(x_loaded.sem, x_loaded.at(b, 16))
                    act.wait_ge(n_turned.sem, n_turned.at(b, 0))
                    for t in range(TILES):
                        last = act.activation(nrm[:, t, :], x_in[:, t, :], ACT.Square, accum_out=ssq[:, t:t + 1])
                    own(last)
                    own(act.activation(lnv, ssq, ACT.Ln, scale=1.0 / D, bias=k("eps0")))
                    act.activation(rms, lnv, ACT.Exp, scale=-0.5).then_inc(rms_ready.sem, 1)

                def keep_q(p):
                    act.wait_ge(q_made.sem, q_made.at(a, p + 1))
                    for e in range(2):
                        r = slice(DH * e, DH * e + DH)
                        last = act.activation(qblk[r, p, e, :], pa[r, 512 * (p % 2):512 * (p % 2) + 512],
                                              ACT.Identity, bias=w("bq0", p, p + 1)[r])
                    last.then_inc(q_kept.sem, 1)

                def exps(t):
                    act.wait_ge(s_shifted.sem, s_shifted.at(a, t + 1))
                    act.activation(st[:, t % 2, :], st[:, t % 2, :], ACT.Exp).then_inc(s_exp.sem, 1)

                def place_p(t):
                    act.wait_ge(s_exp.sem, s_exp.at(a, t + 1))
                    if t >= 1:
                        act.wait_ge(z_made.sem, z_made.at(a, t))
                    for b in range(2):
                        r = slice(S * b, S * b + S)
                        last = act.activation(pblk[r, :, b, :], hview(st[r, t % 2, :]), ACT.Copy)
                    last.then_inc(p_ready.sem, 1)

                def keep_z(t):
                    act.wait_ge(z_made.sem, z_made.at(a, t + 1))
                    act.activation(zta[t % 2].rearrange("p a n -> p (a n)"), pa[:, :],
                                   ACT.Copy).then_inc(z_kept.sem, 1)

                def keep_nt():
                    act.wait_ge(n_turned.sem, n_turned.at(b, 1))
                    act.activation(tT[:, :], pa[:, 512:1024], ACT.Copy).then_inc(nt_ready.sem, 1)

                def keep_x1t():
                    act.wait_ge(x1_turned.sem, x1_turned.at(x, 1))
                    act.activation(tx[:, :], pe_[:, :], ACT.Copy).then_inc(x1t_ready.sem, 1)

                def keep_qx():
                    act.wait_ge(qx_made.sem, qx_made.at(x, 1))
                    for j in range(4):
                        last = act.activation(qg[:, j, :], pe_[:, :], ACT.Identity, scale=mqs[:, j:j + 1],
                                              bias=bxqm[:, j:j + 1])
                    last.then_inc(qx_kept.sem, 1)

                def exps_x(t):
                    act.wait_ge(sx_shifted.sem, sx_shifted.at(x, t + 1))
                    act.activation(stx[:, :], stx[:, :], ACT.Exp).then_inc(sx_exp.sem, 1)

                def keep_px(t):
                    act.wait_ge(px_turned.sem, px_turned.at(x, t + 1))
                    act.activation(pt[t % 2][:, 0:4, :].rearrange("p a n -> p (a n)"), pb[:, 0:512],
                                   ACT.Copy).then_inc(px_a.sem, 1)

                def keep_zxt():
                    act.wait_ge(zx_turned.sem, zx_turned.at(x, 1))
                    act.activation(tx[:, :], pe_[:, :], ACT.Copy).then_inc(zxt_ready.sem, 1)

                def root(n, before, eps, log, means, dst, signal):
                    act.wait_ge(before.sem, before.at(n, 1))
                    own(act.activation(log, means[:, :, 1], ACT.Ln, bias=k(eps)))
                    act.activation(dst, log, ACT.Exp, scale=-0.5).then_inc(signal.sem, 1)

                for p in range(NP):
                    if a is not None:
                        keep_q(p)
                    if x is not None:
                        if p == 2:
                            keep_x1t()
                        if p == 4:
                            keep_qx()
                        if p == 7:
                            exps_x(0)
                for t in range(TILES + 1):
                    if x is not None and t < TILES:
                        keep_px(t)
                    if a is not None and t < TILES:
                        exps(t)
                    if b is not None and t == TILES - 1:
                        rms_root()
                    if x is not None and t == TILES:
                        keep_zxt()
                    if a is not None and t >= 1:
                        keep_z(t - 1)
                    if x is not None and t + 1 < TILES:
                        exps_x(t + 1)
                    if a is not None and t < TILES:
                        place_p(t)
                if x is not None:
                    root(x, r2_ready, "eps5", lnx, mvx, rstdx, rstd2)
                if b is not None:
                    keep_nt()
                if x is not None:
                    root(x, stat3, "eps3", lnx, mvx, rstdf, rstd3)
                if a is not None:
                    root(a, stat1, "eps5", lnv, mv, rstd, rstd1)
                own.done()

            pass_a(0, None, None)
            pass_a(1, 0, None)
            with act.Fori(1, G - 1) as g:
                pass_a(g + 1, g, g - 1)
            pass_a(None, G - 1, G - 2)
            pass_a(None, None, G - 1)
            act.activation(fold[:, D:2 * D], w("ffn"), ACT.Abs, accum_out=ffs[:, 0:1]).then_inc(weight_sum.sem, 1)
            act.wait_ge(loaded.sem, LOADED_B)

            def pass_b(f, m, n):
                own = Chain(act, act_own)

                def root(i, before, log, means, dst, signal):
                    act.wait_ge(before.sem, before.at(i, 1))
                    own(act.activation(log, means[:, :, 1], ACT.Ln, bias=k("eps5")))
                    act.activation(dst, log, ACT.Exp, scale=-0.5).then_inc(signal.sem, 1)

                def root_n(before, signal):
                    root(n, before, lnx, mvx, rstdx, signal)

                def keep(dst, src, before, signal, **affine):
                    act.wait_ge(before.sem, before.at(n, 1))
                    act.activation(dst, src, ACT.Identity if affine else ACT.Copy, **affine).then_inc(signal.sem, 1)

                def exp_1():
                    act.wait_ge(s1_shifted.sem, s1_shifted.at(n, 1))
                    act.activation(s1, s1, ACT.Exp, scale=R ** -0.5).then_inc(s1_exp.sem, 1)

                def keep_ln():
                    if m is not None:
                        act.wait_ge(yq_made.sem, yq_made.at(m, TILES))
                    keep(tl, pe_[:, :], ln_turned, ln_kept, scale=w("gl"), bias=w("bl"))

                def keep_cn():
                    if m is not None:
                        act.wait_ge(yv_made.sem, yv_made.at(m, SEQ))
                    keep(kvt[:, :, 0:S], hview(pe_[:, :]), cn_turned, cn_kept, scale=w("gx"), bias=w("bx"))

                def query_square(i, t):
                    act.wait_ge(yq_made.sem, yq_made.at(i, t + 1))
                    act.activation(v[:, t % 2, :], (pc, pa)[t % 2][:, :], ACT.Square).then_inc(yq_squared.sem, 1)

                def query_root(i, t):
                    act.wait_ge(yq_sum.sem, yq_sum.at(i, t + 1))
                    own(act.activation(rq[:, t % 2, :], mx[:, t % 2, :], ACT.Ln))
                    act.activation(rq[:, t % 2, :], rq[:, t % 2, :], ACT.Exp, scale=-0.5).then_inc(yq_root.sem, 1)

                def keep_q(t):
                    act.wait_ge(yq_turned.sem, yq_turned.at(m, t + 1))
                    act.activation(qblk[0:DH, :, 0, t * P:(t + 1) * P], hview((pc, pa)[t % 2][0:DH, :], P), ACT.Copy,
                                   scale=gqk[0:DH]).then_inc(yq_a.sem, 1)

                def keep_k(c, p):
                    act.wait_ge(yk_made.sem, yk_made.at(m, NP * c + p + 1))
                    keys = (pb, pc)[c][:, 512 * (p % 2):512 * (p % 2) + 512]
                    if p % 2 == 1:
                        if p >= 2:
                            act.wait_ge(yk_summed.sem, yk_summed.at(m, NP * c + p - 1))
                        elif c == 1:
                            act.wait_ge(yz_kept.sem, yz_kept.at(m, 4))
                        act.activation(sqk[1], keys, ACT.Square).then_inc(yk_squared_v.sem, 1)
                    act.activation(kt[:, p, :], keys, ACT.Copy).then_inc(yk_kept.sem, 1)

                def keep_sums(c):
                    act.wait_ge(yk_summed.sem, yk_summed.at(m, NP * c + NP))
                    act.activation(st[:, 0, 0:512], pd[:, :], ACT.Copy).then_inc(yk_sum_kept.sem, 1)

                def key_root(c):
                    act.wait_ge(yk_mean.sem, yk_mean.at(m, c + 1))
                    own(act.activation(rkl, rk, ACT.Ln))
                    act.activation(rk, rkl, ACT.Exp, scale=-0.5).then_inc(yk_root.sem, 1)

                def keep_v(b):
                    act.wait_ge(yv_made.sem, yv_made.at(m, b + 1))
                    if b >= 2:
                        act.wait_ge(yz_made.sem, yz_made.at(m, b - 1))
                    act.activation(v[:, b % 2, :], pa[:, :], ACT.Copy).then_inc(yv_kept.sem, 1)

                def exps(b):
                    if b == 0:
                        act.wait_ge(x4b_ready.sem, x4b_ready.at(m, 1))
                    act.wait_ge(ys_scaled.sem, ys_scaled.at(m, b + 1))
                    act.activation(st[:, b % 2, :], st[:, b % 2, :], ACT.Exp,
                                   bias=mbl[:, b:b + 1]).then_inc(yp_ready.sem, 1)

                def inverse(b):
                    act.wait_ge(yl_made.sem, yl_made.at(m, b + 1))
                    if b >= 2:
                        act.wait_ge(yz_kept.sem, yz_kept.at(m, b - 1))
                    own(act.activation(sqk[b % 2], pd[:, :], ACT.Ln))
                    act.activation(sqk[b % 2], sqk[b % 2], ACT.Exp, scale=-1.0).then_inc(yl_inv.sem, 1)

                def gap():
                    act.wait_ge(gap_ready.sem, gap_ready.at(f, 1))
                    act.activation(p2, p2, ACT.Exp).then_inc(gap_exp.sem, 1)

                def keep_cwt():
                    act.wait_ge(cw_turned.sem, cw_turned.at(f, 1))
                    act.activation(cwt, pe_[0:E8, :], ACT.Copy).then_inc(cwt_ready.sem, 1)

                def keep_x5t():
                    act.wait_ge(x5_turned.sem, x5_turned.at(f, 1))
                    act.activation(tx[:, :], pe_[:, :], ACT.Copy).then_inc(x5t_ready.sem, 1)

                for c in range(2):
                    for p in range(NP + 1):
                        if m is not None and p < NP:
                            keep_k(c, p)
                        if m is not None and c == 0:
                            if p == 1:
                                query_square(m, 1)
                                keep_q(0)
                                query_root(m, 1)
                            if p == 3:
                                keep_q(1)
                                query_square(m, 2)
                            if p == 4:
                                query_root(m, 2)
                            if p == 8:
                                keep_q(3)
                        if f is not None and c == 0:
                            if p == 2:
                                keep_x5t()
                            if p == 4:
                                gap()
                        if m is not None and c == 0:
                            if p == 5:
                                query_square(m, 3)
                            if p == 6:
                                query_root(m, 3)
                                keep_q(2)
                        if n is not None and c == 0 and p == 8:
                            root_n(x3_stat, x3_rstd)
                        if n is not None and c == 1:
                            if p == 3:
                                keep(p1t, pe_[:, :], p1_turned, p1t_ready)
                            if p == 6:
                                keep(z1, pe_[:, :], z1_made, z1_kept, bias=w("bv1"))
                    if m is not None:
                        keep_sums(c)
                    if m is not None:
                        keep_v(4 * c)
                    if f is not None and c == 0:
                        keep_cwt()
                    if n is not None and c == 1:
                        root_n(x4_stat, x4_rstd)
                    if m is not None:
                        key_root(c)
                        exps(4 * c)
                    if n is not None and c == 1:
                        root_n(ln_stat, ln_rstd)
                    for i in range(1, 5):
                        if m is not None and i < 4:
                            keep_v(4 * c + i)
                        if n is not None and c == 0 and i == 1:
                            keep(tT[:, :], pe_[:, :], x3_turned, x3t_ready)
                        if m is not None and i < 4:
                            exps(4 * c + i)
                        if n is not None and c == 0:
                            if i == 1:
                                keep(latt, pe_[0:R, :], lat_made, lat_kept)
                            if i == 2:
                                keep(v1, pe_[:, :], v1_made, v1_kept)
                        if n is not None and c == 1 and i == 4:
                            keep_cn()
                        if m is not None:
                            inverse(4 * c + i - 1)
                        if n is not None and c == 0:
                            if i == 1:
                                root_n(cn_stat, cn_rstd)
                            if i == 3:
                                exp_1()
                        if n is not None and c == 1 and i == 2:
                            keep_ln()
                        if f is not None and c == 1 and i == 2:
                            root(f, x6_stat, lnv, mv, rstd, x6_rstd)
                if n is not None:
                    query_square(n, 0)
                    query_root(n, 0)
                if m is not None:
                    root(m, x5_stat, lnv, mv, rstd, x5_rstd)
                own.done()

            pass_b(None, None, 0)
            pass_b(None, 0, 1)
            with act.Fori(1, G - 1) as g:
                pass_b(g - 1, g, g + 1)
            pass_b(G - 2, G - 1, None)
            pass_b(G - 1, None, None)

        @block.gpsimd
        def _(pool):
            pool.memset(qblk[:, :, :, :], 0.0)
            pool.memset(pblk[:, :, :, :], 0.0)
            pool.memset(peaks, 0.0)
            pool.memset(y[:, :, :], 0.0).then_inc(setup.sem, 1)
            pool.wait_ge(loaded.sem, LOADED_A)
            pool.wait_ge(setup.sem, 2)

            def pass_a(b, a, x):
                own = Chain(pool, pool_own)

                def residual():
                    pool.wait_ge(x_loaded.sem, x_loaded.at(a, 16))
                    pool.wait_ge(stat1.sem, stat1.at(a, 0))
                    pool.tensor_tensor(xb[:, :, :], x_in[:, :, :], tiled(w("ro0"), TILES),
                                       ALU.add).then_inc(xb_ready.sem, 1)

                def residual_x():
                    pool.wait_ge(x1_ready.sem, x1_ready.at(x, 1))
                    pool.wait_ge(r2_ready.sem, r2_ready.at(x, 0))
                    pool.tensor_tensor(xbx[:, :, :], x1[:, :, :], tiled(w("rxo"), TILES),
                                       ALU.add).then_inc(x1b_ready.sem, 1)

                def bias_vx():
                    pool.wait_ge(vx_masked.sem, vx_masked.at(a, 1))
                    pool.tensor_tensor(vdata, vdata, tiled(vbias, SEQ).rearrange("p b (i n) -> p b i n", n=16),
                                       ALU.add).then_inc(vx_ready.sem, 1)

                def scale_v(t):
                    pool.wait_ge(s_norm.sem, s_norm.at(a, t + 1))
                    pool.wait_ge(v_kept.sem, v_kept.at(a, t + 1))
                    pool.tensor_tensor(hview(v[:, t % 2, :]), hview(v[:, t % 2, :]), over(rs[:, t % 2, :], DH),
                                       ALU.mult).then_inc(v_scaled.sem, 1)

                def ffn_input():
                    pool.wait_ge(rstd3.sem, rstd3.at(x, 1))
                    pool.wait_ge(peak_kept.sem, peak_kept.at(x, 1))
                    pool.sem_inc(pool_hold, 1)
                    pool.tensor_copy(state[:, bass.ds(x * GT, GT)], flat(x2))
                    pool.tensor_copy(fstat[:, bass.ds(x * 8, 4)], mvx[:, :, 0])
                    pool.tensor_copy(fstat[:, bass.ds(x * 8 + 4, 4)], rstdf)
                    for t in range(TILES):
                        last = pool.tensor_scalar(y[:, t, :], x2[:, t, :], mvx[:, t, 0:1], rstdf[:, t:t + 1],
                                                  ALU.subtract, ALU.mult)
                    own(last)
                    own(pool.tensor_tensor(y[:, :, :], y[:, :, :], tiled(w("rfg"), TILES), ALU.mult))
                    pool.tensor_tensor(y[:, :, :], y[:, :, :], tiled(w("rfb"), TILES), ALU.add).then_inc(peak_done.sem, 1)

                if a is not None:
                    residual()
                if x is not None:
                    residual_x()
                if a is not None:
                    for t in range(TILES):
                        scale_v(t)
                    bias_vx()
                if x is not None:
                    ffn_input()
                own.done()

            pass_a(0, None, None)
            pass_a(1, 0, None)
            with pool.Fori(1, G - 1) as g:
                pass_a(g + 1, g, g - 1)
            pass_a(None, G - 1, G - 2)
            pass_a(None, None, G - 1)
            pool.wait_ge(peak_local.sem, 1)
            pool.wait_ge(weight_sum.sem, 1)
            pool.partition_all_reduce(ffs[:, 1:2], ffs[:, 3:4], P, bass.bass_isa.ReduceOp.max)
            pool.partition_all_reduce(ffs[:, 2:3], ffs[:, 0:1], P, bass.bass_isa.ReduceOp.add).then_inc(peak_all.sem, 1)

            def pass_b(f, m, n):
                own = Chain(pool, pool_own)

                def residual_m():
                    pool.wait_ge(x4_ready.sem, x4_ready.at(m, 1))
                    pool.wait_ge(x5_stat.sem, x5_stat.at(m, 0))
                    pool.wait_ge(yp_ready.sem, yp_ready.at(m, 0))
                    pool.sem_inc(pool_hold, 1)
                    pool.tensor_copy(mbl, maskb[:, bass.ds(m * SEQ, SEQ)])
                    pool.tensor_tensor(xbx[:, :, :], x4, tiled(w("ryo"), TILES), ALU.add).then_inc(x4b_ready.sem, 1)

                def ffn_input():
                    if m is not None:
                        pool.wait_ge(x3_stat.sem, x3_stat.at(n, 0))
                        pool.wait_ge(ln_turned.sem, ln_turned.at(n, 0))
                    pool.sem_inc(pool_hold, 1)
                    pool.tensor_copy(flat(x2), state[:, bass.ds(n * GT, GT)])
                    own(pool.tensor_copy(fstl, fstat[:, bass.ds(n * 8, 8)]))
                    for t in range(TILES):
                        last = pool.tensor_scalar(nrm[:, t, :], x2[:, t, :], fstl[:, t:t + 1], fstl[:, 4 + t:5 + t],
                                                  ALU.subtract, ALU.mult)
                    own(last)
                    own(pool.tensor_tensor(nrm[:, :, :], nrm[:, :, :], tiled(w("rfg"), TILES), ALU.mult))
                    pool.tensor_tensor(nrm[:, :, :], nrm[:, :, :], tiled(w("rfb"), TILES), ALU.add).then_inc(xn_ready.sem, 1)

                def residual_n():
                    pool.wait_ge(x3_ready.sem, x3_ready.at(n, 1))
                    if m is None:
                        pool.wait_ge(loaded.sem, LOADED_B)
                    if m is not None:
                        pool.wait_ge(x4_stat.sem, x4_stat.at(n, 0))
                    pool.tensor_tensor(xb[:, :, :], x3[:, :, :], tiled(w("ro1"), TILES), ALU.add).then_inc(x3b_ready.sem, 1)

                def square(c, p):
                    if p == 0 and c == 1:
                        pool.wait_ge(yz_kept.sem, yz_kept.at(m, 3))
                    if p >= 2:
                        pool.wait_ge(yk_summed.sem, yk_summed.at(m, NP * c + p - 1))
                    pool.wait_ge(yk_kept.sem, yk_kept.at(m, NP * c + p + 1))
                    pool.tensor_tensor(sqk[0], kt[:, p, :], kt[:, p, :], ALU.mult).then_inc(yk_squared_p.sem, 1)

                def place_latents():
                    pool.wait_ge(ln_kept.sem, ln_kept.at(n, 1))
                    if m is not None:
                        pool.wait_ge(yv_made.sem, yv_made.at(m, SEQ))
                    pool.sem_inc(pool_hold, 1)
                    pool.tensor_copy(kvt[:, :, S:2 * S], hview(tl)).then_inc(lat_placed.sem, 1)

                if n is not None:
                    ffn_input()
                if m is not None:
                    residual_m()
                for c in range(2):
                    if m is not None:
                        for p in range(0, NP, 2):
                            square(c, p)
                    if n is not None and c == 0:
                        residual_n()
                if n is not None:
                    place_latents()
                own.done()

            pass_b(None, None, 0)
            pass_b(None, 0, 1)
            with pool.Fori(1, G - 1) as g:
                pass_b(g - 1, g, g + 1)
            pass_b(G - 2, G - 1, None)
            pass_b(G - 1, None, None)

        @block.vector
        def _(dve):
            dve.wait_ge(loaded.sem, LOADED_A)
            dve.tensor_scalar(mqs, k("maskq"), float(DX) ** -0.5, None, ALU.mult).then_inc(setup_scale.sem, 1)
            dve.wait_ge(setup_scale.sem, 1)
            dve.tensor_scalar(bxqm, mqs, w("bxq"), None, ALU.mult)
            dve.tensor_tensor(vbias, k("mask2"), w("rxv"), ALU.mult)
            dve.tensor_copy(vblk[:, :, :, 16:18].rearrange("p b i n -> p (b i) n"), tiled(k("half"), SEQ * NP))
            dve.memset(maskb[S:P, :], 0.0)
            dve.tensor_scalar(maskb[0:S, :], mask8[:, :], -1.0, 1e30, ALU.add, ALU.mult).then_inc(setup.sem, 1)

            def pass_a(b, a, x):
                own = Chain(dve, dve_own)

                def norm_stats(src, stats, means, signal):
                    for t in range(TILES):
                        last = dve.bn_stats(stats[:, t, :], src[:, t, :])
                    own(last)
                    for t in range(TILES):
                        last = dve.bn_aggr(means[:, t, :], stats[:, t, :])
                    last.then_inc(signal.sem, 1)

                def norm_apply(n, dst, src, means, root, before, signal):
                    dve.wait_ge(before.sem, before.at(n, 1))
                    for t in range(TILES):
                        last = dve.tensor_scalar(dst[:, t, :], src[:, t, :], means[:, t, 0:1], root[:, t:t + 1],
                                                 ALU.subtract, ALU.mult)
                    last.then_inc(signal.sem, 1)

                def normalise():
                    dve.wait_ge(rms_ready.sem, rms_ready.at(b, 1))
                    dve.tensor_tensor(nrm[:, :, :], x_in[:, :, :], over(rms, D), ALU.mult).then_inc(n_ready.sem, 1)

                def keep_k(p):
                    dve.wait_ge(k_made.sem, k_made.at(a, p + 1))
                    dve.tensor_scalar(kt[:, p, :], pc[:, 512 * (p % 2):512 * (p % 2) + 512], w("bk0", p, p + 1), None,
                                      ALU.add).then_inc(k_kept.sem, 1)

                def keep_v(t):
                    dve.wait_ge(v_made.sem, v_made.at(a, t + 1))
                    dve.tensor_tensor(v[:, t % 2, :], pa[:, :], w("rv0"), ALU.add).then_inc(v_kept.sem, 1)

                def shift(t):
                    dve.wait_ge(s_made.sem, s_made.at(a, t + 1))
                    own(dve.tensor_reduce(mx[:, t % 2, :], hview(pc[:, :]), AX.X, ALU.max))
                    if t >= 2:
                        dve.wait_ge(p_ready.sem, p_ready.at(a, t - 1))
                    dve.tensor_tensor(hview(st[:, t % 2, :]), hview(pc[:, :]), over(mx[:, t % 2, :], S),
                                      ALU.subtract).then_inc(s_shifted.sem, 1)

                def sums(t):
                    dve.wait_ge(s_exp.sem, s_exp.at(a, t + 1))
                    own(dve.tensor_reduce(sm[:, t % 2, :], hview(st[:, t % 2, :]), AX.X, ALU.add))
                    if t >= 2:
                        dve.wait_ge(v_scaled.sem, v_scaled.at(a, t - 1))
                    dve.reciprocal(rs[:, t % 2, :], sm[:, t % 2, :]).then_inc(s_norm.sem, 1)

                def keep_kx():
                    dve.wait_ge(kx_made.sem, kx_made.at(a, 1))
                    for j in range(4):
                        last = dve.tensor_scalar(kj[:, j, :], pc[:, 512:1024], w("bxk"), k("mask4", j, j + 1), ALU.add,
                                                 ALU.mult)
                    last.then_inc(kx_kept.sem, 1)

                def keep_vx():
                    dve.wait_ge(vx_made.sem, vx_made.at(a, 1))
                    dve.tensor_tensor(vdata, pb[:, :].rearrange("p (b i n) -> p b i n", b=SEQ, n=16),
                                      tiled(k("mask2"), SEQ).rearrange("p b (i n) -> p b i n", n=16),
                                      ALU.mult).then_inc(vx_masked.sem, 1)

                def last_peak():
                    dve.wait_ge(peak_done.sem, peak_done.at(x, 0))
                    dve.tensor_reduce(peak[:, 0:1], flat(y), AX.X, ALU.max)
                    own(dve.tensor_reduce(peak[:, 1:2], flat(y), AX.X, ALU.min))
                    dve.tensor_tensor(peaks[:, 0:1], peaks[:, 0:1], peak[:, 0:1], ALU.max)
                    dve.tensor_tensor(peaks[:, 1:2], peaks[:, 1:2], peak[:, 1:2], ALU.min).then_inc(peak_kept.sem, 1)

                def shift_x(t):
                    dve.wait_ge(sx_made.sem, sx_made.at(x, t + 1))
                    own(dve.tensor_reduce(mxx, hview(pb[:, :]), AX.X, ALU.max))
                    dve.tensor_tensor(hview(stx[:, :]), hview(pb[:, :]), over(mxx, S),
                                      ALU.subtract).then_inc(sx_shifted.sem, 1)

                def keep_px(t):
                    dve.wait_ge(px_turned.sem, px_turned.at(x, t + 1))
                    dve.tensor_copy(pt[t % 2][:, 4:8, :].rearrange("p a n -> p (a n)"),
                                    pb[:, 512:1024]).then_inc(px_v.sem, 1)

                def keep_zx(t):
                    dve.wait_ge(zx_made.sem, zx_made.at(x, t + 1))
                    for b in range(2):
                        r = slice(S * b, S * b + S)
                        col = pe_[r, 0:36 * NP].rearrange("p (i n) -> p i n", n=36)
                        last = dve.reciprocal(rz[r], col[:, :, 18 * b + 16:18 * b + 18])
                    own(last)
                    for b in range(2):
                        r = slice(S * b, S * b + S)
                        col = pe_[r, 0:36 * NP].rearrange("p (i n) -> p i n", n=36)
                        last = dve.tensor_tensor(
                            zx[r, t, :].rearrange("p (i e d) -> p i e d", e=2, d=DX),
                            col[:, :, 18 * b:18 * b + 16].rearrange("p i (e d) -> p i e d", d=DX),
                            rz[r].unsqueeze(3).broadcast_to([S, NP, 2, DX]), ALU.mult)
                    last.then_inc(zx_ready.sem, 1)

                for p in range(NP):
                    if a is not None:
                        keep_k(p)
                    if x is not None and p == 6:
                        shift_x(0)
                for t in range(TILES + 1):
                    if a is not None and t >= 1:
                        sums(t - 1)
                    if x is not None and t == 2:
                        last_peak()
                    if a is not None and t < TILES:
                        keep_v(t)
                    if x is not None and t < TILES:
                        keep_px(t)
                    if a is not None and t < TILES:
                        shift(t)
                    if x is not None and t < TILES:
                        keep_zx(t)
                        if t + 1 < TILES:
                            shift_x(t + 1)
                if b is not None:
                    normalise()
                if a is not None:
                    keep_kx()
                if x is not None:
                    dve.wait_ge(ox_made.sem, ox_made.at(x, 1))
                    dve.wait_ge(x1b_ready.sem, x1b_ready.at(x, 1))
                    own(dve.tensor_tensor(flat(resx), pe_[:, :], flat(xbx), ALU.add))
                    norm_stats(resx, statsx, mvx, r2_ready)
                if a is not None:
                    keep_vx()
                if x is not None:
                    norm_apply(x, x2, resx, mvx, rstdx, rstd2, x2_ready)
                    dve.wait_ge(x2_ready.sem, x2_ready.at(x, 1))
                    norm_stats(x2, statsx, mvx, stat3)
                if a is not None:
                    dve.wait_ge(o_made.sem, o_made.at(a, 1))
                    dve.wait_ge(xb_ready.sem, xb_ready.at(a, 1))
                    own(dve.tensor_tensor(flat(res), pd[:, :], flat(xb), ALU.add))
                    norm_stats(res, stats, mv, stat1)
                    norm_apply(a, x1, res, mv, rstd, rstd1, x1_ready)
                own.done()

            pass_a(0, None, None)
            pass_a(1, 0, None)
            with dve.Fori(1, G - 1) as g:
                pass_a(g + 1, g, g - 1)
            pass_a(None, G - 1, G - 2)
            pass_a(None, None, G - 1)

            dve.wait_ge(peak_done.sem, G + peak_done.lead)
            steps = [0]

            def link(ins):
                steps[0] += 1
                ins.then_inc(scale_step.sem, 1)
                dve.wait_ge(scale_step.sem, steps[0])

            dve.tensor_reduce(peak[:, 0:1], flat(y), AX.X, ALU.max)
            link(dve.tensor_reduce(peak[:, 1:2], flat(y), AX.X, ALU.min))
            link(dve.tensor_tensor(ffs[:, 4:5], peaks[:, 0:1], peak[:, 0:1], ALU.max))
            link(dve.tensor_tensor(ffs[:, 5:6], peaks[:, 1:2], peak[:, 1:2], ALU.min))
            dve.scalar_tensor_tensor(ffs[:, 3:4], ffs[:, 5:6], -1.0, ffs[:, 4:5], ALU.mult,
                                     ALU.max).then_inc(peak_local.sem, 1)
            dve.wait_ge(peak_all.sem, 1)
            link(dve.reciprocal(ffs[:, 4:5], ffs[:, 1:2]))
            link(dve.tensor_scalar(ffs[:, 4:5], ffs[:, 4:5], QB, None, ALU.mult))
            link(dve.tensor_scalar(ffs[:, 5:6], ffs[:, 2:3], 1.0 / (D * D), None, ALU.mult))
            link(dve.tensor_scalar(ffs[:, 6:7], ffs[:, 5:6], ffs[:, 1:2], 1.0 / QB, ALU.mult, ALU.mult))
            link(dve.tensor_scalar(ffs[:, 7:8], ffs[:, 5:6], 1e-5, None, ALU.add))
            link(dve.reciprocal(ffs[:, 7:8], ffs[:, 7:8]))
            link(dve.tensor_scalar(wq[:, :], w("ffn"), ffs[:, 7:8], None, ALU.mult))
            link(dve.tensor_scalar(wq[:, :], wq[:, :], 12582912.0, None, ALU.add))
            link(dve.tensor_scalar(wq[:, :], wq[:, :], -12582912.0, None, ALU.add))
            dve.tensor_scalar(wq[:, :], wq[:, :], 1.0, -1.0, ALU.min, ALU.max).then_inc(between.sem, 1)
            dve.wait_ge(between.sem, 1)

            dve.wait_ge(loaded.sem, LOADED_B)
            dve.tensor_scalar(gqk, w("qg"), w("kg"), float(DH) ** -0.5, ALU.mult, ALU.mult)

            def pass_b(f, m, n):
                own = Chain(dve, dve_own)

                def norm_stats(src, stats, means, signal):
                    for t in range(TILES):
                        last = dve.bn_stats(stats[:, t, :], src[:, t, :])
                    own(last)
                    for t in range(TILES):
                        last = dve.bn_aggr(means[:, t, :], stats[:, t, :])
                    last.then_inc(signal.sem, 1)

                def norm_apply(i, dst, src, means, root, before, signal):
                    dve.wait_ge(before.sem, before.at(i, 1))
                    for t in range(TILES):
                        last = dve.tensor_scalar(dst[:, t, :], src[:, t, :], means[:, t, 0:1], root[:, t:t + 1],
                                                 ALU.subtract, ALU.mult)
                    last.then_inc(signal.sem, 1)

                def quantise():
                    dve.wait_ge(xn_turned.sem, xn_turned.at(n, 1))
                    own(dve.tensor_scalar(tT[:, :], pe_[:, :], ffs[:, 4:5], QB - 1e-5, ALU.mult, ALU.min))
                    dve.tensor_scalar(tT[:, :], tT[:, :], -QB + 1e-5, None, ALU.max).then_inc(xq_ready.sem, 1)

                def sum_x3():
                    dve.wait_ge(f_made.sem, f_made.at(n, 1))
                    own(dve.scalar_tensor_tensor(flat(res), pe_[:, :], ffs[:, 6:7], flat(x2), ALU.mult, ALU.add))
                    norm_stats(res, statsx, mvx, x3_stat)

                def shift_1():
                    dve.wait_ge(s1_made.sem, s1_made.at(n, 1))
                    own(dve.tensor_reduce(smx, hview(pe_[:, :], P), AX.X, ALU.max))
                    dve.tensor_tensor(hview(s1, P), hview(pe_[:, :], P), over(smx, P),
                                      ALU.subtract).then_inc(s1_shifted.sem, 1)

                def softmax_1():
                    dve.wait_ge(s1_exp.sem, s1_exp.at(n, 1))
                    own(dve.tensor_reduce(smx, hview(s1, P), AX.X, ALU.add))
                    own(dve.reciprocal(smx, smx))
                    dve.tensor_tensor(hview(s1, P), hview(s1, P), over(smx, P), ALU.mult).then_inc(p1_ready.sem, 1)

                def sum_x4():
                    dve.wait_ge(o1_made.sem, o1_made.at(n, 1))
                    dve.wait_ge(x3b_ready.sem, x3b_ready.at(n, 1))
                    own(dve.tensor_tensor(flat(res), pe_[:, :], flat(xb), ALU.add))
                    norm_stats(res, statsx, mvx, x4_stat)

                def make_x4():
                    if m is not None:
                        dve.wait_ge(x4b_ready.sem, x4b_ready.at(m, 1))
                    norm_apply(n, x4, res, mvx, rstdx, x4_rstd, x4_ready)
                    dve.wait_ge(x4_ready.sem, x4_ready.at(n, 1))
                    norm_stats(x4, statsx, mvx, ln_stat)

                def query_sum(i, t):
                    dve.wait_ge(yq_squared.sem, yq_squared.at(i, t + 1))
                    own(dve.tensor_reduce(sm[:, t % 2, :], hview(v[:, t % 2, :]), AX.X, ALU.add))
                    dve.tensor_scalar(mx[:, t % 2, :], sm[:, t % 2, :], 1.0 / DH, 1e-16, ALU.mult,
                                      ALU.max).then_inc(yq_sum.sem, 1)

                def keep_q(t):
                    dve.wait_ge(yq_turned.sem, yq_turned.at(m, t + 1))
                    dve.tensor_scalar(qblk[DH:P, :, 1, t * P:(t + 1) * P], hview((pc, pa)[t % 2][DH:P, :], P), gqk[DH:P],
                                      None, ALU.mult).then_inc(yq_v.sem, 1)

                def scale_q(i, t):
                    dve.wait_ge(yq_root.sem, yq_root.at(i, t + 1))
                    dve.tensor_tensor(hview(st[:, t % 2, :]), hview((pc, pa)[t % 2][:, :]), over(rq[:, t % 2, :], DH),
                                      ALU.mult).then_inc(yq_scaled.sem, 1)

                def key_mean(c):
                    dve.wait_ge(yk_sum_turned.sem, yk_sum_turned.at(m, c + 1))
                    dve.tensor_scalar(rk.rearrange("p b (r n) -> p b r n", n=4),
                                      pd[:, :].rearrange("p (b r n) -> p b r n", b=4, n=32)[:, :, :, 0:4],
                                      1.0 / DH, 1e-16, ALU.mult, ALU.max).then_inc(yk_mean.sem, 1)
                    dve.wait_ge(yk_root.sem, yk_root.at(m, c + 1))

                def scale_s(b):
                    dve.wait_ge(ys_made.sem, ys_made.at(m, b + 1))
                    if b >= 2:
                        dve.wait_ge(yz_made.sem, yz_made.at(m, b - 1))
                    dve.tensor_tensor(hview(st[:, b % 2, :]), hview(pc[:, :]), over(rk[:, b % 4, :], S),
                                      ALU.mult).then_inc(ys_scaled.sem, 1)

                def norm_z(b):
                    dve.wait_ge(yl_inv.sem, yl_inv.at(m, b + 1))
                    dve.wait_ge(yz_made.sem, yz_made.at(m, b + 1))
                    for e in range(2):
                        r = slice(DH * e, DH * e + DH)
                        last = dve.tensor_tensor(
                            zt[r, :, S * b:S * b + S],
                            pb[r, :].rearrange("p (a e n) -> p a e n", e=2, n=S)[:, :, e, :],
                            hview(sqk[b % 2][r]), ALU.mult)
                    last.then_inc(yz_kept.sem, 1)

                def top_gates():
                    dve.wait_ge(gate_made.sem, gate_made.at(f, 1))
                    own(dve.tensor_copy(lg.rearrange("p t e -> p (t e)"), pe_[:, 0:TILES * E8]))
                    for t in range(TILES):
                        last = dve.max(top[:, t, :], lg[:, t, :])
                    own(last)
                    for t in range(TILES):
                        last = dve.max_index(topu[:, t, :], top[:, t, :], lg[:, t, :])
                    own(last)
                    dve.tensor_tensor(p2, top[:, :, 1], top[:, :, 0], ALU.subtract).then_inc(gap_ready.sem, 1)
                    own(dve.tensor_copy(ix, topu[:, :, 0:2]))
                    dve.tensor_tensor(selc, tiled(k("iota"), TILES), over(ix[:, :, 0], E8), ALU.is_equal)
                    own(dve.tensor_tensor(selc2, tiled(k("iota"), TILES), over(ix[:, :, 1], E8), ALU.is_equal))

                def gate_weights():
                    dve.wait_ge(gap_exp.sem, gap_exp.at(f, 1))
                    own(dve.tensor_scalar(p1, p2, 1.0, None, ALU.add))
                    own(dve.reciprocal(p1, p1))
                    own(dve.tensor_tensor(ix[:, :, 1], p2, p1, ALU.mult))
                    dve.tensor_tensor(selc, selc, over(p1, E8), ALU.mult)
                    own(dve.tensor_tensor(selc2, selc2, over(ix[:, :, 1], E8), ALU.mult))
                    dve.tensor_tensor(cw, selc, selc2, ALU.add).then_inc(cw_ready.sem, 1)

                def sum_bias():
                    dve.wait_ge(be_made.sem, be_made.at(f, 1))
                    dve.tensor_tensor(flat(resx), pe_[:, :], flat(x5), ALU.add).then_inc(be_kept.sem, 1)

                def mix(i):
                    t, c = i // 2, i % 2
                    if i == 0:
                        dve.wait_ge(cw_ready.sem, cw_ready.at(f, 1))
                    dve.wait_ge(e_made.sem, e_made.at(f, i + 1))
                    dve.tensor_tensor(hview(mixed[:, 512 * c:512 * c + 512], D), hview(pe_[:, :], D),
                                      over(cw[:, t, 4 * c:4 * c + 4], D), ALU.mult).then_inc(e_scaled.sem, 1)
                    if c == 1:
                        dve.wait_ge(e_scaled.sem, e_scaled.at(f, i + 1))
                        own(dve.tensor_reduce(y[:, t, :], mixed.rearrange("p (e n) -> p n e", e=E8), AX.X, ALU.add))

                def sum_x6():
                    dve.wait_ge(be_kept.sem, be_kept.at(f, 1))
                    own(dve.tensor_tensor(flat(resx), flat(resx), flat(y), ALU.add))
                    norm_stats(resx, stats, mv, x6_stat)

                def make_x6():
                    dve.wait_ge(stored.sem, stored.at(f, 0))
                    norm_apply(f, x6, resx, mv, rstd, x6_rstd, x6_ready)

                if m is not None:
                    query_sum(m, 1)
                    keep_q(0)
                    scale_q(m, 1)
                    keep_q(1)
                    query_sum(m, 2)
                if f is not None:
                    top_gates()
                if m is not None:
                    scale_q(m, 2)
                if n is not None:
                    quantise()
                if m is not None:
                    query_sum(m, 3)
                    keep_q(2)
                    scale_q(m, 3)
                if f is not None:
                    gate_weights()
                if m is not None:
                    keep_q(3)
                if n is not None:
                    sum_x3()
                    norm_apply(n, x3, res, mvx, rstdx, x3_rstd, x3_ready)
                if m is not None:
                    key_mean(0)
                    scale_s(0)
                if f is not None:
                    sum_bias()
                for i in range(1, 5):
                    if m is not None and i < 4:
                        scale_s(i)
                    if n is not None and i == 3:
                        shift_1()
                    if m is not None:
                        norm_z(i - 1)
                    if f is not None:
                        mix(i - 1)
                    if n is not None and i == 1:
                        dve.wait_ge(cb_loaded.sem, cb_loaded.at(n, 16))
                        norm_stats(c_in, statsx, mvx, cn_stat)
                    if n is not None and i == 2:
                        norm_apply(n, cn, c_in, mvx, rstdx, cn_rstd, cn_ready)
                if n is not None:
                    softmax_1()
                if f is not None:
                    mix(4)
                    mix(5)
                if n is not None:
                    sum_x4()
                if m is not None:
                    key_mean(1)
                    scale_s(4)
                if f is not None:
                    mix(6)
                if n is not None:
                    make_x4()
                for i in range(1, 5):
                    if m is not None and i < 4:
                        scale_s(4 + i)
                    if n is not None and i == 1:
                        norm_apply(n, nrm, x4, mvx, rstdx, ln_rstd, ln_ready)
                    if m is not None:
                        norm_z(3 + i)
                    if f is not None:
                        if i == 1:
                            mix(7)
                        if i == 2:
                            sum_x6()
                        if i == 3:
                            make_x6()
                if n is not None:
                    query_sum(n, 0)
                if m is not None:
                    dve.wait_ge(yo_made.sem, yo_made.at(m, 1))
                    dve.wait_ge(x4b_ready.sem, x4b_ready.at(m, 1))
                    own(dve.tensor_tensor(flat(resx), pa[:, 0:512], flat(xbx), ALU.add))
                    norm_stats(resx, stats, mv, x5_stat)
                if n is not None:
                    scale_q(n, 0)
                if m is not None:
                    norm_apply(m, x5, resx, mv, rstd, x5_rstd, x5_ready)
                own.done()

            pass_b(None, None, 0)
            pass_b(None, 0, 1)
            with dve.Fori(1, G - 1) as g:
                pass_b(g - 1, g, g + 1)
            pass_b(G - 2, G - 1, None)
            pass_b(G - 1, None, None)


def pack(table, parts):
    rows = [np.asarray(parts[name]).reshape(P, width) for name, width in table]
    return np.ascontiguousarray(np.concatenate(rows, axis=1))


def constants():
    i, j = np.arange(P)[:, None], np.arange(P)[None, :]
    f = np.float32
    sel = np.zeros((P, 64), f)
    for e in range(2):
        sel[DH * e:DH * e + DH, e] = 1.0
        sel[DH * e:DH * e + DH, 32 + 2 + e] = 1.0
    parts = {
        "ident": (i == j).astype(f), "ones": np.ones((P, P), f), "sel": sel,
        "mask4": ((i % 32) // DX == np.arange(4)[None, :]).astype(f),
        "maskq": (i // 32 == np.arange(4)[None, :]).astype(f),
        "mask2": ((i < S) == ((j // DX) % 2 == 0)).astype(f),
        "half": np.concatenate([(i < S), (i >= S)], axis=1).astype(f),
        "eps0": np.full((P, 1), 1.1920929e-07, f), "eps5": np.full((P, 1), 1e-5, f), "eps3": np.full((P, 1), 1e-3, f),
        "iota": np.broadcast_to(np.arange(E8, dtype=f), (P, E8)),
    }
    low = -60000.0
    m0 = np.where(np.arange(S)[None, :] >= i % S, 0.0, low)
    m1 = np.where((i // S == j // S) & (j <= i), 0.0, low)
    wide = np.concatenate([np.eye(P), np.tile(m0, (1, 8)), np.tile(m1, (1, 4))], axis=1)
    return pack(CONSTS, parts), wide.astype(np.float16)


def kernel(**a):
    from concourse import bacc
    from concourse.bass_utils import run_bass_kernel_spmd

    a = {name: np.asarray(value) for name, value in a.items()}
    ctx = a["ctx_1024"].reshape(B * S, D)
    wqkv = a["L0_attn_W_qkv"].reshape(NH, DH, 3, D)
    bqkv = a["L0_attn_b_qkv"].reshape(NH, DH, 3)

    def by_pair(m):
        return m.reshape(NP, P, D).transpose(1, 0, 2)

    def rows(r):
        return np.broadcast_to(r.reshape(1, -1), (P, r.size))

    def twice(r):
        return np.concatenate([r, r])

    wkv = a["L1_xattn_Wkv"]
    parts = {
        "q0": wqkv[:, :, 0].reshape(INNER, D).T, "k0": wqkv[:, :, 1].reshape(INNER, D).T,
        "v0": wqkv[:, :, 2].reshape(INNER, D).T, "o0": by_pair(a["L0_attn_W_o"].T),
        "xq": a["L0_xattn_Wq"], "xk": a["L0_xattn_Wk"], "xv": a["L0_xattn_Wv"], "xo": a["L0_xattn_Wo"],
        "ffn": a["L0_ffn_weight"], "basis": a["L1_attn_W_basis"].T, "v1": a["L1_attn_W_v"].T,
        "o1": a["L1_attn_W_o"].T, "yq": a["L1_xattn_Wq"], "yk": wkv[:, :INNER], "yv": wkv[:, INNER:],
        "yo": by_pair(a["L1_xattn_Wout"]), "gate": a["L1_ffn_Wg"].T,
        "exp": a["L1_ffn_We"].transpose(2, 0, 1),
        "bq0": bqkv[:, :, 0].reshape(NP, P).T, "bk0": bqkv[:, :, 1].reshape(NP, P).T,
        "bxq": a["L0_xattn_bq"], "bxk": a["L0_xattn_bk"], "bv1": a["L1_attn_b_v"],
        "gx": a["L1_xattn_ln_x_g"], "bx": a["L1_xattn_ln_x_b"], "gl": a["L1_xattn_ln_l_g"],
        "bl": a["L1_xattn_ln_l_b"], "qg": twice(a["L1_xattn_qn_g"]), "kg": twice(a["L1_xattn_kn_g"]),
        "rv0": rows(bqkv[:, :, 2]), "ro0": rows(a["L0_attn_b_o"]), "rxv": rows(a["L0_xattn_bv"]),
        "rxo": rows(a["L0_xattn_bo"]), "rfg": rows(a["L0_ffn_ln_gamma"]), "rfb": rows(a["L0_ffn_ln_beta"]),
        "ro1": rows(a["L1_attn_b_o"]), "ryo": rows(a["L1_xattn_bout"]),
    }
    consts, consts16 = constants()
    arrays = {
        "x": np.ascontiguousarray(a["x"].reshape(B * S, D)),
        "ctx_t": np.ascontiguousarray(ctx.T),
        "ctx": np.ascontiguousarray(ctx),
        "mask_t": np.ascontiguousarray(a["mask_BxS2_bf1"].T).view(np.uint8),
        "weights_a": pack(WEIGHTS_A, parts),
        "weights_b": pack(WEIGHTS_B, parts),
        "weights_ab": pack(WEIGHTS_AB, parts),
        "be": np.ascontiguousarray(a["L1_ffn_be"]),
        "consts": consts,
        "consts16": consts16,
    }
    nc = bacc.Bacc("TRN2", target_bir_lowering=False, num_devices=1)
    args = [nc.dram_tensor(name, v.shape, mybir.dt.from_np(v.dtype), kind="ExternalInput").ap()
            for name, v in arrays.items()]
    args.append(nc.dram_tensor("out", (B * S, D), F32, kind="ExternalOutput").ap())
    decoder(nc, *args)
    r = run_bass_kernel_spmd(nc, [arrays], core_ids=[0])
    return r.results[0]["out"].reshape(B, S, D)
```
